# Optimizing a Trainium2 kernel written in Bass

```python
import numpy as np
import jax
import jax.numpy as jnp

def _softmax(x, axis=-1):
    return jax.nn.softmax(x, axis=axis)

def _gelu(x):
    return jax.nn.gelu(x, approximate=True)

def _silu(x):
    return jax.nn.silu(x)

def _sigmoid(x):
    return jax.nn.sigmoid(x)

def _layernorm(x, axis=-1, eps=1e-05):
    m = jnp.mean(x, axis=axis, keepdims=True)
    v = jnp.var(x, axis=axis, keepdims=True)
    return (x - m) / jnp.sqrt(v + eps)

def _scatter_add(tgt, idx, src, axis=0):
    return tgt.at[idx].add(src)

def _segment_sum(src, seg, n):
    return jax.ops.segment_sum(src, seg, n)
kernel_name = 'mk_decoder_postln_d2_seqx_r8_03956a'

def setup_inputs(seed: int=0):
    np.random.seed(seed)
    _w = jnp.asarray

    def _rec_inputs():
        import jax
        import jax.numpy as jnp
        _rk = jax.random.key(seed)
        x = 0.0003765 + 1 * jax.random.normal(jax.random.fold_in(_rk, 1), (8, 128, 256), jnp.float32)
        _lenS = 128 - jax.random.randint(jax.random.fold_in(_rk, 7), (8,), 0, max(1, 128 // 4) + 1, jnp.int32)
        _lenS2 = 128 - jax.random.randint(jax.random.fold_in(_rk, 8), (8,), 0, max(1, 128 // 4) + 1, jnp.int32)
        _ctx_2048P = jax.random.normal(jax.random.fold_in(_rk, 11), (8, 16, 256), jnp.float32)
        _ctx_2048c = jax.random.dirichlet(jax.random.fold_in(_rk, 511), 0.3 * jnp.ones((16,), jnp.float32), (8, 128))
        _ctx_2048t = jnp.einsum('bsk,bkd->bsd', _ctx_2048c, _ctx_2048P)
        _ctx_2048t = _ctx_2048t * jax.lax.rsqrt(jnp.mean(jnp.square(_ctx_2048t)) + 1e-12) * 0.953939
        ctx_2048 = -0.000292821 + 1.00034 * (_ctx_2048t + 0.3 * jax.random.normal(jax.random.fold_in(_rk, 611), (8, 128, 256), jnp.float32))
        _validS = jnp.arange(128)[None, :] < _lenS[:, None]
        _validS2 = jnp.arange(128)[None, :] < _lenS2[:, None]
        _causal = jnp.tril(jnp.ones((128, 128), dtype=bool))
        mask_BxS2_bk0 = jnp.logical_not(jnp.broadcast_to(_validS2[:, :], (8, 128)))
        return (x, ctx_2048, mask_BxS2_bk0)
    x, ctx_2048, mask_BxS2_bk0 = _rec_inputs()

    def _L0_attn_setup():
        import jax, jax.numpy as jnp
        import numpy as np
        BLOCK = 32
        EPS = 1e-06

        def _silu(x):
            return x * jax.nn.sigmoid(x)
        key = jax.random.key(seed)
        k1, k2, k3, k4 = jax.random.split(key, 4)
        embed_dim, hidden_dim = (256, 256)
        b, n, h = (2, 512, 16)
        x = jax.random.normal(k1, (b, n, embed_dim), dtype=jnp.float32)
        slope_rate = jax.random.uniform(k2, (h, 1, 1), dtype=jnp.float32, minval=0.01, maxval=1.0)
        W_qkvu = jax.random.normal(k3, (4 * hidden_dim, embed_dim), dtype=jnp.float32) / np.sqrt(embed_dim)
        W_out = jax.random.normal(k4, (embed_dim, hidden_dim), dtype=jnp.float32) / np.sqrt(hidden_dim)
        return {'x': x, 'slope_rate': slope_rate, 'W_qkvu': W_qkvu, 'W_out': W_out}
    _L0_attn_all = _L0_attn_setup()
    _L0_attn_in = {k: v for k, v in _L0_attn_all.items() if k in ('slope_rate', 'W_qkvu', 'W_out')}
    del _L0_attn_all

    def _L0_xattn_setup():
        import jax, jax.numpy as jnp
        import numpy as np
        key = jax.random.key(seed)
        k1, k2, k3, k4, k5 = jax.random.split(key, 5)
        B, D_MODEL, L = (2, 128, 256)
        HEAD_DIM = 8
        H = D_MODEL // HEAD_DIM
        return {'k': jax.random.normal(k1, (B, D_MODEL, L), dtype=jnp.float32), 'v': jax.random.normal(k2, (B, D_MODEL, L), dtype=jnp.float32), 'q': jax.random.normal(k3, (B, D_MODEL, L), dtype=jnp.float32), 'ssm_kernel': jax.random.normal(k4, (H, L), dtype=jnp.float32), 'D': jax.random.normal(k5, (H,), dtype=jnp.float32), 'head_dim': HEAD_DIM}
    _L0_xattn_all = _L0_xattn_setup()
    _L0_xattn_in = {k: v for k, v in _L0_xattn_all.items() if k in ('ssm_kernel', 'D')}
    del _L0_xattn_all

    def _L0_ffn_setup():
        import jax, jax.numpy as jnp
        import numpy as np
        B, S, H = (2, 64, 256)
        E, I, K = (64, 176, 6)
        NS = 2
        SH_I = I * NS
        key = jax.random.key(seed)
        ks = jax.random.split(key, 6)
        s = 0.02
        return {'hidden_states': jax.random.normal(ks[0], (B, S, H), jnp.float32), 'gate_w': jax.random.normal(ks[1], (E, H), jnp.float32) * s, 'experts_w1': jax.random.normal(ks[2], (E, I, H), jnp.float32) * s, 'experts_w2': jax.random.normal(ks[3], (E, H, I), jnp.float32) * s, 'shared_gate_up': jax.random.normal(ks[4], (2 * SH_I, H), jnp.float32) * s, 'shared_down': jax.random.normal(ks[5], (H, SH_I), jnp.float32) * s}
    _L0_ffn_all = _L0_ffn_setup()
    _L0_ffn_in = {k: v for k, v in _L0_ffn_all.items() if k in ('gate_w', 'experts_w1', 'experts_w2', 'shared_gate_up', 'shared_down')}
    del _L0_ffn_all

    def _L1_attn_setup():
        import jax, jax.numpy as jnp
        import numpy as np
        HIDDEN = 256
        GAMMA = 0.96875
        SCALE_BASE = 64

        def _xpos(x, downscale=False):
            B, L, d = x.shape
            half = d // 2
            scale_vec = (jnp.arange(0, d, 2, dtype=jnp.float32) + 0.4 * d) / (1.4 * d)
            power = jnp.arange(L, dtype=jnp.float32) / SCALE_BASE
            scale = scale_vec[None, :] ** power[:, None]
            inv_freq = 1.0 / 10000.0 ** (jnp.arange(half, dtype=jnp.float32) / half)
            sinusoid = jnp.arange(L, dtype=jnp.float32)[:, None] * inv_freq[None, :]
            sin, cos = (jnp.sin(sinusoid), jnp.cos(sinusoid))
            if downscale:
                scale = 1.0 / scale
            sin_s = jnp.repeat(sin * scale, 2, axis=-1)
            cos_s = jnp.repeat(cos * scale, 2, axis=-1)
            x1 = x[..., 0::2]
            x2 = x[..., 1::2]
            rot = jnp.stack((-x2, x1), axis=-1).reshape(x.shape)
            return x * cos_s[None] + rot * sin_s[None]

        def _decay_matrix(L):
            n = jnp.arange(L)[:, None]
            m = jnp.arange(L)[None, :]
            mask = n >= m
            D = jnp.where(mask, GAMMA ** jnp.maximum(n - m, 0).astype(jnp.float32), 0.0)
            return D
        key = jax.random.key(seed)
        kx, kq, kk, kv = jax.random.split(key, 4)
        B, S, H = (4, 256, HIDDEN)
        X = jax.random.normal(kx, (B, S, H), dtype=jnp.float32)
        W_Q = jax.random.normal(kq, (H, H), dtype=jnp.float32) / H
        W_K = jax.random.normal(kk, (H, H), dtype=jnp.float32) / H
        W_V = jax.random.normal(kv, (H, H), dtype=jnp.float32) / H
        return {'X': X, 'W_Q': W_Q, 'W_K': W_K, 'W_V': W_V}
    _L1_attn_all = _L1_attn_setup()
    _L1_attn_in = {k: v for k, v in _L1_attn_all.items() if k in ('W_Q', 'W_K', 'W_V')}
    del _L1_attn_all

    def _L1_xattn_setup():
        import jax, jax.numpy as jnp
        import numpy as np
        key = jax.random.key(seed)
        k1, k2, k3 = jax.random.split(key, 3)
        B, S, D, M = (8, 256, 256, 128)
        hidden_states = jax.random.normal(k1, (B, S, D), dtype=jnp.float32)
        memory_tokens = jax.random.normal(k2, (B, M, D), dtype=jnp.float32)
        memory_mask = jax.random.randint(k3, (B, M), 0, 2).astype(jnp.bool_)
        return {'hidden_states': hidden_states, 'memory_tokens': memory_tokens, 'memory_mask': memory_mask}
    _L1_xattn_all = _L1_xattn_setup()
    _L1_xattn_in = {k: v for k, v in _L1_xattn_all.items() if k in ()}
    del _L1_xattn_all

    def _L1_ffn_setup():
        import jax, jax.numpy as jnp
        import numpy as np
        NUM_EXPERTS = 32
        TOP_K = 8
        THRESHOLD = 0.8
        HIDDEN = 256
        INTER = 96
        key = jax.random.key(seed)
        k1, k2, k3, k4 = jax.random.split(key, 4)
        hidden_states = jax.random.normal(k1, (2, 128, HIDDEN), jnp.float32)
        gate_weight = jax.random.normal(k2, (NUM_EXPERTS, HIDDEN), jnp.float32) * 0.02
        gate_up_proj = jax.random.normal(k3, (NUM_EXPERTS, 2 * INTER, HIDDEN), jnp.float32) * 0.02
        down_proj = jax.random.normal(k4, (NUM_EXPERTS, HIDDEN, INTER), jnp.float32) * 0.02
        return {'hidden_states': hidden_states, 'gate_weight': gate_weight, 'gate_up_proj': gate_up_proj, 'down_proj': down_proj}
    _L1_ffn_all = _L1_ffn_setup()
    _L1_ffn_in = {k: v for k, v in _L1_ffn_all.items() if k in ('gate_weight', 'gate_up_proj', 'down_proj')}
    del _L1_ffn_all
    return {'x': x, 'ctx_2048': ctx_2048, 'mask_BxS2_bk0': mask_BxS2_bk0, 'L0_attn_slope_rate': _L0_attn_in['slope_rate'], 'L0_attn_W_qkvu': _L0_attn_in['W_qkvu'], 'L0_attn_W_out': _L0_attn_in['W_out'], 'L0_xattn_ssm_kernel': _L0_xattn_in['ssm_kernel'], 'L0_xattn_D': _L0_xattn_in['D'], 'L0_ffn_gate_w': _L0_ffn_in['gate_w'], 'L0_ffn_experts_w1': _L0_ffn_in['experts_w1'], 'L0_ffn_experts_w2': _L0_ffn_in['experts_w2'], 'L0_ffn_shared_gate_up': _L0_ffn_in['shared_gate_up'], 'L0_ffn_shared_down': _L0_ffn_in['shared_down'], 'L1_attn_W_Q': _L1_attn_in['W_Q'], 'L1_attn_W_K': _L1_attn_in['W_K'], 'L1_attn_W_V': _L1_attn_in['W_V'], 'L1_ffn_gate_weight': _L1_ffn_in['gate_weight'], 'L1_ffn_gate_up_proj': _L1_ffn_in['gate_up_proj'], 'L1_ffn_down_proj': _L1_ffn_in['down_proj']}

def reference(x, ctx_2048, mask_BxS2_bk0, L0_attn_slope_rate, L0_attn_W_qkvu, L0_attn_W_out, L0_xattn_ssm_kernel, L0_xattn_D, L0_ffn_gate_w, L0_ffn_experts_w1, L0_ffn_experts_w2, L0_ffn_shared_gate_up, L0_ffn_shared_down, L1_attn_W_Q, L1_attn_W_K, L1_attn_W_V, L1_ffn_gate_weight, L1_ffn_gate_up_proj, L1_ffn_down_proj):
    import jax
    import jax.numpy as jnp

    def _L0_attn_ref(x, slope_rate, W_qkvu, W_out):
        import jax, jax.numpy as jnp
        import numpy as np
        BLOCK = 32
        EPS = 1e-06

        def _silu(x):
            return x * jax.nn.sigmoid(x)
        b, n, embed_dim = x.shape
        h = slope_rate.shape[0]
        hidden_dim = W_qkvu.shape[0] // 4
        d = hidden_dim // h
        NB = n // BLOCK
        qkvu = x @ W_qkvu.T
        q, k, v, u = jnp.split(qkvu, 4, axis=-1)

        def to_heads(t):
            return t.reshape(b, n, h, d).transpose(0, 2, 1, 3)
        q = _silu(to_heads(q))
        k = _silu(to_heads(k))
        v = to_heads(v)
        s = slope_rate
        arr = jnp.arange(1, BLOCK + 1, dtype=x.dtype)
        q_decay = jnp.exp(-s * arr[:, None])
        k_decay = jnp.exp(-s * (BLOCK - arr[:, None]))
        idx = arr[:, None] - arr[None, :]
        diag_decay = jnp.exp(jnp.where(idx >= 0, -s * idx, -jnp.inf))
        block_decay = jnp.exp(-s * BLOCK)

        def blk(t):
            return t.reshape(b, h, NB, BLOCK, d).transpose(2, 0, 1, 3, 4)
        qb, kb, vb = (blk(q), blk(k), blk(v))

        def step(kv, inp):
            qi, ki, vi = inp
            qkv_none_diag = jnp.einsum('bhmd,bhde->bhme', qi * q_decay, kv)
            qk = jnp.einsum('bhmd,bhsd->bhms', qi, ki) * diag_decay
            qkv_diag = jnp.einsum('bhms,bhse->bhme', qk, vi)
            kv_new = block_decay * kv + jnp.einsum('bhsd,bhse->bhde', ki * k_decay, vi)
            return (kv_new, qkv_none_diag + qkv_diag)
        kv0 = jnp.zeros((b, h, d, d), dtype=jnp.float32)
        _, outs = jax.lax.scan(step, kv0, (qb, kb, vb))
        o = outs.transpose(1, 2, 0, 3, 4).reshape(b, h, n, d)
        o = o.transpose(0, 2, 1, 3).reshape(b, n, hidden_dim)
        o = o * jax.lax.rsqrt(jnp.mean(o * o, axis=-1, keepdims=True) + EPS)
        o = u * o
        return o @ W_out.T

    def _L0_xattn_ref(k, v, q, ssm_kernel, D, head_dim):
        import jax, jax.numpy as jnp
        import numpy as np
        B, HD, L = k.shape
        H = HD // head_dim
        fft_size = 2 * L
        k_ = k.reshape(B, H, head_dim, L)
        v_ = v.reshape(B, H, head_dim, L)
        q_ = q.reshape(B, H, head_dim, L)
        kv = jnp.einsum('bhil,bhjl->bijhl', k_, v_)
        kv_f = jnp.fft.rfft(kv, n=fft_size)
        kernel_f = jnp.fft.rfft(ssm_kernel, n=fft_size)
        y = jnp.fft.irfft(kv_f * kernel_f, n=fft_size)[..., :L]
        out = y + kv * D[None, None, None, :, None]
        out = jnp.einsum('bijhl,bhil->bjhl', out, q_)
        out = jnp.transpose(out, (0, 2, 1, 3)).reshape(B, H * head_dim, L)
        return out.astype(k.dtype)

    def _L0_ffn_ref(hidden_states, gate_w, experts_w1, experts_w2, shared_gate_up, shared_down):
        import jax, jax.numpy as jnp
        import numpy as np
        B, S, H = (2, 64, 256)
        E, I, K = (64, 176, 6)
        NS = 2
        SH_I = I * NS
        orig_shape = hidden_states.shape
        x = hidden_states.reshape(-1, orig_shape[-1])
        router_logits = x @ gate_w.T
        probs = jax.nn.softmax(router_logits, axis=-1)
        topk_w, topk_idx = jax.lax.top_k(probs, K)
        topk_w = topk_w / jnp.sum(topk_w, axis=-1, keepdims=True)
        combine = jnp.sum(jax.nn.one_hot(topk_idx, E, dtype=x.dtype) * topk_w[..., None], axis=1)
        h = jax.nn.silu(jnp.einsum('th,eih->tei', x, experts_w1))
        y = jnp.einsum('tei,ehi->teh', h, experts_w2)
        routed_out = jnp.einsum('teh,te->th', y, combine)
        gu = x @ shared_gate_up.T
        g, u = jnp.split(gu, 2, axis=-1)
        shared_out = jax.nn.silu(g) * u @ shared_down.T
        return (routed_out + shared_out).reshape(orig_shape)

    def _L1_attn_ref(X, W_Q, W_K, W_V):
        import jax, jax.numpy as jnp
        import numpy as np
        HIDDEN = 256
        GAMMA = 0.96875
        SCALE_BASE = 64

        def _xpos(x, downscale=False):
            B, L, d = x.shape
            half = d // 2
            scale_vec = (jnp.arange(0, d, 2, dtype=jnp.float32) + 0.4 * d) / (1.4 * d)
            power = jnp.arange(L, dtype=jnp.float32) / SCALE_BASE
            scale = scale_vec[None, :] ** power[:, None]
            inv_freq = 1.0 / 10000.0 ** (jnp.arange(half, dtype=jnp.float32) / half)
            sinusoid = jnp.arange(L, dtype=jnp.float32)[:, None] * inv_freq[None, :]
            sin, cos = (jnp.sin(sinusoid), jnp.cos(sinusoid))
            if downscale:
                scale = 1.0 / scale
            sin_s = jnp.repeat(sin * scale, 2, axis=-1)
            cos_s = jnp.repeat(cos * scale, 2, axis=-1)
            x1 = x[..., 0::2]
            x2 = x[..., 1::2]
            rot = jnp.stack((-x2, x1), axis=-1).reshape(x.shape)
            return x * cos_s[None] + rot * sin_s[None]

        def _decay_matrix(L):
            n = jnp.arange(L)[:, None]
            m = jnp.arange(L)[None, :]
            mask = n >= m
            D = jnp.where(mask, GAMMA ** jnp.maximum(n - m, 0).astype(jnp.float32), 0.0)
            return D
        B, S, H = X.shape
        Q = _xpos(X @ W_Q)
        K = _xpos(X @ W_K, downscale=True)
        V = X @ W_V
        D = _decay_matrix(S)
        att = jnp.einsum('bnh,bmh->bnm', Q, K) * D[None]
        return att @ V

    def _L1_xattn_ref(hidden_states, memory_tokens, memory_mask):
        import jax, jax.numpy as jnp
        import numpy as np
        B, S, D = hidden_states.shape
        scale = 1.0 / jnp.sqrt(jnp.asarray(D, hidden_states.dtype))
        scores = jnp.einsum('bsd,bmd->bsm', hidden_states, memory_tokens) * scale
        neg_inf = jnp.asarray(-1e+30, scores.dtype)
        scores = jnp.where(memory_mask[:, None, :], scores, neg_inf)
        attn = jax.nn.softmax(scores, axis=-1)
        readout = jnp.einsum('bsm,bmd->bsd', attn, memory_tokens)
        valid_b = jnp.any(memory_mask, axis=-1)
        out = jnp.where(valid_b[:, None, None], readout, jnp.zeros_like(readout))
        return out

    def _L1_ffn_ref(hidden_states, gate_weight, gate_up_proj, down_proj):
        import jax, jax.numpy as jnp
        import numpy as np
        NUM_EXPERTS = 32
        TOP_K = 8
        THRESHOLD = 0.8
        HIDDEN = 256
        INTER = 96
        B, S, H = hidden_states.shape
        x = hidden_states.reshape(-1, H)
        logits = x @ gate_weight.T
        probs = jax.nn.softmax(logits.astype(jnp.float32), axis=-1).astype(logits.dtype)
        top_vals, top_idx = jax.lax.top_k(probs, TOP_K)
        renorm = top_vals / jnp.clip(jnp.sum(top_vals, axis=-1, keepdims=True), 1e-12)
        cum = jnp.cumsum(renorm, axis=-1)
        num_keep = jnp.minimum(jnp.sum((cum < THRESHOLD).astype(jnp.int32), axis=-1) + 1, TOP_K)
        active = jnp.arange(TOP_K)[None, :] < num_keep[:, None]
        rw = top_vals * active.astype(top_vals.dtype)
        rw = rw / jnp.clip(jnp.sum(rw, axis=-1, keepdims=True), 1e-12)
        combine = jnp.sum(jax.nn.one_hot(top_idx, NUM_EXPERTS, dtype=rw.dtype) * rw[..., None], axis=1)

        def body(acc, params):
            w_gu, w_d, ce = params
            gu = x @ w_gu.T
            g, u = jnp.split(gu, 2, axis=-1)
            h = jax.nn.silu(g) * u
            return (acc + h @ w_d.T * ce[:, None], None)
        out, _ = jax.lax.scan(body, jnp.zeros_like(x), (gate_up_proj, down_proj, combine.T))
        return out.reshape(B, S, H)
    x = _layernorm(x + _L0_attn_ref(x, L0_attn_slope_rate, L0_attn_W_qkvu, L0_attn_W_out), axis=-1)
    x = _layernorm(x + _L0_xattn_ref(ctx_2048, ctx_2048, x, L0_xattn_ssm_kernel, L0_xattn_D, 8), axis=-1)
    x = _layernorm(x + _L0_ffn_ref(x, L0_ffn_gate_w, L0_ffn_experts_w1, L0_ffn_experts_w2, L0_ffn_shared_gate_up, L0_ffn_shared_down), axis=-1)
    x = _layernorm(x + _L1_attn_ref(x, L1_attn_W_Q, L1_attn_W_K, L1_attn_W_V), axis=-1)
    x = _layernorm(x + _L1_xattn_ref(x, ctx_2048, mask_BxS2_bk0), axis=-1)
    x = _layernorm(x + _L1_ffn_ref(x, L1_ffn_gate_weight, L1_ffn_gate_up_proj, L1_ffn_down_proj), axis=-1)
    return x

_drawn_inputs = setup_inputs


def setup_inputs(seed=0):
    import zlib

    import numpy as np

    out = dict(_drawn_inputs(seed))
    spreads = {}
    factors = {'L0_ffn_gate_w': 3.628,
     'L0_ffn_experts_w1': 3.519,
     'L0_ffn_experts_w2': 3.487,
     'L0_ffn_shared_gate_up': 3.146,
     'L0_ffn_shared_down': 3.182,
     'L1_attn_W_Q': 3.288,
     'L1_attn_W_K': 3.301,
     'L1_attn_W_V': 3.264,
     'L1_ffn_gate_weight': 8.0,
     'L1_ffn_gate_up_proj': 8.0,
     'L1_ffn_down_proj': 8.0}
    for name, (base, spread) in spreads.items():
        noise = np.random.default_rng([zlib.crc32(name.encode()), seed]).standard_normal(out[name].shape)
        drawn = base * np.exp(spread * noise) if base else spread * noise
        out[name] = jnp.asarray(drawn.astype(out[name].dtype))
    for name, factor in factors.items():
        out[name] = (out[name] * factor).astype(out[name].dtype)
    return out
```

```python
import numpy as np
from contextlib import ExitStack

import concourse.bass as bass
from concourse import mybir

F32 = mybir.dt.float32
F16 = mybir.dt.float16
I32 = mybir.dt.int32
U32 = mybir.dt.uint32
U8 = mybir.dt.uint8
ALU = mybir.AluOpType
ACT = mybir.ActivationFunctionType
AX = mybir.AxisListType

P = 128
D = 256
DH = D // P
B = 8
T = B * P
H = 16
HD = D // H
CJ = P // H
WS = 256.0
GAMMA = 0.96875
SCALE_BASE = 64
LN_EPS = 1e-5
RMS_EPS = 1e-6
ARENA = 28672
ARENA2 = 14336
CONV_WORDS = 9216
IOTA = 192
HALF = T // 2


class Chain:

    def __init__(self, engine, semaphore):
        self.engine, self.semaphore, self.n = engine, semaphore, 0

    def link(self, instruction):
        self.n += 1
        instruction.then_inc(self.semaphore, 1)
        self.engine.wait_ge(self.semaphore, self.n)

    def mark(self, instruction):
        self.n += 1
        instruction.then_inc(self.semaphore, 1)
        return self.n


def build_program(nc, ins, out):
    with ExitStack() as ctx:
        def sb(name, shape, dt=F32):
            return ctx.enter_context(nc.sbuf_tensor(name, shape, dt))

        def sem(name):
            return ctx.enter_context(nc.semaphore(name))

        arena = sb("arena", [P, ARENA])
        arena2 = sb("arena2", [P, ARENA2])

        class Region:

            def __init__(self, start=0, memory=None):
                self.at = start
                self.memory = arena if memory is None else memory

            def __call__(self, name, shape, dt=F32):
                size = int(np.prod(shape[1:]))
                words = {F16: size // 2, U8: size // 4}.get(dt, size)
                view = self.memory[0:shape[0], self.at:self.at + words]
                self.at += words
                if dt != F32:
                    view = view.bitcast(dt)
                names = " ".join("abcde"[:len(shape) - 1])
                sizes = dict(zip("abcde", shape[1:]))
                return view.rearrange(f"p ({names}) -> p {names}", **sizes) if len(shape) > 2 else view

        bank = [ctx.enter_context(nc.psum_tensor(f"bank{i}", [P, 512], F32)) for i in range(8)]

        X = sb("X", [P, B, D])
        R = sb("R", [P, 4, D])
        xTh = sb("xTh", [P, DH, T], F16)
        xTl = sb("xTl", [P, DH, T], F16)
        stats = sb("stats", [P, 4, 6])
        mv = sb("mv", [P, B, 2])
        veps = sb("veps", [P, B])
        rstd = sb("rstd", [P, B])
        minus_half = sb("minus_half", [P, B])
        ident = sb("ident", [P, P])
        s_x = sem("s_x")
        s_ident = sem("s_ident")
        s_mh = sem("s_mh")
        s_out = sem("s_out")

        early = Region()
        xT0 = early("xT0", [P, DH, T])
        w1f = early("w1f", [P, DH, 3, 512])
        w1h = early("w1h", [P, DH, 3, 512], F16)
        w1l = early("w1l", [P, DH, 3, 512], F16)
        wof = early("wof", [P, DH, D])
        woh = early("woh", [P, DH, D], F16)
        wol = early("wol", [P, DH, D], F16)
        qT = early("qT", [P, 4, T])
        kT = early("kT", [P, 4, T])
        vu = early("vu", [P, B, 2 * D])
        diff = early("diff", [P, P])
        causal = early("causal", [P, P])
        slope = early("slope", [P, H])
        nslope = early("nslope", [P, H])
        decay = early("decay", [P, H, P])
        prob = early("prob", [P, 4, 4, P])
        junk = early("junk", [P, D])
        ssq = early("ssq", [P, B])
        rms = early("rms", [P, B])
        gated = early("gated", [P, 4, D])
        gTh = early("gTh", [P, 2, DH, P], F16)
        gTl = early("gTl", [P, 2, DH, P], F16)

        a_x = sem("a_x")
        a_w = [sem(f"a_w{i}") for i in range(3)]
        a_wo = sem("a_wo")
        a_c = sem("a_c")
        a_xh = sem("a_xh")
        a_xl = sem("a_xl")
        a_wh = sem("a_wh")
        a_wl = sem("a_wl")
        a_woh = sem("a_woh")
        a_wol = sem("a_wol")
        a_ns = sem("a_ns")
        a_dec = sem("a_dec")
        a_decm = sem("a_decm")
        a_qk = sem("a_qk")
        a_qkc = sem("a_qkc")
        a_vu = sem("a_vu")
        a_vue = sem("a_vue")
        a_vuo = sem("a_vuo")
        a_sc = sem("a_sc")
        a_pr = sem("a_pr")
        a_pv = sem("a_pv")
        a_sq = sem("a_sq")
        a_rms = sem("a_rms")
        a_g = sem("a_g")
        a_gt = sem("a_gt")
        a_gh = sem("a_gh")
        a_gl = sem("a_gl")
        a_y = sem("a_y")
        dve_chain_sem = sem("dve_chain")
        pool_chain_sem = sem("pool_chain")

        class NormDone:
            sum = sem("norm_sum")
            mv = sem("norm_mv")
            rstd = sem("norm_rstd")
            x = sem("norm_x")
            t = sem("norm_t")
            hi = sem("norm_hi")
            lo = sem("norm_lo")

        done = NormDone

        class Norm:

            def __init__(self, stage, sums, highs):
                self.sum = B * sums
                self.mv = self.rstd = self.x = B * (stage - 1)
                self.t = self.lo = B // 2 * (stage - 1)
                self.hi = B // 2 * highs

        n1 = Norm(1, 0, 0)

        def norm_sum(dve, chain, n, b, y, scale):
            if b >= 4:
                dve.wait_ge(done.x, n.x + b - 3)
            dve.scalar_tensor_tensor(out=R[:, b % 4, :], in0=y, scalar=scale, in1=X[:, b, :],
                                     op0=ALU.mult, op1=ALU.add).then_inc(done.sum, 1)
            dve.wait_ge(done.sum, n.sum + b + 1)
            norm_stats(dve, chain, n, b, R[:, b % 4, :])

        def norm_stats(dve, chain, n, b, src):
            chain.link(dve.bn_stats(stats[:, b % 4, :], src))
            dve.bn_aggr(mv[:, b, :], stats[:, b % 4, :]).then_inc(done.mv, 1)

        def norm_rstd(pool, chain, n, b):
            pool.wait_ge(done.mv, n.mv + b + 1)
            chain.link(pool.tensor_scalar(veps[:, b:b + 1], mv[:, b, 1:2], LN_EPS, None, ALU.add))
            pool.tensor_tensor(rstd[:, b:b + 1], veps[:, b:b + 1], minus_half[:, 0:1], ALU.pow).then_inc(done.rstd, 1)

        def norm_all_dve(dve, chain, n):
            for b in range(B + 1):
                if b < B:
                    norm_stats(dve, chain, n, b, acc[:, b, :])
                if b >= 1:
                    norm_apply(dve, n, b - 1, acc[:, b - 1, :])
                if b >= 2 and b % 2 == 0:
                    norm_lo(dve, n, b // 2 - 1)

        def norm_apply(dve, n, b, src=None):
            dve.wait_ge(done.rstd, n.rstd + b + 1)
            dve.tensor_scalar(X[:, b, :], R[:, b % 4, :] if src is None else src, mv[:, b, 0:1], rstd[:, b:b + 1],
                              ALU.subtract, ALU.mult).then_inc(done.x, 1)

        def norm_transpose(pe, n, p):
            pe.wait_ge(done.x, n.x + 2 * p + 2)
            if p >= 2:
                pe.wait_ge(done.lo, n.lo + p - 1)
            v = bank[6 + p % 2][:, :].rearrange("q (d b t) -> q d b t", d=DH, b=2)
            for i in range(2):
                for d in range(DH):
                    mm = pe.transpose(v[:, d, i, :], X[:, 2 * p + i, d * P:(d + 1) * P], ident[:, :])
            mm.then_inc(done.t, 1)

        def norm_hi(act, n, p):
            act.wait_ge(done.t, n.t + p + 1)
            act.activation(xTh[:, :, p * 256:(p + 1) * 256], bank[6 + p % 2][:, :].rearrange("q (d t) -> q d t", d=DH),
                           ACT.Copy).then_inc(done.hi, 1)

        def norm_lo(dve, n, p):
            dve.wait_ge(done.hi, n.hi + p + 1)
            dve.tensor_tensor(xTl[:, :, p * 256:(p + 1) * 256], bank[6 + p % 2][:, :].rearrange("q (d t) -> q d t", d=DH),
                              xTh[:, :, p * 256:(p + 1) * 256], ALU.subtract).then_inc(done.lo, 1)

        def stage1_sp(sp):
            sp.dma_start(xT0[:, :, :], ins["xT"].rearrange("(d p) t -> p d t", p=P)).then_inc(a_x, 16)
            wv = ins["w_qkvu"].rearrange("(d p) (c n) -> p d c n", p=P, c=3)
            for c in range(3):
                sp.dma_start(w1f[:, :, c, :], wv[:, :, c, :]).then_inc(a_w[c], 16)
            sp.dma_start(X[:, :, :], ins["x"].rearrange("b p d -> p b d")).then_inc(s_x, 16)
            sp.dma_start(diff[:, :], ins["c_diff"]).then_inc(a_c, 16)
            sp.dma_start(causal[:, :], ins["c_causal"]).then_inc(a_c, 16)
            sp.dma_start(slope[:, :], ins["slope"].partition_broadcast(P)).then_inc(a_c, 16)
            sp.dma_start(ident[:, :], ins["c_ident"]).then_inc(s_ident, 16)
            sp.dma_start(wof[:, :, :], ins["w_out"].rearrange("(d p) n -> p d n", p=P)).then_inc(a_wo, 16)

        def stage1_pe(pe):
            def proj(dst, cols, c, t0, n, m0=None):
                k = 0
                for d in range(DH):
                    for wp, xp in ((w1h, xTh), (w1l, xTh), (w1h, xTl)):
                        mm = pe.matmul(dst, wp[:, d, c, cols:cols + P], xp[:, d, t0:t0 + n],
                                       start=(k == 0), stop=(k == 3 * DH - 1))
                        k += 1
                return mm

            pe.wait_ge(a_xh, DH)
            pe.wait_ge(a_xl, DH)
            g = 0
            for c in range(2):
                pe.wait_ge(a_wh, c + 1)
                pe.wait_ge(a_wl, c + 1)
                for th in range(2):
                    for q in range(4):
                        if g >= 4:
                            pe.wait_ge(a_qkc, g - 3)
                        proj(bank[g % 4][:, :], q * P, c, th * HALF, HALF).then_inc(a_qk, 1)
                        g += 1
            pe.wait_ge(a_wh, 3)
            pe.wait_ge(a_wl, 3)
            pe.wait_ge(a_qkc, 16)
            for b in range(B):
                if b >= 2:
                    pe.wait_ge(a_vue if b % 2 == 0 else a_vuo, b // 2)
                k = 0
                for d in range(DH):
                    for wp, xp in ((w1h, xTh), (w1l, xTh), (w1h, xTl)):
                        mm = pe.matmul(bank[b % 2][:, :], xp[:, d, b * P:(b + 1) * P], wp[:, d, 2, :],
                                       start=(k == 0), stop=(k == 3 * DH - 1))
                        k += 1
                mm.then_inc(a_vu, 1)

            pe.wait_ge(a_vue, 4)
            pe.wait_ge(a_vuo, 4)

            def weigh(j):
                th, h = j // H, j % H
                pe.wait_ge(a_pr, j + 1)
                for i in range(4):
                    b = 4 * th + i
                    mm = pe.matmul(bank[4 + b // 2][:, (b % 2) * D + h * HD:(b % 2) * D + (h + 1) * HD],
                                   prob[:, j % 4, i, :], vu[:, b, h * HD:(h + 1) * HD], start=True, stop=True)
                mm.then_inc(a_pv, 1)

            for j in range(2 * H):
                th, h = j // H, j % H
                q, a = h // 4, 32 * (h % 4)
                if j >= 3:
                    pe.wait_ge(a_pr, j - 2)
                for i in range(4):
                    t0 = th * HALF + i * P
                    mm = pe.matmul(bank[j % 3][:, i * P:(i + 1) * P], kT[a:a + HD, q, t0:t0 + P],
                                   qT[a:a + HD, q, t0:t0 + P], start=True, stop=True)
                mm.then_inc(a_sc, 1)
                if j >= 1:
                    weigh(j - 1)
            weigh(2 * H - 1)

            pe.wait_ge(s_ident, 16)
            pe.wait_ge(a_woh, 1)
            pe.wait_ge(a_wol, 1)

            def turn(b):
                pe.wait_ge(a_g, b + 1)
                if b >= 2:
                    pe.wait_ge(a_gl, b - 1)
                for d in range(DH):
                    mm = pe.transpose(bank[b % 2][:, d * P:(d + 1) * P], gated[:, b % 4, d * P:(d + 1) * P], ident[:, :])
                mm.then_inc(a_gt, 1)

            def back(b):
                pe.wait_ge(a_gl, b + 1)
                if b >= 2:
                    pe.wait_ge(done.sum, n1.sum + b - 1)
                k = 0
                for d in range(DH):
                    for wp, xp in ((woh, gTh), (wol, gTh), (woh, gTl)):
                        mm = pe.matmul(bank[2 + b % 2][:, 0:D], xp[:, b % 2, d, :], wp[:, d, :],
                                       start=(k == 0), stop=(k == 3 * DH - 1))
                        k += 1
                mm.then_inc(a_y, 1)

            for b in range(B + 1):
                if b < B:
                    turn(b)
                if b >= 1:
                    back(b - 1)
            for p in range(4):
                norm_transpose(pe, n1, p)

        def stage1_act(act):
            act.wait_ge(a_x, 16)
            for d in range(DH):
                act.activation(xTh[:, d, :], xT0[:, d, :], ACT.Copy).then_inc(a_xh, 1)
            for c in range(3):
                act.wait_ge(a_w[c], 16)
                act.activation(w1h[:, :, c, :], w1f[:, :, c, :], ACT.Copy, scale=WS).then_inc(a_wh, 1)
            for g in range(16):
                c, th, q = g // 8, g // 4 % 2, g % 4
                act.wait_ge(a_qk, g + 1)
                act.activation((qT, kT)[c][:, q, th * HALF:(th + 1) * HALF], bank[g % 4][:, :], ACT.Silu,
                               scale=1.0 / WS).then_inc(a_qkc, 1)
            for b in range(0, B, 2):
                act.wait_ge(a_vu, b + 1)
                act.activation(vu[:, b, :], bank[b % 2][:, :], ACT.Copy, scale=1.0 / WS).then_inc(a_vue, 1)
            act.wait_ge(a_wo, 16)
            act.activation(woh[:, :, :], wof[:, :, :], ACT.Copy, scale=WS).then_inc(a_woh, 1)
            act.wait_ge(a_ns, 1)
            for h in range(H):
                act.activation(decay[:, h, :], diff[:, :], ACT.Exp, scale=nslope[:, h:h + 1]).then_inc(a_dec, 1)
            for b in range(B):
                act.wait_ge(a_pv, H * (b // 4 + 1))
                if b:
                    act.wait_ge(a_sq, b)
                act.activation(junk[:, :], bank[4 + b // 2][:, (b % 2) * D:(b % 2 + 1) * D], ACT.Square,
                               accum_out=ssq[:, b:b + 1]).then_inc(a_sq, 1)
            for b in range(B):
                act.wait_ge(a_gt, b + 1)
                if b >= 2:
                    act.wait_ge(a_y, b - 1)
                act.activation(gTh[:, b % 2, :, :], bank[b % 2][:, 0:D].rearrange("q (d t) -> q d t", d=DH),
                               ACT.Copy).then_inc(a_gh, 1)

        def stage1_dve(dve, chain):
            dve.wait_ge(a_x, 16)
            for d in range(DH):
                dve.wait_ge(a_xh, d + 1)
                dve.tensor_tensor(xTl[:, d, :], xT0[:, d, :], xTh[:, d, :], ALU.subtract).then_inc(a_xl, 1)
            for c in range(3):
                dve.wait_ge(a_wh, c + 1)
                dve.scalar_tensor_tensor(out=w1l[:, :, c, :], in0=w1f[:, :, c, :], scalar=WS, in1=w1h[:, :, c, :],
                                         op0=ALU.mult, op1=ALU.subtract).then_inc(a_wl, 1)
            dve.wait_ge(a_c, 48)
            dve.tensor_scalar(nslope[:, :], slope[:, :], -1.0, None, ALU.mult).then_inc(a_ns, 1)
            for b in range(1, B, 2):
                dve.wait_ge(a_vu, b + 1)
                dve.tensor_scalar(vu[:, b, :], bank[b % 2][:, :], 1.0 / WS, None, ALU.mult).then_inc(a_vuo, 1)
            dve.wait_ge(a_woh, 1)
            dve.scalar_tensor_tensor(out=wol[:, :, :], in0=wof[:, :, :], scalar=WS, in1=woh[:, :, :],
                                     op0=ALU.mult, op1=ALU.subtract).then_inc(a_wol, 1)
            conv_filters_dve(dve)
            dve.wait_ge(a_dec, H)
            dve.tensor_tensor(decay[:, :, :], decay[:, :, :], causal[:, None, :].broadcast_to([P, H, P]),
                              ALU.mult).then_inc(a_decm, 1)
            dve.wait_ge(a_decm, 1)
            for j in range(2 * H):
                dve.wait_ge(a_sc, j + 1)
                if j >= 4:
                    dve.wait_ge(a_pv, j - 3)
                dve.tensor_tensor(prob[:, j % 4, :, :], bank[j % 3][:, :].rearrange("q (i t) -> q i t", i=4),
                                  decay[:, j % H, None, :].broadcast_to([P, 4, P]), ALU.mult).then_inc(a_pr, 1)

            def gate(b):
                dve.wait_ge(a_rms, b // 4 + 1)
                if b >= 4:
                    dve.wait_ge(a_gt, b - 3)
                dve.scalar_tensor_tensor(out=gated[:, b % 4, :], in0=bank[4 + b // 2][:, (b % 2) * D:(b % 2 + 1) * D],
                                         scalar=rms[:, b:b + 1], in1=vu[:, b, D:2 * D],
                                         op0=ALU.mult, op1=ALU.mult).then_inc(a_g, 1)

            def low(b):
                dve.wait_ge(a_gh, b + 1)
                if b >= 2:
                    dve.wait_ge(a_y, b - 1)
                dve.tensor_tensor(gTl[:, b % 2, :, :], bank[b % 2][:, 0:D].rearrange("q (d t) -> q d t", d=DH),
                                  gTh[:, b % 2, :, :], ALU.subtract).then_inc(a_gl, 1)

            dve.wait_ge(s_x, 16)
            for b in range(B + 3):
                if b < B:
                    gate(b)
                if 1 <= b < B + 1:
                    low(b - 1)
                if 2 <= b < B + 2:
                    dve.wait_ge(a_y, b - 1)
                    norm_sum(dve, chain, n1, b - 2, bank[2 + b % 2][:, 0:D], 1.0 / WS)
                if b >= 3:
                    norm_apply(dve, n1, b - 3)

        def stage1_pool(pool, chain):
            pool.memset(minus_half[:, :], -0.5).then_inc(s_mh, 1)
            pool.wait_ge(s_mh, 1)
            pool.wait_ge(b_c, 16)
            for h in range(KVH):
                conv_products_pool(pool, h)
            for th in range(2):
                pool.wait_ge(a_sq, 4 * th + 4)
                v = slice(4 * th, 4 * th + 4)
                chain.link(pool.tensor_scalar(ssq[:, v], ssq[:, v], 1.0 / D, RMS_EPS, ALU.mult, ALU.add))
                pool.tensor_tensor(rms[:, v], ssq[:, v], minus_half[:, 0:4], ALU.pow).then_inc(a_rms, 1)
            for b in range(B):
                norm_rstd(pool, chain, n1, b)
        conv = Region()
        filtering = Region(0, arena2)
        KVH = H // 2
        ctxr = filtering("ctxr", [P, DH, P, B])
        toep = filtering("toep", [P, H, 2 * P])
        dvec = sb("dvec", [P, H])
        anti = sb("anti", [P, P])
        kv = filtering("kv", [P, KVH, DH, CJ * CJ * B])
        qc = conv("qc", [P, DH, P, B])
        pr = conv("pr", [P, 3, DH, CJ, CJ * B])
        pr4 = conv("pr4", [P, 3, DH, CJ // 2, CJ * B])
        pr2 = conv("pr2", [P, 2, DH, CJ // 4, CJ * B])
        convT = conv("convT", [P, DH, B, P])

        b_c = sem("b_c")
        b_k = sem("b_k")
        b_toep = sem("b_toep")
        b_kv = sem("b_kv")
        b_y = sem("b_y")
        b_pr = sem("b_pr")
        b_p4 = sem("b_p4")
        b_o = sem("b_o")
        b_t = sem("b_t")
        n2 = Norm(2, 1, 0)

        def stage2_sp(sp):
            sp.dma_start(ctxr[:, :, :, :], ins["ctx_rev"].rearrange("p (d s b) -> p d s b", d=DH, b=B)).then_inc(b_c, 16)
            filters = bass.AP(ins["filters"].tensor, 0, [[1, P], [3 * P - 1, H], [1, 2 * P]])
            sp.dma_start(toep[:, :, :], filters).then_inc(b_k, 16)
            sp.dma_start(dvec[:, :], ins["conv_d"].partition_broadcast(P)).then_inc(b_k, 16)
            sp.dma_start(anti[:, :], ins["c_anti"]).then_inc(b_k, 16)

        def conv_products_pool(pool, h):
                for d in range(DH):
                    if h >= KVH:
                        pool.wait_ge(b_y, 2 * (h - KVH) + 2)
                    c = ctxr[:, d, h * CJ:(h + 1) * CJ, :]
                    pool.tensor_tensor(kv[:, h % KVH, d, :].rearrange("p (i j b) -> p i j b", i=CJ, j=CJ),
                                       c[:, :, None, :].broadcast_to([P, CJ, CJ, B]),
                                       c[:, None, :, :].broadcast_to([P, CJ, CJ, B]), ALU.mult).then_inc(b_kv, 1)

        def conv_filters_dve(dve):
            dve.wait_ge(b_k, 48)
            for h in range(H):
                dve.scalar_tensor_tensor(out=toep[:, h, 0:P], in0=anti[:, :], scalar=dvec[:, h:h + 1],
                                         in1=toep[:, h, 0:P], op0=ALU.mult, op1=ALU.add).then_inc(b_toep, 1)

        def stage2_pe(pe):
            pe.wait_ge(b_toep, H)
            for h in range(H):
                pe.wait_ge(b_kv, 2 * h + 2)
                for d in range(DH):
                    u = 2 * h + d
                    if u >= 4:
                        pe.wait_ge(b_pr, u - 3)
                    if d:
                        pe.matmul(bank[u % 4][:, :], toep[:, h, P:2 * P], kv[:, h % KVH, 0, :], start=True, stop=False)
                    pe.matmul(bank[u % 4][:, :], toep[:, h, 0:P], kv[:, h % KVH, d, :], start=not d, stop=True).then_inc(b_y, 1)
            pe.wait_ge(b_o, H)
            for b in range(B):
                if b >= 2:
                    pe.wait_ge(done.sum, n2.sum + b - 1)
                for d in range(DH):
                    mm = pe.transpose(bank[4 + b % 2][:, d * P:(d + 1) * P], convT[:, d, b, :], ident[:, :])
                mm.then_inc(b_t, 1)
            for p in range(4):
                norm_transpose(pe, n2, p)

        def stage2_act(act):
            for p in range(4):
                act.wait_ge(done.t, n1.t + p + 1)
                act.activation(qc[:, :, :, 2 * p:2 * p + 2].rearrange("q d t b -> q d b t"),
                               bank[6 + p % 2][:, :].rearrange("q (d b t) -> q d b t", d=DH, b=2),
                               ACT.Copy).then_inc(done.lo, 1)
            for p in range(4):
                norm_hi(act, n2, p)

        def stage2_dve(dve, chain):
            dve.wait_ge(done.lo, n1.lo + 4)

            def fold(h):
                dve.wait_ge(b_p4, h + 1)
                chain.link(dve.tensor_tensor(pr2[:, h % 2, :, :, :], pr4[:, h % 3, :, 0:2, :], pr4[:, h % 3, :, 2:4, :], ALU.add))
                dve.tensor_tensor(convT[:, :, :, h * CJ:(h + 1) * CJ].rearrange("p d b j -> p d j b"),
                                  pr2[:, h % 2, :, 0, :].rearrange("p d (j b) -> p d j b", b=B),
                                  pr2[:, h % 2, :, 1, :].rearrange("p d (j b) -> p d j b", b=B), ALU.add).then_inc(b_o, 1)

            for h in range(H + 2):
                if h < H:
                    if h >= 3:
                        dve.wait_ge(b_p4, h - 2)
                    for d in range(DH):
                        u = 2 * h + d
                        dve.wait_ge(b_y, u + 1)
                        dve.tensor_tensor(pr[:, h % 3, d, :, :].rearrange("p i (j b) -> p i j b", b=B),
                                          bank[u % 4][:, :].rearrange("p (i j b) -> p i j b", i=CJ, j=CJ),
                                          qc[:, d, h * CJ:(h + 1) * CJ, None, :].broadcast_to([P, CJ, CJ, B]),
                                          ALU.mult).then_inc(b_pr, 1)
                if h >= 2:
                    fold(h - 2)
            for b in range(B + 1):
                if b < B:
                    dve.wait_ge(b_t, b + 1)
                    norm_sum(dve, chain, n2, b, bank[4 + b % 2][:, 0:D], 1.0)
                if b >= 1:
                    norm_apply(dve, n2, b - 1)
            for p in range(4):
                norm_lo(dve, n2, p)

        def stage2_pool(pool, chain):
            for h in range(H):
                pool.wait_ge(b_pr, 2 * h + 2)
                if h >= 3:
                    pool.wait_ge(b_o, h - 2)
                pool.tensor_tensor(pr4[:, h % 3, :, :, :], pr[:, h % 3, :, 0:4, :], pr[:, h % 3, :, 4:8, :],
                                   ALU.add).then_inc(b_p4, 1)
                if h < H - KVH:
                    conv_products_pool(pool, h + KVH)
            for b in range(B):
                norm_rstd(pool, chain, n2, b)

        acc = sb("acc", [P, B, D])
        identh = sb("identh", [P, P], F16)
        before = sb("before", [P, P], F16)
        onesh = sb("onesh", [P, P], F16)
        before_f = sb("before_f", [P, P])
        iota = sb("iota", [P, IOTA])
        iotah = sb("iotah", [P, IOTA], F16)
        tokens = sb("tokens", [P, B])
        s_plain = sem("s_plain")
        s_c3 = sem("s_c3")
        s_idh = sem("s_idh")

        rows = nc.dram_tensor("token_rows", [T, 2 * D], F16).ap()

        routing_counts = {"gate": 16, "gh": 1, "gl": 1, "logit": B, "lread": B, "soft": B, "scaled": B, "mask": B, "rank": B + 1,
                          "rread": B, "named": B, "rounds": 1, "rowsh": B, "rowsl": B, "rows": 16 * B}
        routing = {edge: sem("route_" + edge) for edge in routing_counts if edge != "rows"}
        rows_out_sem = sem("rows_out")

        class Experts:

            def __init__(self, name, region, experts, top, width, gated, lot, tiles, w_gate, w_up, w_down, earlier):
                self.name, self.E, self.K, self.gated = name, experts, top, gated
                self.lot, self.nt = lot, tiles
                self.C = lot * tiles
                self.im = width
                self.nk = 1 if gated else 2
                self.NI = experts // 8
                self.max_rounds = -(-T // self.C)
                self.w_gate, self.w_up, self.w_down = w_gate, w_up, w_down
                E, K, C, im, nk = self.E, self.K, self.C, self.im, self.nk
                self.gate_f = region(name + "_gate_f", [P, DH, E])
                self.gate_h = region(name + "_gate_h", [P, DH, E], F16)
                self.gate_l = region(name + "_gate_l", [P, DH, E], F16)
                self.logits = region(name + "_logits", [P, 2, E])
                self.top = region(name + "_top", [P, B, 8])
                self.pick = region(name + "_pick", [P, B, 8], U32)
                self.pickf = region(name + "_pickf", [P, B, 8])
                self.negmax = region(name + "_negmax", [P, B])
                self.weight = region(name + "_weight", [P, B, 8])
                self.total = region(name + "_total", [P, B])
                self.active = region(name + "_active", [P, B, 8])
                self.cum = region(name + "_cum", [P, B, 8])
                self.one = region(name + "_one", [P, K, E])
                self.picked = region(name + "_picked", [P, K, E])
                self.rank = region(name + "_rank", [P, B, K])
                self.mask = region(name + "_mask", [P, B, E], F16)
                self.named = region(name + "_named", [P, B, K, E], F16)
                self.most = region(name + "_most", [P, 16])
                self.rounds = region(name + "_rounds", [P, 2], I32)
                self.place = region(name + "_place", [P, 4, C], F16)
                self.list = region(name + "_list", [P, tiles, E], I32)
                self.inside = region(name + "_inside", [P, B, K])
                self.share = region(name + "_share", [P, B, K])
                self.yrowf = region(name + "_yrowf", [P, B, K])
                self.yrow = region(name + "_yrow", [P, B, K], I32)
                self.cols = region(name + "_cols", [P, 2, tiles, 4], I32)
                self.xg = region(name + "_xg", [P, 4, 2 * D], F16)
                self.xgT = region(name + "_xgT", [P, 2, 4, C], F16)
                self.ring_up = region(name + "_ring_up", [P, 2, 4, DH * 2 * im])
                self.ring_dn = region(name + "_ring_dn", [P, 2, 4, nk * D])
                self.up_h = region(name + "_up_h", [P, 4, DH * 2 * im], F16)
                self.up_l = region(name + "_up_l", [P, 4, DH * 2 * im], F16)
                self.dn_h = region(name + "_dn_h", [P, 4, nk * D], F16)
                self.dn_l = region(name + "_dn_l", [P, 4, nk * D], F16)
                self.act = region(name + "_act", [P, 2, (2 if not gated else 1) * C])
                self.hid = region(name + "_hid", [P, 2, C]) if gated else None
                self.hid_h = region(name + "_hid_h", [P, 2, nk * C], F16)
                self.hid_l = region(name + "_hid_l", [P, 2, nk * C], F16)
                self.y = region(name + "_y", [P, 4, D])
                self.back = region(name + "_back", [P, 4, D])
                self.y_rows = nc.dram_tensor(name + "_y_rows", [E * C, D], F32).ap()
                edges = ("place placed list cols t xc wuh wdh wl u silu hh hl y ye acc share").split() + ["hread"] * gated
                self.s = routing | {edge: sem(f"{name}_{edge}") for edge in edges}
                self.before = {edge: count * earlier for edge, count in routing_counts.items()}
                if not gated:
                    self.s["hread"] = self.s["silu"]
                self.s_rows = rows_out_sem
                self.s_ring = [sem(f"{name}_ring{i}") for i in range(2)]
                self.s_xg = [sem(f"{name}_xg{i}") for i in range(4)]
                self.s_yw = [sem(f"{name}_yw{i}") for i in range(4)]
                self.s_back = [sem(f"{name}_back{i}") for i in range(4)]

        def load_group(sp, m, group, slot):
            sp.dma_start(m.ring_up[:, slot, :, :], m.w_up[bass.ds(group, 1), :, :, :].rearrange("g p e n -> p (g e) n")
                         ).then_inc(m.s_ring[slot], 16)
            sp.dma_start(m.ring_dn[0:m.im, slot, :, :], m.w_down[bass.ds(group, 1), :, :, :].rearrange("g p e n -> p (g e) n")
                         ).then_inc(m.s_ring[slot], 16)

        def route_sp(sp, m, n):
            sp.dma_start(m.gate_f[:, :, :], m.w_gate.rearrange("(d p) e -> p d e", p=P)).then_inc(m.s["gate"], 16)
            for g in range(2):
                load_group(sp, m, g, g)

        def rows_sp(sp, m):
            for b in range(B):
                sp.wait_ge(m.s["rowsl"], m.before["rowsl"] + b + 1)
                sp.dma_start(rows[b * P:(b + 1) * P, :], row_parts[:, b, :]).then_inc(m.s_rows, 16)

        def rows_act(act, m, n, b):
            act.wait_ge(done.x, n.x + b + 1)
            act.activation(row_parts[:, b, 0:D], X[:, b, :], ACT.Copy).then_inc(m.s["rowsh"], 1)

        def rows_pool(pool, m, b):
            pool.wait_ge(m.s["rowsh"], m.before["rowsh"] + b + 1)
            pool.tensor_tensor(row_parts[:, b, D:2 * D], X[:, b, :], row_parts[:, b, 0:D],
                               ALU.subtract).then_inc(m.s["rowsl"], 1)

        def gate_act(act, m):
            act.wait_ge(m.s["gate"], m.before["gate"] + 16)
            act.activation(m.gate_h[:, :, :], m.gate_f[:, :, :], ACT.Copy, scale=WS).then_inc(m.s["gh"], 1)

        def gate_dve(dve, m):
            dve.wait_ge(m.s["gh"], m.before["gh"] + 1)
            dve.scalar_tensor_tensor(out=m.gate_l[:, :, :], in0=m.gate_f[:, :, :], scalar=WS, in1=m.gate_h[:, :, :],
                                     op0=ALU.mult, op1=ALU.subtract).then_inc(m.s["gl"], 1)

        def logits_pe(pe, m, n, b):
            pe.wait_ge(done.lo, n.lo + b // 2 + 1)
            if b >= 2:
                pe.wait_ge(m.s["lread"], m.before["lread"] + b - 1)
            k = 0
            for d in range(DH):
                for wp, xp in ((m.gate_h, xTh), (m.gate_l, xTh), (m.gate_h, xTl)):
                    mm = pe.matmul(bank[b % 2][:, 0:m.E], xp[:, d, b * P:(b + 1) * P], wp[:, d, :],
                                   start=(k == 0), stop=(k == 3 * DH - 1))
                    k += 1
            mm.then_inc(m.s["logit"], 1)

        def pick_dve(dve, chain, m, b):
            dve.wait_ge(m.s["logit"], m.before["logit"] + b + 1)
            dve.tensor_scalar(m.logits[:, b % 2, :], bank[b % 2][:, 0:m.E], 1.0 / WS, None, ALU.mult).then_inc(m.s["lread"], 1)
            dve.wait_ge(m.s["lread"], m.before["lread"] + b + 1)
            chain.link(dve.max(m.top[:, b, :], m.logits[:, b % 2, :]))
            dve.tensor_scalar(m.negmax[:, b:b + 1], m.top[:, b, 0:1], -1.0, None, ALU.mult).then_inc(m.s["scaled"], 1)
            chain.link(dve.max_index(m.pick[:, b, :], m.top[:, b, :], m.logits[:, b % 2, :]))
            chain.link(dve.tensor_copy(m.pickf[:, b, :], m.pick[:, b, :]))
            chain.link(dve.tensor_tensor(m.one[:, :, :], m.pickf[:, b, 0:m.K, None].broadcast_to([P, m.K, m.E]),
                                         iota[:, None, 0:m.E].broadcast_to([P, m.K, m.E]), ALU.is_equal))

        def soft_act(act, m, b):
            act.wait_ge(m.s["scaled"], m.before["scaled"] + b + 1)
            act.activation(m.weight[:, b, 0:m.K], m.top[:, b, 0:m.K], ACT.Exp, bias=m.negmax[:, b:b + 1],
                           accum_out=m.total[:, b:b + 1]).then_inc(m.s["soft"], 1)

        def keep_dve(dve, chain, m, b, threshold):
            dve.wait_ge(m.s["soft"], m.before["soft"] + b + 1)
            w = m.weight[:, b, 0:m.K]
            chain.link(dve.reciprocal(m.total[:, b:b + 1], m.total[:, b:b + 1]))
            chain.link(dve.tensor_scalar(w, w, m.total[:, b:b + 1], None, ALU.mult))
            if threshold is not None:
                chain.link(dve.memset(m.active[:, b, :], 1.0))
                chain.link(dve.tensor_tensor_scan(m.cum[:, b, :], m.active[:, b, :], w, 0.0, ALU.mult, ALU.add))
                chain.link(dve.tensor_scalar(m.active[:, b, 1:8], m.cum[:, b, 0:7], threshold, None, ALU.is_lt))
                chain.link(dve.tensor_tensor(w, w, m.active[:, b, :], ALU.mult))
                chain.link(dve.tensor_reduce(m.total[:, b:b + 1], w, AX.X, ALU.add))
                chain.link(dve.reciprocal(m.total[:, b:b + 1], m.total[:, b:b + 1]))
                chain.link(dve.tensor_scalar(w, w, m.total[:, b:b + 1], None, ALU.mult))
                chain.link(dve.tensor_tensor(m.one[:, :, :], m.one[:, :, :],
                                             m.active[:, b, :, None].broadcast_to([P, m.K, m.E]), ALU.mult))
            with nc.allow_low_precision(reason="a pick is 0 or 1"):
                dve.tensor_reduce(m.mask[:, b, :], m.one[:, :, :].rearrange("p k e -> p e k"), AX.X, ALU.add).then_inc(m.s["mask"], 1)
            dve.tensor_scalar(m.named[:, b, :, :], m.one[:, :, :], tokens[:, b:b + 1], None, ALU.mult).then_inc(m.s["named"], 1)

        def rank_pe(pe, m, b):
            pe.wait_ge(m.s["mask"], m.before["mask"] + min(b + 1, B))
            if b >= 2:
                pe.wait_ge(m.s["rread"], m.before["rread"] + b - 1)
            for i in range(min(b, B)):
                mm = pe.matmul(bank[2 + b % 2][:, 0:m.E], onesh[:, :], m.mask[:, i, :], start=(i == 0), stop=(b == B and i == B - 1))
            if b < B:
                mm = pe.matmul(bank[2 + b % 2][:, 0:m.E], before[:, :], m.mask[:, b, :], start=(b == 0), stop=True)
            mm.then_inc(m.s["rank"], 1)

        def rank_dve(dve, chain, m, b, threshold):
            dve.wait_ge(m.s["rank"], m.before["rank"] + b + 1)
            dve.tensor_tensor(m.picked[:, :, :], m.one[:, :, :], bank[2 + b % 2][:, None, 0:m.E].broadcast_to([P, m.K, m.E]),
                              ALU.mult).then_inc(m.s["rread"], 1)
            dve.wait_ge(m.s["rread"], m.before["rread"] + b + 1)
            chain.link(dve.tensor_reduce(m.rank[:, b, :], m.picked[:, :, :], AX.X, ALU.add))
            if threshold is not None:
                chain.link(dve.tensor_scalar(m.cum[:, b, :], m.active[:, b, :], -4.0 * T, 4.0 * T, ALU.mult, ALU.add))
                chain.link(dve.tensor_tensor(m.rank[:, b, :], m.rank[:, b, :], m.cum[:, b, :], ALU.add))

        def rounds_dve(dve, chain, m):
            dve.wait_ge(m.s["rank"], m.before["rank"] + B + 1)
            n = m.max_rounds - 1
            chain.link(dve.tensor_reduce(m.most[:, 0:1], bank[2 + B % 2][:, 0:m.E], AX.X, ALU.max))
            chain.link(dve.tensor_scalar(m.most[:, 1:1 + n], iota[:, 1:1 + n], float(m.C), None, ALU.mult))
            chain.link(dve.tensor_scalar(m.most[:, 1:1 + n], m.most[:, 1:1 + n], m.most[:, 0:1], None, ALU.is_lt))
            chain.link(dve.tensor_reduce(m.most[:, 9:10], m.most[:, 1:1 + n], AX.X, ALU.add))
            dve.tensor_scalar(m.rounds[:, 0:1], m.most[:, 9:10], 1.0, None, ALU.add).then_inc(m.s["rounds"], 1)

        def read_rounds(engine, m):
            engine.wait_ge(m.s["rounds"], m.before["rounds"] + 1)
            return engine.value_load(m.rounds[0:1, 0:1], min_val=1, max_val=m.max_rounds)

        def lists_dve(dve, m, r):
            ranks = m.rank.rearrange("p b k -> p (b k)")
            with dve.Fori(0, B * m.K // 8) as g:
                for i in range(8):
                    dve.wait_ge(m.s["placed"], r * (B * m.K) + g * 8 + (i + 1))
                    dve.tensor_scalar(m.place[:, i % 4, :], iotah[:, 0:m.C], ranks[:, bass.ds(g * 8 + i, 1)], None,
                                      ALU.is_equal).then_inc(m.s["place"], 1)
            dve.wait_ge(m.s["placed"], r * (B * m.K) + (B * m.K + 4))
            for i in range(m.nt):
                mm = dve.tensor_copy(m.list[0:m.lot, i, :], bank[6 + i][0:m.lot, 0:m.E])
            mm.then_inc(m.s["list"], 1)
            flat = [v.rearrange("p b k -> p (b k)") for v in (m.rank, m.inside, m.yrowf, m.yrow, m.share)]
            rank, inside, yrowf, yrow, share = flat
            step = [0]

            def then(ins):
                step[0] += 1
                ins.then_inc(m.s["share"], 1)
                dve.wait_ge(m.s["share"], r * 7 + step[0])

            then(dve.tensor_scalar(inside, rank, 0.0, None, ALU.is_ge))
            then(dve.scalar_tensor_tensor(out=inside, in0=rank, scalar=float(m.C), in1=inside, op0=ALU.is_lt, op1=ALU.mult))
            then(dve.scalar_tensor_tensor(out=m.yrowf[:, :, :], in0=m.pickf[:, :, 0:m.K], scalar=float(m.C), in1=m.rank[:, :, :],
                                          op0=ALU.mult, op1=ALU.add))
            then(dve.tensor_tensor(yrowf, yrowf, inside, ALU.mult))
            then(dve.tensor_copy(yrow, yrowf))
            then(dve.tensor_tensor(m.share[:, :, :], m.weight[:, :, 0:m.K], m.inside[:, :, :], ALU.mult))
            then(dve.tensor_scalar(rank, rank, -float(m.C), None, ALU.add))

        def lists_pe(pe, m, r):
            pe.wait_ge(m.s["named"], m.before["named"] + B)
            for q in range(B * m.K):
                b, k = q // m.K, q % m.K
                pe.wait_ge(m.s["place"], r * (B * m.K) + q + 1)
                for i in range(m.nt):
                    mm = pe.matmul(bank[6 + i][0:m.lot, 0:m.E], m.place[:, q % 4, i * m.lot:(i + 1) * m.lot], m.named[:, b, k, :],
                                   start=(q == 0), stop=(q == B * m.K - 1))
                    if i == m.nt - 1:
                        mm.then_inc(m.s["placed"], 1)

        def experts_loop(engine, m, r, ahead, before_loop, step):
            before_loop(r * m.E)
            with engine.Fori(0, m.NI - 1) as it:
                for j in range(8):
                    step(r * m.E + it * 8, it, r * m.NI + it, j, True)
            for j in range(8):
                step(r * m.E + (m.NI - 1) * 8, m.NI - 1, r * m.NI + (m.NI - 1), j, j + ahead < 8)

        def plain(pool):
            pool.sem_inc(s_plain, 1)

        def round_pool(pool, m, r):
            pool.wait_ge(m.s["list"], r + 1)
            plain(pool)

            def fetch(n, it, turn, j):
                for i in range(m.nt):
                    q = j * m.nt + i
                    pool.wait_ge(m.s["t"], n * m.nt + (q + 1))
                    plain(pool)
                    pool.indirect_dma_start(out=m.xg[0:m.lot, q % 4, :], out_offset=None, in_=rows,
                                            in_offset=bass.IndirectOffsetOnAxis(ap=m.cols[0:m.lot, j // 4, i, j % 4:j % 4 + 1], axis=0)
                                            ).then_inc(m.s_xg[q % 4], 16)

            def step(n, it, turn, j, more):
                if j % 4 == 0:
                    plain(pool)
                    pool.tensor_copy(m.cols[0:m.lot, j // 4, :, :], m.list[0:m.lot, :, bass.ds(it * 8 + j, 4)]
                                     ).then_inc(m.s["cols"], 1)
                    pool.wait_ge(m.s["cols"], turn * 2 + (j // 4 + 1))
                fetch(n, it, turn, j)
                pool.wait_ge(m.s_ring[j // 4], 32 * turn + 32)
                pool.wait_ge(m.s["u"], n + j + 1)
                plain(pool)
                pool.tensor_scalar(m.up_h[:, j % 4, :], m.ring_up[:, j // 4, j % 4, :], WS, 0.0, ALU.mult, ALU.add
                                   ).then_inc(m.s["wuh"], 1)

            experts_loop(pool, m, r, 0, lambda n: None, step)
            for i in range(4):
                pool.wait_ge(m.s_yw[i], 16 * (m.E * m.nt // 4) * r + 16 * (m.E * m.nt // 4) + 16)
            pool.wait_ge(m.s["share"], r * 7 + 7)
            for q in range(B * m.K):
                b, k = q // m.K, q % m.K
                pool.wait_ge(m.s["acc"], r * (B * m.K) + q + 1)
                plain(pool)
                pool.indirect_dma_start(out=m.back[:, q % 4, :], out_offset=None, in_=m.y_rows,
                                        in_offset=bass.IndirectOffsetOnAxis(ap=m.yrow[:, b, k:k + 1], axis=0)
                                        ).then_inc(m.s_back[q % 4], 16)

        def round_pe(pe, m, r):
            def turn_tiles(n, turn, j):
                for i in range(m.nt):
                    q = j * m.nt + i
                    pe.wait_ge(m.s_xg[q % 4], 16 * (2 * m.nt) * turn + 16 * (q // 4 + 1))
                    pe.wait_ge(m.s["xc"], n * m.nt + (q + 1))
                    v = bank[q % 2][:, :].bitcast(F16)
                    for c in range(4):
                        mm = pe.transpose(v[:, c * P:c * P + m.lot], m.xg[0:m.lot, q % 4, c * P:(c + 1) * P],
                                          identh[0:m.lot, 0:m.lot])
                    mm.then_inc(m.s["t"], 1)

            def up(n, turn, j):
                pe.wait_ge(m.s["xc"], n * m.nt + (j + 1) * m.nt + 2)
                pe.wait_ge(m.s["wl"], n + j + 1)
                pe.wait_ge(m.s["hread"], n + j + 1)
                for i in range(2):
                    k = 0
                    for d in range(DH):
                        c0 = d * 2 * m.im + i * m.im
                        for wp, xp in ((m.up_h, d), (m.up_l, d), (m.up_h, 2 + d)):
                            mm = pe.matmul(bank[2 + j % 2][0:m.im, i * m.C:(i + 1) * m.C], wp[:, j % 4, c0:c0 + m.im],
                                           m.xgT[:, j % 2, xp, :], start=(k == 0), stop=(k == 3 * DH - 1))
                            k += 1
                mm.then_inc(m.s["u"], 1)

            def down(n, turn, j):
                pe.wait_ge(m.s["hl"], n + j + 3)
                for i in range(m.nt):
                    q = j * m.nt + i
                    pe.wait_ge(m.s["ye"], n * m.nt + (q + 1))
                    k = 0
                    for t in range(m.nk):
                        c0 = t * m.C + i * m.lot
                        for wp, hp in ((m.dn_h, m.hid_h), (m.dn_l, m.hid_h), (m.dn_h, m.hid_l)):
                            mm = pe.matmul(bank[4 + q % 2][0:m.lot, 0:D], hp[0:m.im, j % 2, c0:c0 + m.lot],
                                           wp[0:m.im, j % 4, t * D:(t + 1) * D], start=(k == 0), stop=(k == 3 * m.nk - 1))
                            k += 1
                mm.then_inc(m.s["y"], 1)

            def before_loop(n):
                turn_tiles(n, r * m.NI, 0)
                turn_tiles(n, r * m.NI, 1)
                up(n, None, 0)

            def step(n, it, turn, j, more):
                if more or j + 2 < 8:
                    if j + 2 < 8:
                        turn_tiles(n, turn, j + 2)
                    else:
                        turn_tiles(n + 8, turn + 1, j + 2 - 8)
                if more or j + 1 < 8:
                    if j + 1 < 8:
                        up(n, turn, j + 1)
                    else:
                        up(n + 8, turn + 1, 0)
                down(n, turn, j)

            experts_loop(pe, m, r, 2, before_loop, step)

        def round_act(act, m, r):
            def copy_tiles(n, j):
                if j >= 0:
                    act.wait_ge(m.s["u"], n + j + 3)
                for i in range(m.nt):
                    q = j * m.nt + i
                    act.wait_ge(m.s["t"], n * m.nt + (q + 5))
                    v = bank[q % 2][:, :].bitcast(F16)[:, 0:4 * P].rearrange("p (c t) -> p c t", c=4)
                    act.activation(m.xgT[:, j % 2, :, i * m.lot:(i + 1) * m.lot], v[:, :, 0:m.lot], ACT.Copy).then_inc(m.s["xc"], 1)

            def down_high(n, turn, j):
                act.wait_ge(m.s_ring[j // 4], 32 * turn + 32)
                act.wait_ge(m.s["y"], n + j + 1)
                act.activation(m.dn_h[0:m.im, j % 4, :], m.ring_dn[0:m.im, j // 4, j % 4, :], ACT.Copy, scale=WS
                               ).then_inc(m.s["wdh"], 1)

            def silu(n, j):
                act.wait_ge(m.s["u"], n + j + 5)
                act.wait_ge(m.s["hl"], n + j + 1)
                w = (1 if m.gated else 2) * m.C
                act.activation(m.act[0:m.im, j % 2, :], bank[2 + j % 2][0:m.im, 0:w], ACT.Silu, scale=1.0 / WS
                               ).then_inc(m.s["silu"], 1)

            def before_loop(n):
                for j in range(2):
                    copy_tiles(n, j)
                    down_high(n, r * m.NI, j)

            def step(n, it, turn, j, more):
                silu(n, j)
                if more or j + 2 < 8:
                    if j + 2 < 8:
                        copy_tiles(n, j + 2)
                        down_high(n, turn, j + 2)
                    else:
                        copy_tiles(n + 8, j + 2 - 8)
                        down_high(n + 8, turn + 1, j + 2 - 8)

            experts_loop(act, m, r, 2, before_loop, step)

        def round_dve(dve, m, r):
            def low(n, turn, j):
                dve.wait_ge(m.s["wuh"], n + j + 1)
                dve.scalar_tensor_tensor(out=m.up_l[:, j % 4, :], in0=m.ring_up[:, j // 4, j % 4, :], scalar=WS,
                                         in1=m.up_h[:, j % 4, :], op0=ALU.mult, op1=ALU.subtract)
                dve.wait_ge(m.s["wdh"], n + j + 1)
                dve.scalar_tensor_tensor(out=m.dn_l[0:m.im, j % 4, :], in0=m.ring_dn[0:m.im, j // 4, j % 4, :], scalar=WS,
                                         in1=m.dn_h[0:m.im, j % 4, :], op0=ALU.mult, op1=ALU.subtract).then_inc(m.s["wl"], 1)

            def hidden(n, j):
                dve.wait_ge(m.s["silu"], n + j + 3)
                dve.wait_ge(m.s["y"], n + j + 3)
                if m.gated:
                    dve.scalar_tensor_tensor(out=m.hid[0:m.im, j % 2, :], in0=bank[2 + j % 2][0:m.im, m.C:2 * m.C], scalar=1.0 / WS,
                                             in1=m.act[0:m.im, j % 2, :], op0=ALU.mult, op1=ALU.mult).then_inc(m.s["hread"], 1)
                    dve.wait_ge(m.s["hread"], n + j + 3)
                    h = m.hid
                else:
                    h = m.act
                dve.tensor_copy(m.hid_h[0:m.im, j % 2, :], h[0:m.im, j % 2, :]).then_inc(m.s["hh"], 1)
                dve.wait_ge(m.s["hh"], n + j + 1)
                dve.tensor_tensor(m.hid_l[0:m.im, j % 2, :], h[0:m.im, j % 2, :], m.hid_h[0:m.im, j % 2, :],
                                  ALU.subtract).then_inc(m.s["hl"], 1)

            def rows_out(n, turn, j):
                dve.wait_ge(m.s["y"], n + j + 5)
                for i in range(m.nt):
                    q = j * m.nt + i
                    dve.wait_ge(m.s_yw[q % 4], 16 * (2 * m.nt) * turn + 16 * (q // 4 + 1))
                    dve.tensor_scalar(m.y[0:m.lot, q % 4, :], bank[4 + q % 2][0:m.lot, 0:D], 1.0 / WS, None, ALU.mult
                                      ).then_inc(m.s["ye"], 1)

            def before_loop(n):
                low(n, r * m.NI, 0)
                low(n, r * m.NI, 1)

            def step(n, it, turn, j, more):
                hidden(n, j)
                if more or j + 2 < 8:
                    if j + 2 < 8:
                        low(n, turn, j + 2)
                    else:
                        low(n + 8, turn + 1, j + 2 - 8)
                rows_out(n, turn, j)

            experts_loop(dve, m, r, 2, before_loop, step)
            unit = 8 if m.K == 8 else 2 * m.K
            shares = m.share.rearrange("p b k -> p (b k)")
            with dve.Fori(0, B * m.K // unit) as g:
                for i in range(unit):
                    mine = acc[:, bass.ds(g * (unit // m.K) + i // m.K, 1), :].rearrange("p o n -> p (o n)")
                    dve.wait_ge(m.s_back[i % 4], 16 * (B * m.K // 4) * r + g * (16 * unit // 4) + 16 * (i // 4 + 1))
                    dve.wait_ge(m.s["acc"], r * (B * m.K) + g * unit + (i + 4))
                    dve.scalar_tensor_tensor(out=mine, in0=m.back[:, i % 4, :], scalar=shares[:, bass.ds(g * unit + i, 1)],
                                             in1=mine, op0=ALU.mult, op1=ALU.add).then_inc(m.s["acc"], 1)

        def round_sp(sp, m, r):
            def rows_out(n, it, turn, j):
                for i in range(m.nt):
                    q = j * m.nt + i
                    sp.wait_ge(m.s["ye"], n * m.nt + (q + 3))
                    sp.dma_start(m.y_rows[bass.ds(it * (8 * m.C) + (j * m.C + i * m.lot), m.lot), :], m.y[0:m.lot, q % 4, :]
                                 ).then_inc(m.s_yw[q % 4], 16)

            def step(n, it, turn, j, more):
                rows_out(n, it, turn, j)
                if j % 4 == 3:
                    sp.wait_ge(m.s["wl"], n + j + 1)
                    load_group(sp, m, (it * 2 + 2 + j // 4) if more else j // 4, j // 4)

            with sp.Fori(0, m.NI - 1) as it:
                for j in range(8):
                    step(r * m.E + it * 8, it, r * m.NI + it, j, True)
            for j in range(8):
                step(r * m.E + (m.NI - 1) * 8, m.NI - 1, r * m.NI + (m.NI - 1), j, False)

        def credits_sp(sp, m):
            for edge, free in (("t", 4), ("xc", 2), ("u", 4), ("y", 4), ("hl", 2), ("silu", 2), ("ye", 2),
                               ("placed", 4), ("acc", 4)):
                sp.sem_inc(m.s[edge], free)
            if m.gated:
                sp.sem_inc(m.s["hread"], 2)
            for i in range(4):
                sp.sem_inc(m.s_yw[i], 16)

        second = Region(CONV_WORDS)
        e0 = Experts("e0", second, 64, 6, 88, False, P, 1, ins["gate0"], ins["up0"], ins["down0"], 0)
        row_parts = sb("row_parts", [P, B, 2 * D], F16)
        shared = Region(0, arena2)
        SW = 352
        SI = SW // 4
        sg_f = shared("sg_f", [P, DH, 2 * SW])
        sg_h = shared("sg_h", [P, DH, 2 * SW], F16)
        sg_l = shared("sg_l", [P, DH, 2 * SW], F16)
        sd_f = shared("sd_f", [P, 4, D])
        sd_h = shared("sd_h", [P, 4, D], F16)
        sd_l = shared("sd_l", [P, 4, D], F16)
        sact = shared("sact", [P, 2, HALF])
        shid = shared("shid", [P, 2, HALF])
        shid_h = shared("shid_h", [P, B, HALF], F16)
        shid_l = shared("shid_l", [P, B, HALF], F16)
        weights_in = sem("weights_in")
        weights_high = sem("weights_high")
        weights_low = sem("weights_low")
        c_u = sem("c_u")
        c_act = sem("c_act")
        c_hid = sem("c_hid")
        c_hh = sem("c_hh")
        c_hl = sem("c_hl")
        y_ready = sem("y_ready")
        acc_ready = sem("acc_ready")
        n3 = Norm(3, 2, 1)

        def stage3_sp(sp):
            sp.dma_start(before_f[:, :], ins["c_before"]).then_inc(s_c3, 16)
            sp.dma_start(iota[:, :], ins["c_iota"].partition_broadcast(P)).then_inc(s_c3, 16)
            sp.dma_start(tokens[:, :], ins["c_tokens"]).then_inc(s_c3, 16)
            credits_sp(sp, e0)
            sp.wait_ge(done.x, n1.x + B)
            route_sp(sp, e0, n2)
            sp.wait_ge(b_o, H)
            sp.dma_start(sg_f[:, :, :], ins["shared_up"].rearrange("(d p) n -> p d n", p=P)).then_inc(weights_in, 16)
            sp.dma_start(sd_f[0:SI, :, :], ins["shared_down"].rearrange("(t p) n -> p t n", p=SI)).then_inc(weights_in, 16)
            rows_sp(sp, e0)
            rounds = read_rounds(sp, e0)
            with sp.Fori(0, rounds) as r:
                round_sp(sp, e0, r)
            for i in range(2):
                sp.wait_ge(e0.s_ring[i], rounds * (32 * e0.NI) + 32)

        def stage3_act(act):
            act.wait_ge(s_c3, 48)
            act.activation(before[:, :], before_f[:, :], ACT.Copy).then_inc(s_idh, 1)
            act.activation(identh[:, :], ident[:, :], ACT.Copy).then_inc(s_idh, 1)
            act.activation(iotah[:, :], iota[:, :], ACT.Copy).then_inc(s_idh, 1)
            gate_act(act, e0)
            act.wait_ge(weights_in, 32)
            act.activation(sg_h[:, :, :], sg_f[:, :, :], ACT.Copy, scale=WS).then_inc(weights_high, 1)
            act.activation(sd_h[0:SI, :, :], sd_f[0:SI, :, :], ACT.Copy, scale=WS).then_inc(weights_high, 1)
            for b in range(B):
                rows_act(act, e0, n2, b)
            for b in range(B):
                soft_act(act, e0, b)
                act.wait_ge(c_u, b + 1)
                if b >= 2:
                    act.wait_ge(c_hid, b - 1)
                act.activation(sact[0:SI, b % 2, :], bank[4 + 2 * (b % 2)][0:SI, :], ACT.Silu, scale=1.0 / WS).then_inc(c_act, 1)
                act.wait_ge(c_hid, b + 1)
                act.activation(shid_h[0:SI, b, :], shid[0:SI, b % 2, :], ACT.Copy).then_inc(c_hh, 1)
            rounds = read_rounds(act, e0)
            with act.Fori(0, rounds) as r:
                round_act(act, e0, r)
            for p in range(4):
                norm_hi(act, n3, p)

        def stage3_dve(dve, chain):
            chain.link(dve.memset(onesh[:, :], 1.0))
            gate_dve(dve, e0)
            dve.wait_ge(weights_high, 2)
            dve.scalar_tensor_tensor(out=sg_l[:, :, :], in0=sg_f[:, :, :], scalar=WS, in1=sg_h[:, :, :],
                                     op0=ALU.mult, op1=ALU.subtract).then_inc(weights_low, 1)
            dve.scalar_tensor_tensor(out=sd_l[0:SI, :, :], in0=sd_f[0:SI, :, :], scalar=WS, in1=sd_h[0:SI, :, :],
                                     op0=ALU.mult, op1=ALU.subtract).then_inc(weights_low, 1)
            dve.wait_ge(s_c3, 48)
            dve.wait_ge(s_idh, 3)

            def share_out(b):
                dve.wait_ge(y_ready, b + 1)
                dve.scalar_tensor_tensor(out=acc[:, b, :], in0=bank[b % 2][:, 0:D], scalar=1.0 / WS, in1=X[:, b, :],
                                         op0=ALU.mult, op1=ALU.add).then_inc(acc_ready, 1)

            for b in range(B):
                pick_dve(dve, chain, e0, b)
                keep_dve(dve, chain, e0, b, None)
                dve.wait_ge(c_act, b + 1)
                if b >= 2:
                    dve.wait_ge(c_hh, b - 1)
                dve.scalar_tensor_tensor(out=shid[0:SI, b % 2, :], in0=bank[5 + 2 * (b % 2)][0:SI, :], scalar=1.0 / WS,
                                         in1=sact[0:SI, b % 2, :], op0=ALU.mult, op1=ALU.mult).then_inc(c_hid, 1)
                rank_dve(dve, chain, e0, b, None)
                dve.wait_ge(c_hh, b + 1)
                dve.tensor_tensor(shid_l[0:SI, b, :], shid[0:SI, b % 2, :], shid_h[0:SI, b, :],
                                  ALU.subtract).then_inc(c_hl, 1)
            rounds_dve(dve, chain, e0)
            for b in range(B):
                share_out(b)
            rounds = read_rounds(dve, e0)
            with dve.Fori(0, rounds) as r:
                lists_dve(dve, e0, r)
                round_dve(dve, e0, r)
            norm_all_dve(dve, chain, n3)

        def stage3_pe(pe):
            pe.wait_ge(e0.s["gl"], e0.before["gl"] + 1)
            for b in range(2):
                logits_pe(pe, e0, n2, b)
            pe.wait_ge(weights_low, 2)
            pe.wait_ge(s_idh, 3)

            def shared_up(b):
                th, t = b // 4, b % 4
                if b >= 2:
                    pe.wait_ge(c_hid, b - 1)
                for i in range(2):
                    k = 0
                    c0 = i * SW + t * SI
                    for d in range(DH):
                        for wp, xp in ((sg_h, xTh), (sg_l, xTh), (sg_h, xTl)):
                            mm = pe.matmul(bank[4 + 2 * (b % 2) + i][0:SI, :], wp[:, d, c0:c0 + SI],
                                           xp[:, d, th * HALF:(th + 1) * HALF], start=(k == 0), stop=(k == 3 * DH - 1))
                            k += 1
                mm.then_inc(c_u, 1)

            def shared_down(th):
                pe.wait_ge(c_hl, 4 * th + 4)
                for i in range(4):
                    b = 4 * th + i
                    if b >= 2:
                        pe.wait_ge(acc_ready, b - 1)
                    k = 0
                    for t in range(4):
                        for wp, hp in ((sd_h, shid_h), (sd_l, shid_h), (sd_h, shid_l)):
                            mm = pe.matmul(bank[b % 2][:, 0:D], hp[0:SI, 4 * th + t, i * P:(i + 1) * P], wp[0:SI, t, :],
                                           start=(k == 0), stop=(k == 11))
                            k += 1
                    mm.then_inc(y_ready, 1)

            for b in range(B):
                shared_up(b)
                rank_pe(pe, e0, b)
                if b + 2 < B:
                    logits_pe(pe, e0, n2, b + 2)
            rank_pe(pe, e0, B)
            pe.wait_ge(e0.s["lread"], e0.before["lread"] + B)
            shared_down(0)
            shared_down(1)
            rounds = read_rounds(pe, e0)
            with pe.Fori(0, rounds) as r:
                lists_pe(pe, e0, r)
                round_pe(pe, e0, r)
            for p in range(4):
                norm_transpose(pe, n3, p)

        def stage3_pool(pool, chain):
            for b in range(B):
                rows_pool(pool, e0, b)
            pool.wait_ge(e0.s_rows, e0.before["rows"] + 16 * B)
            rounds = read_rounds(pool, e0)
            with pool.Fori(0, rounds) as r:
                round_pool(pool, e0, r)
            for b in range(B):
                norm_rstd(pool, chain, n3, b)

        retain = Region(0, arena2)
        r_wf = retain("r_wf", [P, DH, 5, D])
        r_wh = retain("r_wh", [P, DH, 5, D], F16)
        r_wl = retain("r_wl", [P, DH, 5, D], F16)
        turns = retain("turns", [P, 4, DH, P])
        rqk = retain("rqk", [P, 2, DH, T])
        part = retain("part", [P, 2, 2, HALF])
        fade = retain("fade", [P, P])
        att = retain("att", [P, 2, P])
        tables_in = sem("tables_in")
        d_p = sem("d_p")
        d_pr = sem("d_pr")
        d_qk = sem("d_qk")
        d_v = sem("d_v")
        d_vc = sem("d_vc")
        scores_ready = sem("scores_ready")
        d_a = sem("d_a")
        n4 = Norm(4, 2, 2)

        def stage4_sp(sp):
            sp.wait_ge(acc_ready, B)
            sp.dma_start(r_wf[:, :, :, :], ins["w_qkv1"].rearrange("(d p) (c n) -> p d c n", p=P, c=5)).then_inc(weights_in, 16)
            sp.dma_start(turns[:, :, :, :], ins["c_turns"].rearrange("c (d p) t -> p c d t", p=P)).then_inc(tables_in, 16)
            sp.dma_start(fade[:, :], ins["c_fade"]).then_inc(tables_in, 16)

        def stage4_pe(pe):
            pe.wait_ge(weights_high, 2 + 1)
            pe.wait_ge(weights_low, 2 + 1)
            for u in range(8):
                th, o, qk = u // 4, u // 2 % 2, u % 2
                pe.wait_ge(done.lo, n3.lo + 2 * th + 2)
                if u >= 2:
                    pe.wait_ge(d_pr, u - 1)
                for i in range(2):
                    k = 0
                    for d in range(DH):
                        for wp, xp in ((r_wh, xTh), (r_wl, xTh), (r_wh, xTl)):
                            mm = pe.matmul(bank[2 * (u % 2) + i][:, :], wp[:, d, 2 * qk + i, o * P:(o + 1) * P],
                                           xp[:, d, th * HALF:(th + 1) * HALF], start=(k == 0), stop=(k == 3 * DH - 1))
                            k += 1
                mm.then_inc(d_p, 1)
            for b in range(B):
                if b >= 2:
                    pe.wait_ge(d_vc, b - 1)
                k = 0
                for d in range(DH):
                    for wp, xp in ((r_wh, xTh), (r_wl, xTh), (r_wh, xTl)):
                        mm = pe.matmul(bank[4 + b % 2][:, 0:D], xp[:, d, b * P:(b + 1) * P], wp[:, d, 4, :],
                                       start=(k == 0), stop=(k == 3 * DH - 1))
                        k += 1
                mm.then_inc(d_v, 1)
            pe.wait_ge(d_pr, 8)

            def scores(b):
                pe.wait_ge(d_qk, 4 * (b // 4) + 4)
                if b >= 2:
                    pe.wait_ge(d_a, b - 1)
                for d in range(DH):
                    mm = pe.matmul(bank[b % 2][:, 0:P], rqk[:, 1, d, b * P:(b + 1) * P], rqk[:, 0, d, b * P:(b + 1) * P],
                                   start=(d == 0), stop=(d == DH - 1))
                mm.then_inc(scores_ready, 1)

            for b in range(B + 1):
                if b < B:
                    scores(b)
                if b >= 1:
                    pe.wait_ge(d_a, b)
                    pe.wait_ge(d_vc, b)
                    if b >= 3:
                        pe.wait_ge(done.sum, n4.sum + b - 2)
                    pe.matmul(bank[2 + (b - 1) % 2][:, 0:D], att[:, (b - 1) % 2, :], acc[:, b - 1, :], start=True, stop=True
                              ).then_inc(y_ready, 1)
            for p in range(4):
                norm_transpose(pe, n4, p)

        def stage4_act(act):
            act.wait_ge(weights_in, 32 + 16)
            act.activation(r_wh[:, :, :, :], r_wf[:, :, :, :], ACT.Copy, scale=WS).then_inc(weights_high, 1)
            act.wait_ge(done.x, n3.x + B)
            for b in range(B):
                act.wait_ge(d_v, b + 1)
                act.activation(acc[:, b, :], bank[4 + b % 2][:, 0:D], ACT.Copy, scale=1.0 / WS).then_inc(d_vc, 1)
            for p in range(4):
                act.wait_ge(done.t, n4.t + p + 1)
                act.activation(xTf[:, :, p * 256:(p + 1) * 256], bank[6 + p % 2][:, :].rearrange("q (d t) -> q d t", d=DH),
                               ACT.Copy).then_inc(done.lo, 1)

        def stage4_dve(dve, chain):
            dve.wait_ge(weights_high, 2 + 1)
            dve.scalar_tensor_tensor(out=r_wl[:, :, :, :].rearrange("p d c n -> p (d c n)"),
                                     in0=r_wf[:, :, :, :].rearrange("p d c n -> p (d c n)"), scalar=WS,
                                     in1=r_wh[:, :, :, :].rearrange("p d c n -> p (d c n)"),
                                     op0=ALU.mult, op1=ALU.subtract).then_inc(weights_low, 1)
            dve.wait_ge(tables_in, 32)
            for u in range(8):
                th, o, qk = u // 4, u // 2 % 2, u % 2
                dve.wait_ge(d_p, u + 1)
                if u >= 2:
                    dve.wait_ge(d_qk, u - 1)
                for i in range(2):
                    mm = dve.scalar_tensor_tensor(out=part[:, u % 2, i, :].rearrange("p (b t) -> p b t", b=4),
                                                  in0=bank[2 * (u % 2) + i][:, :].rearrange("p (b t) -> p b t", b=4), scalar=1.0 / WS,
                                                  in1=turns[:, 2 * qk + i, o, None, :].broadcast_to([P, 4, P]),
                                                  op0=ALU.mult, op1=ALU.mult)
                mm.then_inc(d_pr, 1)

            def fade_scores(b):
                dve.wait_ge(scores_ready, b + 1)
                if b >= 2:
                    dve.wait_ge(y_ready, B + b - 1)
                dve.tensor_tensor(att[:, b % 2, :], bank[b % 2][:, 0:P], fade[:, :], ALU.mult).then_inc(d_a, 1)

            for b in range(B + 2):
                if b < B:
                    fade_scores(b)
                if 1 <= b < B + 1:
                    dve.wait_ge(y_ready, B + b)
                    norm_sum(dve, chain, n4, b - 1, bank[2 + (b - 1) % 2][:, 0:D], 1.0)
                if b >= 2:
                    norm_apply(dve, n4, b - 2)

        def stage4_pool(pool, chain):
            for u in range(8):
                th, o, qk = u // 4, u // 2 % 2, u % 2
                pool.wait_ge(d_pr, u + 1)
                pool.tensor_tensor(rqk[:, qk, o, th * HALF:(th + 1) * HALF], part[:, u % 2, 0, :], part[:, u % 2, 1, :],
                                   ALU.add).then_inc(d_qk, 1)
            for b in range(B):
                norm_rstd(pool, chain, n4, b)

        look = Region()
        ctxT = look("ctxT", [P, DH, T])
        ctxm = look("ctxm", [P, B, D])
        xTf = look("xTf", [P, DH, T])
        seen = look("seen", [P, T])
        unseen = look("unseen", [P, T])
        seen8 = look("seen8", [P, T], U8)
        sc5 = look("sc5", [P, 2, P])
        p5 = look("p5", [P, 2, P])
        pT5 = look("pT5", [P, 2, P])
        valid = sb("valid", [P, B])
        peak = sb("peak", [P, B])
        sum5 = sb("sum5", [P, B])
        f_sr = sem("f_sr")
        f_mx = sem("f_mx")
        f_e = sem("f_e")
        ctx_in = sem("ctx_in")
        n5 = Norm(5, 3, 2)

        def stage5_sp(sp):
            sp.wait_ge(done.sum, n2.sum + B)
            sp.dma_start(ctxT[:, :, :], ins["ctxT"].rearrange("(d p) t -> p d t", p=P)).then_inc(ctx_in, 16)
            sp.dma_start(ctxm[:, :, :], ins["ctx"].rearrange("b p d -> p b d")).then_inc(ctx_in, 16)
            sp.dma_start(seen8[:, :], ins["mask"].partition_broadcast(P)).then_inc(ctx_in, 16)

        def stage5_pe(pe):
            pe.wait_ge(ctx_in, 48)

            def scores(b):
                pe.wait_ge(done.lo, n4.lo + b // 2 + 1)
                if b >= 2:
                    pe.wait_ge(f_sr, b - 1)
                for d in range(DH):
                    mm = pe.matmul(bank[b % 2][:, 0:P], xTf[:, d, b * P:(b + 1) * P], ctxT[:, d, b * P:(b + 1) * P],
                                   start=(d == 0), stop=(d == DH - 1))
                mm.then_inc(scores_ready, 1)

            def turn(b):
                pe.wait_ge(f_e, b + 1)
                if b >= 2:
                    pe.wait_ge(d_vc, B + b - 1)
                pe.transpose(bank[2 + b % 2][:, 0:P], p5[:, b % 2, :], ident[:, :]).then_inc(d_v, 1)

            def read(b):
                pe.wait_ge(d_vc, B + b + 1)
                if b >= 2:
                    pe.wait_ge(done.sum, n5.sum + b - 1)
                pe.matmul(bank[4 + b % 2][:, 0:D], pT5[:, b % 2, :], ctxm[:, b, :], start=True, stop=True).then_inc(y_ready, 1)

            for b in range(B + 2):
                if b < B:
                    scores(b)
                if 1 <= b < B + 1:
                    turn(b - 1)
                if b >= 2:
                    read(b - 2)
            for p in range(4):
                norm_transpose(pe, n5, p)

        def stage5_act(act):
            def weigh(b):
                act.wait_ge(f_mx, b + 1)
                if b >= 2:
                    act.wait_ge(d_v, B + b - 1)
                act.activation(p5[:, b % 2, :], sc5[:, b % 2, :], ACT.Exp, bias=peak[:, b:b + 1],
                               accum_out=sum5[:, b:b + 1]).then_inc(f_e, 1)

            def copy(b):
                act.wait_ge(d_v, B + b + 1)
                if b >= 2:
                    act.wait_ge(y_ready, 2 * B + b - 1)
                act.activation(pT5[:, b % 2, :], bank[2 + b % 2][:, 0:P], ACT.Copy).then_inc(d_vc, 1)

            for b in range(B + 1):
                if b < B:
                    weigh(b)
                if b >= 1:
                    copy(b - 1)
            for p in range(4):
                norm_hi(act, n5, p)

        def masks_dve(dve, chain):
            dve.wait_ge(ctx_in, 48)
            chain.link(dve.tensor_copy(seen[:, :], seen8[:, :]))
            chain.link(dve.tensor_scalar(unseen[:, :], seen[:, :], -1.0, 1e30, ALU.add, ALU.mult))
            chain.link(dve.tensor_reduce(valid[:, :], seen[:, :].rearrange("p (b m) -> p b m", b=B), AX.X, ALU.max))

        def stage5_dve(dve, chain):
            def mask(b):
                dve.wait_ge(scores_ready, B + b + 1)
                if b >= 2:
                    dve.wait_ge(f_e, b - 1)
                dve.scalar_tensor_tensor(out=sc5[:, b % 2, :], in0=bank[b % 2][:, 0:P], scalar=float(D) ** -0.5,
                                         in1=seen[:, b * P:(b + 1) * P], op0=ALU.mult, op1=ALU.mult).then_inc(f_sr, 1)
                dve.wait_ge(f_sr, b + 1)
                chain.link(dve.tensor_tensor(sc5[:, b % 2, :], sc5[:, b % 2, :], unseen[:, b * P:(b + 1) * P], ALU.add))
                chain.link(dve.tensor_reduce(peak[:, b:b + 1], sc5[:, b % 2, :], AX.X, ALU.max))
                dve.tensor_scalar(peak[:, b:b + 1], peak[:, b:b + 1], -1.0, None, ALU.mult).then_inc(f_mx, 1)

            def add(b):
                dve.wait_ge(f_e, b + 1)
                chain.link(dve.reciprocal(sum5[:, b:b + 1], sum5[:, b:b + 1]))
                chain.link(dve.tensor_tensor(sum5[:, b:b + 1], sum5[:, b:b + 1], valid[:, b:b + 1], ALU.mult))
                dve.wait_ge(y_ready, 2 * B + b + 1)
                norm_sum(dve, chain, n5, b, bank[4 + b % 2][:, 0:D], sum5[:, b:b + 1])

            for b in range(B + 4):
                if b < B:
                    mask(b)
                if 2 <= b < B + 2:
                    add(b - 2)
                if 3 <= b < B + 3:
                    norm_apply(dve, n5, b - 3)
            for p in range(4):
                norm_lo(dve, n5, p)

        def stage5_pool(pool, chain):
            for b in range(B):
                norm_rstd(pool, chain, n5, b)

        e1 = Experts("e1", Region(CONV_WORDS), 32, 8, 96, True, 96, 2, ins["gate1"], ins["up1"], ins["down1"], 1)
        n6 = Norm(6, 4, 3)
        KEEP = 0.8

        def stage6_sp(sp):
            credits_sp(sp, e1)
            sp.wait_ge(done.x, n3.x + B)
            route_sp(sp, e1, n5)
            rows_sp(sp, e1)
            rounds = read_rounds(sp, e1)
            with sp.Fori(0, rounds) as r:
                round_sp(sp, e1, r)
            for i in range(2):
                sp.wait_ge(e1.s_ring[i], rounds * (32 * e1.NI) + 32)
            for b in range(B):
                sp.wait_ge(done.x, n6.x + b + 1)
                sp.dma_start(out[b, :, :], X[:, b, :]).then_inc(s_out, 16)
            sp.wait_ge(s_out, 16 * B)

        def stage6_act(act):
            gate_act(act, e1)
            for b in range(B):
                rows_act(act, e1, n5, b)
            for b in range(B):
                soft_act(act, e1, b)
            rounds = read_rounds(act, e1)
            with act.Fori(0, rounds) as r:
                round_act(act, e1, r)

        def stage6_dve(dve, chain):
            gate_dve(dve, e1)
            for b in range(B):
                pick_dve(dve, chain, e1, b)
                keep_dve(dve, chain, e1, b, KEEP)
                dve.tensor_copy(acc[:, b, :], X[:, b, :]).then_inc(acc_ready, 1)
                rank_dve(dve, chain, e1, b, KEEP)
            rounds_dve(dve, chain, e1)
            dve.wait_ge(acc_ready, B + B)
            rounds = read_rounds(dve, e1)
            with dve.Fori(0, rounds) as r:
                lists_dve(dve, e1, r)
                round_dve(dve, e1, r)
            for b in range(B + 1):
                if b < B:
                    norm_stats(dve, chain, n6, b, acc[:, b, :])
                if b >= 1:
                    norm_apply(dve, n6, b - 1, acc[:, b - 1, :])

        def stage6_pe(pe):
            pe.wait_ge(e1.s["gl"], e1.before["gl"] + 1)
            for b in range(2):
                logits_pe(pe, e1, n5, b)
            for b in range(B):
                rank_pe(pe, e1, b)
                if b + 2 < B:
                    logits_pe(pe, e1, n5, b + 2)
            rank_pe(pe, e1, B)
            rounds = read_rounds(pe, e1)
            with pe.Fori(0, rounds) as r:
                lists_pe(pe, e1, r)
                round_pe(pe, e1, r)

        def stage6_pool(pool, chain):
            for b in range(B):
                rows_pool(pool, e1, b)
            pool.wait_ge(e1.s_rows, e1.before["rows"] + 16 * B)
            rounds = read_rounds(pool, e1)
            with pool.Fori(0, rounds) as r:
                round_pool(pool, e1, r)
            for b in range(B):
                norm_rstd(pool, chain, n6, b)


        block = ctx.enter_context(nc.Block())

        @block.sync
        def _(sp):
            stage1_sp(sp)
            stage2_sp(sp)
            stage3_sp(sp)
            stage4_sp(sp)
            stage5_sp(sp)
            stage6_sp(sp)

        @block.tensor
        def _(pe):
            stage1_pe(pe)
            stage2_pe(pe)
            stage3_pe(pe)
            stage4_pe(pe)
            stage5_pe(pe)
            stage6_pe(pe)

        @block.scalar
        def _(act):
            stage1_act(act)
            stage2_act(act)
            stage3_act(act)
            stage4_act(act)
            stage5_act(act)
            stage6_act(act)

        @block.vector
        def _(dve):
            chain = Chain(dve, dve_chain_sem)
            stage1_dve(dve, chain)
            stage2_dve(dve, chain)
            stage3_dve(dve, chain)
            stage4_dve(dve, chain)
            masks_dve(dve, chain)
            stage5_dve(dve, chain)
            stage6_dve(dve, chain)

        @block.gpsimd
        def _(pool):
            chain = Chain(pool, pool_chain_sem)
            stage1_pool(pool, chain)
            stage2_pool(pool, chain)
            stage3_pool(pool, chain)
            stage4_pool(pool, chain)
            stage5_pool(pool, chain)
            stage6_pool(pool, chain)

def _heads_apart(w):
    apart = np.zeros((D, H, 32), w.dtype)
    apart[:, :, :HD] = w.reshape(D, H, HD)
    return apart.reshape(D, 512)


def _way_up(w):
    e, n, _ = w.shape
    return w.reshape(e // 4, 4, n, DH, P).transpose(0, 4, 1, 3, 2).reshape(e // 4, P, 4, DH * n)


def _way_down(w, tiles):
    e, _, n = w.shape
    return w.reshape(e // 4, 4, D, tiles, n // tiles).transpose(0, 4, 1, 3, 2).reshape(e // 4, n // tiles, 4, tiles * D)


def _turns():
    at = np.arange(P, dtype=np.float32)
    pair = np.arange(0, D, 2, dtype=np.float32)
    scale = ((pair + np.float32(0.4 * D)) / np.float32(1.4 * D))[None, :] ** (at / np.float32(SCALE_BASE))[:, None]
    angle = at[:, None] * (np.float32(1.0) / np.float32(10000.0) ** (np.arange(D // 2, dtype=np.float32) / np.float32(D // 2)))
    sign = np.where(np.arange(D) % 2 == 0, -1.0, 1.0)[None, :]
    tables = []
    for s in (scale, np.float32(1.0) / scale):
        tables.append(np.repeat(np.cos(angle) * s, 2, axis=1).T)
        tables.append((np.repeat(np.sin(angle) * s, 2, axis=1) * sign).T)
    return np.stack(tables)


def _swap_pairs(w):
    return w.reshape(D, D // 2, 2)[:, :, ::-1].reshape(D, D)


def _constants():
    i = np.arange(P)
    key, query = i[:, None], i[None, :]
    c = {
        "c_ident": np.eye(P),
        "c_diff": np.maximum(query - key, 0),
        "c_causal": query >= key,
        "c_turns": _turns(),
        "c_fade": np.where(query >= key, GAMMA ** np.maximum(query - key, 0), 0.0),
        "c_before": key < query,
        "c_iota": np.arange(IOTA),
        "c_tokens": key + P * np.arange(B),
        "c_anti": key + query == P - 1,
    }
    return {k: np.ascontiguousarray(v, np.float32) for k, v in c.items()}


def _layout(i):
    w = i["L0_attn_W_qkvu"].T
    a = {
        "x": i["x"],
        "xT": i["x"].reshape(T, D).T,
        "w_qkvu": np.concatenate([_heads_apart(w[:, :D]), _heads_apart(w[:, D:2 * D]), w[:, 2 * D:]], axis=1),
        "w_out": i["L0_attn_W_out"].T,
        "ctx_rev": i["ctx_2048"].transpose(2, 1, 0).reshape(DH, P, P * B)[:, ::-1].transpose(1, 0, 2).reshape(P, -1),
        "filters": np.concatenate([np.zeros((H, P - 1), np.float32), i["L0_xattn_ssm_kernel"]], axis=1),
        "w_qkv1": np.concatenate([i["L1_attn_W_Q"], _swap_pairs(i["L1_attn_W_Q"]), i["L1_attn_W_K"],
                                  _swap_pairs(i["L1_attn_W_K"]), i["L1_attn_W_V"]], axis=1),
        "ctx": i["ctx_2048"],
        "ctxT": i["ctx_2048"].reshape(T, D).T,
        "mask": i["mask_BxS2_bk0"].reshape(T),
        "gate1": i["L1_ffn_gate_weight"].T,
        "up1": _way_up(i["L1_ffn_gate_up_proj"]),
        "down1": _way_down(i["L1_ffn_down_proj"], 1),
        "gate0": i["L0_ffn_gate_w"].T,
        "up0": _way_up(i["L0_ffn_experts_w1"]),
        "down0": _way_down(i["L0_ffn_experts_w2"], 2),
        "shared_up": i["L0_ffn_shared_gate_up"].T,
        "shared_down": i["L0_ffn_shared_down"].T,
        "conv_d": i["L0_xattn_D"],
        "slope": i["L0_attn_slope_rate"].reshape(H),
    }
    return {k: np.ascontiguousarray(v) for k, v in a.items()} | _constants()


def kernel(**inputs):
    import concourse.bacc as bacc
    from concourse.bass_utils import run_bass_kernel_spmd

    nc = bacc.Bacc("TRN2", target_bir_lowering=False, num_devices=1)
    laid_out = _layout({name: np.asarray(value) for name, value in inputs.items()})
    arrays, ins = {}, {}
    for name, array in laid_out.items():
        arrays[f"in_{name}_dram"] = array
        ins[name] = nc.dram_tensor(f"in_{name}_dram", array.shape, mybir.dt.from_np(array.dtype), kind="ExternalInput").ap()
    out = nc.dram_tensor("out_0_dram", (B, P, D), F32, kind="ExternalOutput").ap()
    build_program(nc, ins, out)
    return run_bass_kernel_spmd(nc, [arrays], core_ids=[0]).results[0]["out_0_dram"]
```

```python
import numpy as np
from contextlib import ExitStack

import concourse.bass as bass
from concourse import mybir

F32 = mybir.dt.float32
F16 = mybir.dt.float16
I32 = mybir.dt.int32
U32 = mybir.dt.uint32
U8 = mybir.dt.uint8
ALU = mybir.AluOpType
ACT = mybir.ActivationFunctionType
AX = mybir.AxisListType

P = 128
D = 256
DH = D // P
B = 8
T = B * P
H = 16
HD = D // H
CJ = P // H
WS = 256.0
GAMMA = 0.96875
SCALE_BASE = 64
LN_EPS = 1e-5
RMS_EPS = 1e-6
ARENA = 28672
ARENA2 = 14336
BACK = 8192
PICKS = 11008
CONV_WORDS = 9216
IOTA = 192
HALF = T // 2


class Chain:

    def __init__(self, engine, semaphore):
        self.engine, self.semaphore, self.n = engine, semaphore, 0

    def link(self, instruction):
        self.n += 1
        instruction.then_inc(self.semaphore, 1)
        self.engine.wait_ge(self.semaphore, self.n)

    def mark(self, instruction):
        self.n += 1
        instruction.then_inc(self.semaphore, 1)
        return self.n


def build_program(nc, ins, out):
    with ExitStack() as ctx:
        def sb(name, shape, dt=F32):
            return ctx.enter_context(nc.sbuf_tensor(name, shape, dt))

        def sem(name):
            return ctx.enter_context(nc.semaphore(name))

        arena = sb("arena", [P, ARENA])
        arena2 = sb("arena2", [P, ARENA2])

        class Region:

            def __init__(self, start=0, memory=None):
                self.at = start
                self.memory = arena if memory is None else memory

            def __call__(self, name, shape, dt=F32):
                size = int(np.prod(shape[1:]))
                words = {F16: size // 2, U8: size // 4}.get(dt, size)
                view = self.memory[0:shape[0], self.at:self.at + words]
                self.at += words
                assert self.at <= self.memory.shape[1], (name, self.at)
                if dt != F32:
                    view = view.bitcast(dt)
                names = " ".join("abcde"[:len(shape) - 1])
                sizes = dict(zip("abcde", shape[1:]))
                return view.rearrange(f"p ({names}) -> p {names}", **sizes) if len(shape) > 2 else view

        bank = [ctx.enter_context(nc.psum_tensor(f"bank{i}", [P, 512], F32)) for i in range(8)]

        X = sb("X", [P, B, D])
        R = sb("R", [P, 4, D])
        xTh = sb("xTh", [P, DH, T], F16)
        xTl = sb("xTl", [P, DH, T], F16)
        stats = sb("stats", [P, 4, 6])
        mv = sb("mv", [P, B, 2])
        veps = sb("veps", [P, B])
        rstd = sb("rstd", [P, B])
        minus_half = sb("minus_half", [P, B])
        ident = sb("ident", [P, P])
        s_x = sem("s_x")
        s_ident = sem("s_ident")
        s_mh = sem("s_mh")
        s_out = sem("s_out")

        early = Region()
        xT0 = early("xT0", [P, DH, T])
        w1f = early("w1f", [P, DH, 3, 512])
        w1h = early("w1h", [P, DH, 3, 512], F16)
        w1l = early("w1l", [P, DH, 3, 512], F16)
        wof = early("wof", [P, DH, D])
        woh = early("woh", [P, DH, D], F16)
        wol = early("wol", [P, DH, D], F16)
        later = Region(early.at)
        fresh = early("fresh", [P, 4, HALF])
        fresh_h = early("fresh_h", [P, 2, HALF], F16)
        lows = early("lows", [P, 1])
        qh = early("qh", [P, 4, T], F16)
        ql = early("ql", [P, 4, T], F16)
        kk = early("kk", [P, 4, T], F16)
        vh = early("vh", [P, B, D], F16)
        vl = early("vl", [P, B, D], F16)
        uu = early("uu", [P, B, D])
        diff = early("diff", [P, P])
        causal = early("causal", [P, P])
        slope = early("slope", [P, H])
        nslope = early("nslope", [P, H])
        decay = early("decay", [P, H, P])
        prob = early("prob", [P, 3, 4, P])
        ph = early("ph", [P, 3, 4, P], F16)
        pl = early("pl", [P, 3, 4, P], F16)
        junk = later("junk", [P, D])
        ssq = early("ssq", [P, B])
        rms = early("rms", [P, B])
        gated = later("gated", [P, 4, D])
        gTh = early("gTh", [P, 2, DH, P], F16)
        gTl = early("gTl", [P, 2, DH, P], F16)

        a_x = sem("a_x")
        a_w = [sem(f"a_w{i}") for i in range(3)]
        weights_in = sem("weights_in")
        a_c = sem("a_c")
        a_xh = sem("a_xh")
        a_xl = sem("a_xl")
        a_wh = sem("a_wh")
        a_wl = sem("a_wl")
        weights_high = sem("weights_high")
        weights_low = sem("weights_low")
        a_ns = sem("a_ns")
        a_dec = sem("a_dec")
        a_decm = sem("a_decm")
        a_qk = sem("a_qk")
        a_qkc = sem("a_qkc")
        a_vu = sem("a_vu")
        a_qks = sem("a_qks")
        a_kh = sem("a_kh")
        a_vh = sem("a_vh")
        a_vl = sem("a_vl")
        a_ph = sem("a_ph")
        a_pl = sem("a_pl")
        a_sc = sem("a_sc")
        a_pr = sem("a_pr")
        a_pv = sem("a_pv")
        a_sq = sem("a_sq")
        a_rms = sem("a_rms")
        a_g = sem("a_g")
        a_gt = sem("a_gt")
        a_gh = sem("a_gh")
        a_gl = sem("a_gl")
        a_y = sem("a_y")
        dve_chain_sem = sem("dve_chain")
        pool_chain_sem = sem("pool_chain")

        class NormDone:
            sum = sem("norm_sum")
            mv = sem("norm_mv")
            rstd = sem("norm_rstd")
            x = sem("norm_x")
            t = sem("norm_t")
            hi = sem("norm_hi")
            lo = sem("norm_lo")

        done = NormDone

        class Norm:

            def __init__(self, stage, sums, highs):
                self.sum = B * sums
                self.mv = self.rstd = self.x = B * (stage - 1)
                self.t = self.lo = B // 2 * (stage - 1)
                self.hi = B // 2 * highs

        n1 = Norm(1, 0, 0)

        def norm_sum(dve, chain, n, b, y, scale):
            if b >= 4:
                dve.wait_ge(done.x, n.x + b - 3)
            dve.scalar_tensor_tensor(out=R[:, b % 4, :], in0=y, scalar=scale, in1=X[:, b, :],
                                     op0=ALU.mult, op1=ALU.add).then_inc(done.sum, 1)
            dve.wait_ge(done.sum, n.sum + b + 1)
            norm_stats(dve, chain, n, b, R[:, b % 4, :])

        def norm_stats(dve, chain, n, b, src):
            chain.link(dve.bn_stats(stats[:, b % 4, :], src))
            dve.bn_aggr(mv[:, b, :], stats[:, b % 4, :]).then_inc(done.mv, 1)

        def norm_rstd(pool, chain, n, b):
            pool.wait_ge(done.mv, n.mv + b + 1)
            chain.link(pool.tensor_scalar(veps[:, b:b + 1], mv[:, b, 1:2], LN_EPS, None, ALU.add))
            pool.tensor_tensor(rstd[:, b:b + 1], veps[:, b:b + 1], minus_half[:, 0:1], ALU.pow).then_inc(done.rstd, 1)

        def norm_apply(dve, n, b, src=None):
            dve.wait_ge(done.rstd, n.rstd + b + 1)
            dve.tensor_scalar(X[:, b, :], R[:, b % 4, :] if src is None else src, mv[:, b, 0:1], rstd[:, b:b + 1],
                              ALU.subtract, ALU.mult).then_inc(done.x, 1)

        def norm_transpose(pe, n, p):
            pe.wait_ge(done.x, n.x + 2 * p + 2)
            if p >= 2:
                pe.wait_ge(done.lo, n.lo + p - 1)
            v = bank[6 + p % 2][:, :].rearrange("q (d b t) -> q d b t", d=DH, b=2)
            for i in range(2):
                for d in range(DH):
                    mm = pe.transpose(v[:, d, i, :], X[:, 2 * p + i, d * P:(d + 1) * P], ident[:, :])
            mm.then_inc(done.t, 1)

        def norm_hi(act, n, p):
            act.wait_ge(done.t, n.t + p + 1)
            act.activation(xTh[:, :, p * 256:(p + 1) * 256], bank[6 + p % 2][:, :].rearrange("q (d t) -> q d t", d=DH),
                           ACT.Copy).then_inc(done.hi, 1)

        def norm_lo(dve, n, p):
            dve.wait_ge(done.hi, n.hi + p + 1)
            dve.tensor_tensor(xTl[:, :, p * 256:(p + 1) * 256], bank[6 + p % 2][:, :].rearrange("q (d t) -> q d t", d=DH),
                              xTh[:, :, p * 256:(p + 1) * 256], ALU.subtract).then_inc(done.lo, 1)

        def stage1_sp(sp):
            sp.dma_start(xT0[:, :, :], ins["xT"].rearrange("(d p) t -> p d t", p=P)).then_inc(a_x, 16)
            wv = ins["w_qkvu"].rearrange("(d p) (c n) -> p d c n", p=P, c=3)
            for c in range(3):
                sp.dma_start(w1f[:, :, c, :], wv[:, :, c, :]).then_inc(a_w[c], 16)
            sp.dma_start(X[:, :, :], ins["x"].rearrange("b p d -> p b d")).then_inc(s_x, 16)
            sp.dma_start(lows[:, :], ins["c_lows"]).then_inc(s_x, 16)
            sp.dma_start(diff[:, :], ins["c_diff"]).then_inc(a_c, 16)
            sp.dma_start(causal[:, :], ins["c_causal"]).then_inc(a_c, 16)
            sp.dma_start(slope[:, :], ins["slope"].partition_broadcast(P)).then_inc(a_c, 16)
            sp.dma_start(ident[:, :], ins["c_ident"]).then_inc(s_ident, 16)
            sp.dma_start(wof[:, :, :], ins["w_out"].rearrange("(d p) n -> p d n", p=P)).then_inc(weights_in, 16)

        def stage1_pe(pe):
            def proj(dst, cols, c, t0, n, m0=None):
                k = 0
                for d in range(DH):
                    for wp, xp in ((w1h, xTh), (w1l, xTh), (w1h, xTl)):
                        mm = pe.matmul(dst, wp[:, d, c, cols:cols + P], xp[:, d, t0:t0 + n],
                                       start=(k == 0), stop=(k == 3 * DH - 1))
                        k += 1
                return mm

            pe.wait_ge(a_xh, DH)
            pe.wait_ge(a_xl, DH)
            g = 0
            for c in range(2):
                pe.wait_ge(a_wh, c + 1)
                pe.wait_ge(a_wl, c + 1)
                for th in range(2):
                    for q in range(4):
                        if g >= 4:
                            pe.wait_ge(a_qkc, g - 3)
                        proj(bank[g % 4][:, :], q * P, c, th * HALF, HALF).then_inc(a_qk, 1)
                        g += 1
            pe.wait_ge(a_wh, 3)
            pe.wait_ge(a_wl, 3)
            pe.wait_ge(a_qkc, 16)
            for b in range(B):
                if b >= 2:
                    pe.wait_ge(a_vl, b - 1)
                k = 0
                for d in range(DH):
                    for wp, xp in ((w1h, xTh), (w1l, xTh), (w1h, xTl)):
                        mm = pe.matmul(bank[b % 2][:, :], xp[:, d, b * P:(b + 1) * P], wp[:, d, 2, :],
                                       start=(k == 0), stop=(k == 3 * DH - 1))
                        k += 1
                mm.then_inc(a_vu, 1)

            pe.wait_ge(a_qks, 16)
            pe.wait_ge(a_vl, B)

            def weigh(j):
                th, h = j // H, j % H
                pe.wait_ge(a_ph, j + 1)
                pe.wait_ge(a_pl, j + 1)
                for i in range(4):
                    b = 4 * th + i
                    for k, (pp, vp) in enumerate(((ph, vh), (ph, vl), (pl, vh))):
                        mm = pe.matmul(bank[4 + b // 2][:, (b % 2) * D + h * HD:(b % 2) * D + (h + 1) * HD],
                                       pp[:, j % 3, i, :], vp[:, b, h * HD:(h + 1) * HD], start=(k == 0), stop=(k == 2))
                mm.then_inc(a_pv, 1)

            for j in range(2 * H):
                th, h = j // H, j % H
                q, a = h // 4, 32 * (h % 4)
                if j >= 3:
                    pe.wait_ge(a_pr, j - 2)
                for i in range(4):
                    t0 = th * HALF + i * P
                    for k, qp in enumerate((qh, ql)):
                        mm = pe.matmul(bank[j % 3][:, i * P:(i + 1) * P], kk[a:a + 2 * HD, q, t0:t0 + P],
                                       qp[a:a + 2 * HD, q, t0:t0 + P], start=(k == 0), stop=(k == 1))
                mm.then_inc(a_sc, 1)
                if j >= 2:
                    weigh(j - 2)
            weigh(2 * H - 2)
            weigh(2 * H - 1)

            pe.wait_ge(s_ident, 16)
            pe.wait_ge(weights_high, 1)
            pe.wait_ge(weights_low, 1)

            def turn(b):
                pe.wait_ge(a_g, b + 1)
                if b >= 2:
                    pe.wait_ge(a_gl, b - 1)
                for d in range(DH):
                    mm = pe.transpose(bank[b % 2][:, d * P:(d + 1) * P], gated[:, b % 4, d * P:(d + 1) * P], ident[:, :])
                mm.then_inc(a_gt, 1)

            def back(b):
                pe.wait_ge(a_gl, b + 1)
                if b >= 2:
                    pe.wait_ge(done.sum, n1.sum + b - 1)
                k = 0
                for d in range(DH):
                    for wp, xp in ((woh, gTh), (wol, gTh), (woh, gTl)):
                        mm = pe.matmul(bank[2 + b % 2][:, 0:D], xp[:, b % 2, d, :], wp[:, d, :],
                                       start=(k == 0), stop=(k == 3 * DH - 1))
                        k += 1
                mm.then_inc(a_y, 1)

            for b in range(B + 1):
                if b < B:
                    turn(b)
                if b >= 1:
                    back(b - 1)
            for p in range(4):
                norm_transpose(pe, n1, p)

        def stage1_act(act):
            act.wait_ge(a_x, 16)
            for d in range(DH):
                act.activation(xTh[:, d, :], xT0[:, d, :], ACT.Copy).then_inc(a_xh, 1)
            for c in range(3):
                act.wait_ge(a_w[c], 16)
                act.activation(w1h[:, :, c, :], w1f[:, :, c, :], ACT.Copy, scale=WS).then_inc(a_wh, 1)
            for g in range(16):
                c, th, q = g // 8, g // 4 % 2, g % 4
                act.wait_ge(a_qk, g + 1)
                if g >= 4:
                    act.wait_ge(a_qks, g - 3)
                if c == 0:
                    act.activation(qh[:, q, th * HALF:(th + 1) * HALF], bank[g % 4][:, :], ACT.Silu, scale=1.0 / WS)
                act.activation(fresh[:, g % 4, :], bank[g % 4][:, :], ACT.Silu, scale=1.0 / WS).then_inc(a_qkc, 1)
            for b in range(B):
                act.wait_ge(a_vu, b + 1)
                act.activation(uu[:, b, :], bank[b % 2][:, D:2 * D], ACT.Copy, scale=1.0 / WS)
                act.activation(vh[:, b, :], bank[b % 2][:, 0:D], ACT.Copy, scale=1.0 / WS).then_inc(a_vh, 1)
            act.wait_ge(weights_in, 16)
            act.activation(woh[:, :, :], wof[:, :, :], ACT.Copy, scale=WS).then_inc(weights_high, 1)
            act.wait_ge(a_ns, 1)
            for h in range(H):
                act.activation(decay[:, h, :], diff[:, :], ACT.Exp, scale=nslope[:, h:h + 1]).then_inc(a_dec, 1)
            for j in range(2 * H):
                act.wait_ge(a_pr, j + 1)
                if j >= 3:
                    act.wait_ge(a_pv, j - 2)
                act.activation(ph[:, j % 3, :, :], prob[:, j % 3, :, :], ACT.Copy).then_inc(a_ph, 1)
            for b in range(B):
                act.wait_ge(a_pv, H * (b // 4 + 1))
                if b:
                    act.wait_ge(a_sq, b)
                act.activation(junk[:, :], bank[4 + b // 2][:, (b % 2) * D:(b % 2 + 1) * D], ACT.Square,
                               accum_out=ssq[:, b:b + 1]).then_inc(a_sq, 1)
            for b in range(B):
                act.wait_ge(a_gt, b + 1)
                if b >= 2:
                    act.wait_ge(a_y, b - 1)
                act.activation(gTh[:, b % 2, :, :], bank[b % 2][:, 0:D].rearrange("q (d t) -> q d t", d=DH),
                               ACT.Copy).then_inc(a_gh, 1)

        def stage1_dve(dve, chain):
            dve.wait_ge(a_x, 16)
            for d in range(DH):
                dve.wait_ge(a_xh, d + 1)
                dve.tensor_tensor(xTl[:, d, :], xT0[:, d, :], xTh[:, d, :], ALU.subtract).then_inc(a_xl, 1)
            for c in range(3):
                dve.wait_ge(a_wh, c + 1)
                dve.scalar_tensor_tensor(out=w1l[:, :, c, :], in0=w1f[:, :, c, :], scalar=WS, in1=w1h[:, :, c, :],
                                         op0=ALU.mult, op1=ALU.subtract).then_inc(a_wl, 1)
            dve.wait_ge(a_c, 48)
            dve.tensor_scalar(nslope[:, :], slope[:, :], -1.0, None, ALU.mult).then_inc(a_ns, 1)
            dve.wait_ge(s_x, 32)
            for g in range(16):
                c, th, q = g // 8, g // 4 % 2, g % 4
                at = slice(th * HALF, (th + 1) * HALF)
                dve.wait_ge(a_qkc, g + 1)
                if c == 0:
                    dve.tensor_tensor(ql[:, q, at], fresh[:, g % 4, :], qh[:, q, at], ALU.subtract).then_inc(a_qks, 1)
                else:
                    if g >= 10:
                        dve.wait_ge(a_qks, g - 1)
                    dve.tensor_copy(fresh_h[:, g % 2, :], fresh[:, g % 4, :]).then_inc(a_kh, 1)
                    dve.wait_ge(a_kh, g - 7)
                    dve.scalar_tensor_tensor(out=kk[:, q, at], in0=fresh_h[:, g % 2, :], scalar=lows[:, 0:1],
                                             in1=fresh[:, g % 4, :], op0=ALU.mult, op1=ALU.add).then_inc(a_qks, 1)
            for b in range(B):
                dve.wait_ge(a_vh, b + 1)
                dve.scalar_tensor_tensor(out=vl[:, b, :], in0=bank[b % 2][:, 0:D], scalar=1.0 / WS, in1=vh[:, b, :],
                                         op0=ALU.mult, op1=ALU.subtract).then_inc(a_vl, 1)
            dve.wait_ge(weights_high, 1)
            dve.scalar_tensor_tensor(out=wol[:, :, :], in0=wof[:, :, :], scalar=WS, in1=woh[:, :, :],
                                     op0=ALU.mult, op1=ALU.subtract).then_inc(weights_low, 1)
            conv_filters_dve(dve)
            dve.wait_ge(a_dec, H)
            dve.tensor_tensor(decay[:, :, :], decay[:, :, :], causal[:, None, :].broadcast_to([P, H, P]),
                              ALU.mult).then_inc(a_decm, 1)
            dve.wait_ge(a_decm, 1)
            for j in range(2 * H + 1):
                if j < 2 * H:
                    dve.wait_ge(a_sc, j + 1)
                    if j >= 3:
                        dve.wait_ge(a_ph, j - 2)
                        dve.wait_ge(a_pl, j - 2)
                    dve.tensor_tensor(prob[:, j % 3, :, :], bank[j % 3][:, :].rearrange("q (i t) -> q i t", i=4),
                                      decay[:, j % H, None, :].broadcast_to([P, 4, P]), ALU.mult).then_inc(a_pr, 1)
                if j >= 1:
                    dve.wait_ge(a_ph, j)
                    if j >= 4:
                        dve.wait_ge(a_pv, j - 3)
                    dve.tensor_tensor(pl[:, (j - 1) % 3, :, :], prob[:, (j - 1) % 3, :, :], ph[:, (j - 1) % 3, :, :],
                                      ALU.subtract).then_inc(a_pl, 1)

            def gate(b):
                dve.wait_ge(a_rms, b // 4 + 1)
                if b >= 4:
                    dve.wait_ge(a_gt, b - 3)
                dve.scalar_tensor_tensor(out=gated[:, b % 4, :], in0=bank[4 + b // 2][:, (b % 2) * D:(b % 2 + 1) * D],
                                         scalar=rms[:, b:b + 1], in1=uu[:, b, :],
                                         op0=ALU.mult, op1=ALU.mult).then_inc(a_g, 1)

            def low(b):
                dve.wait_ge(a_gh, b + 1)
                if b >= 2:
                    dve.wait_ge(a_y, b - 1)
                dve.tensor_tensor(gTl[:, b % 2, :, :], bank[b % 2][:, 0:D].rearrange("q (d t) -> q d t", d=DH),
                                  gTh[:, b % 2, :, :], ALU.subtract).then_inc(a_gl, 1)

            for b in range(B + 3):
                if b < B:
                    gate(b)
                if 1 <= b < B + 1:
                    low(b - 1)
                if 2 <= b < B + 2:
                    dve.wait_ge(a_y, b - 1)
                    norm_sum(dve, chain, n1, b - 2, bank[2 + b % 2][:, 0:D], 1.0 / WS)
                if b >= 3:
                    norm_apply(dve, n1, b - 3)

        def stage1_pool(pool, chain):
            pool.memset(minus_half[:, :], -0.5).then_inc(s_mh, 1)
            pool.wait_ge(s_mh, 1)
            pool.wait_ge(b_c, 16)
            for h in range(KVH):
                conv_products_pool(pool, h)
            for th in range(2):
                pool.wait_ge(a_sq, 4 * th + 4)
                v = slice(4 * th, 4 * th + 4)
                chain.link(pool.tensor_scalar(ssq[:, v], ssq[:, v], 1.0 / D, RMS_EPS, ALU.mult, ALU.add))
                pool.tensor_tensor(rms[:, v], ssq[:, v], minus_half[:, 0:4], ALU.pow).then_inc(a_rms, 1)
            for b in range(B):
                norm_rstd(pool, chain, n1, b)
        conv = Region()
        filtering = Region(0, arena2)
        KVH = H // 2
        ctxr = filtering("ctxr", [P, DH, P, B])
        toep = filtering("toep", [P, H, 2 * P])
        dvec = sb("dvec", [P, H])
        anti = sb("anti", [P, P])
        kv = filtering("kv", [P, KVH, DH, CJ * CJ * B])
        qc = conv("qc", [P, DH, P, B])
        pr = conv("pr", [P, 3, DH, CJ, CJ * B])
        pr4 = conv("pr4", [P, 3, DH, CJ // 2, CJ * B])
        pr2 = conv("pr2", [P, 2, DH, CJ // 4, CJ * B])
        convT = conv("convT", [P, DH, B, P])

        b_c = sem("b_c")
        b_k = sem("b_k")
        b_toep = sem("b_toep")
        b_kv = sem("b_kv")
        b_y = sem("b_y")
        b_pr = sem("b_pr")
        b_p4 = sem("b_p4")
        b_o = sem("b_o")
        b_t = sem("b_t")
        n2 = Norm(2, 1, 0)

        def stage2_sp(sp):
            sp.dma_start(ctxr[:, :, :, :], ins["ctx_rev"].rearrange("p (d s b) -> p d s b", d=DH, b=B)).then_inc(b_c, 16)
            filters = bass.AP(ins["filters"].tensor, 0, [[1, P], [3 * P - 1, H], [1, 2 * P]])
            sp.dma_start(toep[:, :, :], filters).then_inc(b_k, 16)
            sp.dma_start(dvec[:, :], ins["conv_d"].partition_broadcast(P)).then_inc(b_k, 16)
            sp.dma_start(anti[:, :], ins["c_anti"]).then_inc(b_k, 16)

        def conv_products_pool(pool, h):
                for d in range(DH):
                    if h >= KVH:
                        pool.wait_ge(b_y, 2 * (h - KVH) + 2)
                    c = ctxr[:, d, h * CJ:(h + 1) * CJ, :]
                    pool.tensor_tensor(kv[:, h % KVH, d, :].rearrange("p (i j b) -> p i j b", i=CJ, j=CJ),
                                       c[:, :, None, :].broadcast_to([P, CJ, CJ, B]),
                                       c[:, None, :, :].broadcast_to([P, CJ, CJ, B]), ALU.mult).then_inc(b_kv, 1)

        def conv_filters_dve(dve):
            dve.wait_ge(b_k, 48)
            for h in range(H):
                dve.scalar_tensor_tensor(out=toep[:, h, 0:P], in0=anti[:, :], scalar=dvec[:, h:h + 1],
                                         in1=toep[:, h, 0:P], op0=ALU.mult, op1=ALU.add).then_inc(b_toep, 1)

        def stage2_pe(pe):
            pe.wait_ge(b_toep, H)
            for h in range(H):
                pe.wait_ge(b_kv, 2 * h + 2)
                for d in range(DH):
                    u = 2 * h + d
                    if u >= 4:
                        pe.wait_ge(b_pr, u - 3)
                    if d:
                        pe.matmul(bank[u % 4][:, :], toep[:, h, P:2 * P], kv[:, h % KVH, 0, :], start=True, stop=False)
                    pe.matmul(bank[u % 4][:, :], toep[:, h, 0:P], kv[:, h % KVH, d, :], start=not d, stop=True).then_inc(b_y, 1)
            pe.wait_ge(b_o, H)
            for b in range(B):
                if b >= 2:
                    pe.wait_ge(done.sum, n2.sum + b - 1)
                for d in range(DH):
                    mm = pe.transpose(bank[4 + b % 2][:, d * P:(d + 1) * P], convT[:, d, b, :], ident[:, :])
                mm.then_inc(b_t, 1)
            for p in range(4):
                norm_transpose(pe, n2, p)

        def stage2_act(act):
            for p in range(4):
                act.wait_ge(done.t, n1.t + p + 1)
                act.activation(qc[:, :, :, 2 * p:2 * p + 2].rearrange("q d t b -> q d b t"),
                               bank[6 + p % 2][:, :].rearrange("q (d b t) -> q d b t", d=DH, b=2),
                               ACT.Copy).then_inc(done.lo, 1)
            for p in range(4):
                norm_hi(act, n2, p)

        def stage2_dve(dve, chain):
            dve.wait_ge(done.lo, n1.lo + 4)

            def fold(h):
                dve.wait_ge(b_p4, h + 1)
                chain.link(dve.tensor_tensor(pr2[:, h % 2, :, :, :], pr4[:, h % 3, :, 0:2, :], pr4[:, h % 3, :, 2:4, :], ALU.add))
                dve.tensor_tensor(convT[:, :, :, h * CJ:(h + 1) * CJ].rearrange("p d b j -> p d j b"),
                                  pr2[:, h % 2, :, 0, :].rearrange("p d (j b) -> p d j b", b=B),
                                  pr2[:, h % 2, :, 1, :].rearrange("p d (j b) -> p d j b", b=B), ALU.add).then_inc(b_o, 1)

            for h in range(H + 2):
                if h < H:
                    if h >= 3:
                        dve.wait_ge(b_p4, h - 2)
                    for d in range(DH):
                        u = 2 * h + d
                        dve.wait_ge(b_y, u + 1)
                        dve.tensor_tensor(pr[:, h % 3, d, :, :].rearrange("p i (j b) -> p i j b", b=B),
                                          bank[u % 4][:, :].rearrange("p (i j b) -> p i j b", i=CJ, j=CJ),
                                          qc[:, d, h * CJ:(h + 1) * CJ, None, :].broadcast_to([P, CJ, CJ, B]),
                                          ALU.mult).then_inc(b_pr, 1)
                if h >= 2:
                    fold(h - 2)
            for b in range(B + 1):
                if b < B:
                    dve.wait_ge(b_t, b + 1)
                    norm_sum(dve, chain, n2, b, bank[4 + b % 2][:, 0:D], 1.0)
                if b >= 1:
                    norm_apply(dve, n2, b - 1)
            for p in range(4):
                norm_lo(dve, n2, p)

        def stage2_pool(pool, chain):
            for h in range(H):
                pool.wait_ge(b_pr, 2 * h + 2)
                if h >= 3:
                    pool.wait_ge(b_o, h - 2)
                pool.tensor_tensor(pr4[:, h % 3, :, :, :], pr[:, h % 3, :, 0:4, :], pr[:, h % 3, :, 4:8, :],
                                   ALU.add).then_inc(b_p4, 1)
                if h < H - KVH:
                    conv_products_pool(pool, h + KVH)
            for b in range(B):
                norm_rstd(pool, chain, n2, b)

        acc = sb("acc", [P, B, D])
        identh = sb("identh", [P, P], F16)
        before = sb("before", [P, P], F16)
        onesh = sb("onesh", [P, P], F16)
        before_f = sb("before_f", [P, P])
        iota = sb("iota", [P, IOTA])
        iotah = sb("iotah", [P, IOTA], F16)
        tokens = sb("tokens", [P, B])
        kth = sb("kth", [P, 8])
        s_plain = sem("s_plain")
        s_c3 = sem("s_c3")
        s_idh = sem("s_idh")

        rows = nc.dram_tensor("token_rows", [T, 2 * D], F16).ap()

        routing_counts = {"gate": 16, "gh": 1, "gl": 1, "logit": B, "lread": B, "soft": 1, "scaled": 1, "mask": 1, "rank": 2,
                          "named": 2, "rounds": 1, "rowsh": B, "rowsl": B, "rows": 16 * B}
        routing = {edge: sem("route_" + edge) for edge in routing_counts if edge != "rows"}
        rows_out_sem = sem("rows_out")

        class Experts:

            def __init__(self, name, region, experts, top, width, gated, lot, tiles, w_gate, w_up, w_down, earlier):
                self.name, self.E, self.K, self.gated = name, experts, top, gated
                self.lot, self.nt = lot, tiles
                self.C = lot * tiles
                self.im = width
                self.nk = 1 if gated else 2
                self.NI = experts // 8
                self.max_rounds = -(-T // self.C)
                self.w_gate, self.w_up, self.w_down = w_gate, w_up, w_down
                E, K, C, im, nk = self.E, self.K, self.C, self.im, self.nk
                self.gate_f = region(name + "_gate_f", [P, DH, E])
                self.gate_h = region(name + "_gate_h", [P, DH, E], F16)
                self.gate_l = region(name + "_gate_l", [P, DH, E], F16)
                self.top = region(name + "_top", [P, B, 8])
                self.pick = region(name + "_pick", [P, B, 8], U32)
                self.pickf = region(name + "_pickf", [P, B, 8])
                self.weight = region(name + "_weight", [P, B, 8])
                self.total = region(name + "_total", [P, B])
                self.active = region(name + "_active", [P, B, 8])
                self.cum = region(name + "_cum", [P, B, 8])
                self.one = Region(PICKS, arena2)(name + "_one", [P, B, K, E], F16)
                self.picked = Region(PICKS + B * K * E // 2, arena2)(name + "_picked", [P, B, K, E], F16)
                self.rank = region(name + "_rank", [P, B, K])
                self.mask = region(name + "_mask", [P, B, E], F16)
                self.named = region(name + "_named", [P, B, K, 2, E], F16)
                self.most = region(name + "_most", [P, 16])
                self.rounds = region(name + "_rounds", [P, 2], I32)
                self.place = region(name + "_place", [P, 4, C], F16)
                self.list = region(name + "_list", [P, tiles, E], I32)
                self.home = region(name + "_home", [P, tiles, E], I32)
                self.homef = region(name + "_homef", [P, tiles, E])
                self.spare = region(name + "_spare", [P, tiles, E])
                self.fetch = region(name + "_fetch", [P, 2, tiles, 4], I32)
                self.send = region(name + "_send", [P, 2, tiles, 4], I32)
                self.xg = region(name + "_xg", [P, 4, tiles, 2 * D], F16)
                self.xgT = region(name + "_xgT", [P, 2, 4, C], F16)
                self.ring_up = region(name + "_ring_up", [P, 2, 4, DH * 2 * im])
                self.ring_dn = region(name + "_ring_dn", [P, 2, 4, nk * D])
                self.up_h = region(name + "_up_h", [P, 4, DH * 2 * im], F16)
                self.up_l = region(name + "_up_l", [P, 4, DH * 2 * im], F16)
                self.dn_h = region(name + "_dn_h", [P, 4, nk * D], F16)
                self.dn_l = region(name + "_dn_l", [P, 4, nk * D], F16)
                self.act = region(name + "_act", [P, 2, (2 if not gated else 1) * C])
                self.hid = region(name + "_hid", [P, 2, C]) if gated else None
                self.hid_h = region(name + "_hid_h", [P, 2, nk * C], F16)
                self.hid_l = region(name + "_hid_l", [P, 2, nk * C], F16)
                self.y = region(name + "_y", [P, 4, tiles, D])
                self.back = Region(BACK, arena2)(name + "_back", [P, 3, K, D])
                self.y_rows = nc.dram_tensor(name + "_y_rows", [K * T + E * tiles * P + 4 * tiles, D], F32).ap()
                edges = ("place placed list fetch send t xc wuh wdh wl u silu hh hl y ye acc").split() + ["hread"] * gated
                self.s = routing | {edge: sem(f"{name}_{edge}") for edge in edges}
                self.before = {edge: count * earlier for edge, count in routing_counts.items()}
                if not gated:
                    self.s["hread"] = self.s["silu"]
                self.s_rows = rows_out_sem
                self.s_ring = [sem(f"{name}_ring{i}") for i in range(2)]
                self.s_xg = [sem(f"{name}_xg{i}") for i in range(4)]
                self.s_yw = [sem(f"{name}_yw{i}") for i in range(4)]
                self.s_back = [sem(f"{name}_back{i}") for i in range(3)]

        def load_group(sp, m, group, slot):
            sp.dma_start(m.ring_up[:, slot, :, :], m.w_up[bass.ds(group, 1), :, :, :].rearrange("g p e n -> p (g e) n")
                         ).then_inc(m.s_ring[slot], 16)
            sp.dma_start(m.ring_dn[0:m.im, slot, :, :], m.w_down[bass.ds(group, 1), :, :, :].rearrange("g p e n -> p (g e) n")
                         ).then_inc(m.s_ring[slot], 16)

        def route_sp(sp, m, n):
            sp.dma_start(m.gate_f[:, :, :], m.w_gate.rearrange("(d p) e -> p d e", p=P)).then_inc(m.s["gate"], 16)
            for g in range(2):
                load_group(sp, m, g, g)

        def rows_sp(sp, m):
            for b in range(B):
                sp.wait_ge(m.s["rowsl"], m.before["rowsl"] + b + 1)
                sp.dma_start(rows[b * P:(b + 1) * P, :], row_parts[:, b, :]).then_inc(m.s_rows, 16)

        def rows_act(act, m, n, b):
            act.wait_ge(done.x, n.x + b + 1)
            act.activation(row_parts[:, b, 0:D], X[:, b, :], ACT.Copy).then_inc(m.s["rowsh"], 1)

        def rows_pool(pool, m, b):
            pool.wait_ge(m.s["rowsh"], m.before["rowsh"] + b + 1)
            pool.tensor_tensor(row_parts[:, b, D:2 * D], X[:, b, :], row_parts[:, b, 0:D],
                               ALU.subtract).then_inc(m.s["rowsl"], 1)

        def gate_act(act, m):
            act.wait_ge(m.s["gate"], m.before["gate"] + 16)
            act.activation(m.gate_h[:, :, :], m.gate_f[:, :, :], ACT.Copy, scale=WS).then_inc(m.s["gh"], 1)

        def gate_dve(dve, m):
            dve.wait_ge(m.s["gh"], m.before["gh"] + 1)
            dve.scalar_tensor_tensor(out=m.gate_l[:, :, :], in0=m.gate_f[:, :, :], scalar=WS, in1=m.gate_h[:, :, :],
                                     op0=ALU.mult, op1=ALU.subtract).then_inc(m.s["gl"], 1)

        def logits_pe(pe, m, n, b):
            pe.wait_ge(done.lo, n.lo + b // 2 + 1)
            if b >= 2:
                pe.wait_ge(m.s["lread"], m.before["lread"] + b - 1)
            k = 0
            for d in range(DH):
                for wp, xp in ((m.gate_h, xTh), (m.gate_l, xTh), (m.gate_h, xTl)):
                    mm = pe.matmul(bank[b % 2][:, 0:m.E], xp[:, d, b * P:(b + 1) * P], wp[:, d, :],
                                   start=(k == 0), stop=(k == 3 * DH - 1))
                    k += 1
            mm.then_inc(m.s["logit"], 1)

        def pick_dve(dve, chain, m, b):
            dve.wait_ge(m.s["logit"], m.before["logit"] + b + 1)
            chain.link(dve.max(m.top[:, b, :], bank[b % 2][:, 0:m.E]))
            dve.max_index(m.pick[:, b, :], m.top[:, b, :], bank[b % 2][:, 0:m.E]).then_inc(m.s["lread"], 1)

        def soft_act(act, m):
            act.wait_ge(m.s["scaled"], m.before["scaled"] + 1)
            act.activation(m.weight[:, :, :], m.weight[:, :, :], ACT.Exp, scale=1.0 / WS).then_inc(m.s["soft"], 1)

        def weigh_dve(dve, chain, m, threshold):
            w = m.weight[:, :, 0:m.K]

            def normalise():
                chain.link(dve.tensor_reduce(m.total[:, :], w, AX.X, ALU.add))
                chain.link(dve.reciprocal(m.total[:, :], m.total[:, :]))
                chain.link(dve.tensor_tensor(w, w, m.total[:, :, None].broadcast_to([P, B, m.K]), ALU.mult))

            dve.wait_ge(m.s["lread"], m.before["lread"] + B)
            dve.tensor_tensor(m.weight[:, :, :], m.top[:, :, :], m.top[:, :, 0:1].broadcast_to([P, B, 8]),
                              ALU.subtract).then_inc(m.s["scaled"], 1)
            chain.link(dve.tensor_copy(m.pickf[:, :, :], m.pick[:, :, :]))
            chain.link(dve.tensor_scalar(m.pickf[:, :, :], m.pickf[:, :, :], 1.0, None, ALU.add))
            if threshold is not None:
                chain.link(dve.memset(m.active[:, :, :], 1.0))
                chain.link(dve.memset(m.active[:, :, 0:1], 0.0))
            dve.wait_ge(m.s["soft"], m.before["soft"] + 1)
            normalise()
            if threshold is not None:
                flat = [v[:, :, :].rearrange("p b k -> p (b k)") for v in (m.cum, m.active, m.weight)]
                chain.link(dve.tensor_tensor_scan(flat[0], flat[1], flat[2], 0.0, ALU.mult, ALU.add))
                chain.link(dve.tensor_scalar(m.active[:, :, 1:8], m.cum[:, :, 0:7], threshold, None, ALU.is_lt))
                chain.link(dve.memset(m.active[:, :, 0:1], 1.0))
                chain.link(dve.tensor_tensor(m.pickf[:, :, :], m.pickf[:, :, :], m.active[:, :, :], ALU.mult))
                chain.link(dve.tensor_tensor(w, w, m.active[:, :, :], ALU.mult))
            chain.link(dve.tensor_tensor(m.one[:, :, :, :], m.pickf[:, :, 0:m.K, None].broadcast_to([P, B, m.K, m.E]),
                                         iota[:, None, None, 1:m.E + 1].broadcast_to([P, B, m.K, m.E]), ALU.is_equal))
            with nc.allow_low_precision(reason="a pick is 0 or 1"):
                dve.tensor_reduce(m.mask[:, :, :], m.one[:, :, :, :].rearrange("p b k e -> p b e k"), AX.X, ALU.add
                                  ).then_inc(m.s["mask"], 1)
            if threshold is not None:
                normalise()

        def name_pool(pool, m):
            pool.wait_ge(m.s["mask"], m.before["mask"] + 1)
            pool.tensor_tensor(m.named[:, :, :, 0, :], m.one[:, :, :, :], tokens[:, :, None, None].broadcast_to([P, B, m.K, m.E]),
                               ALU.mult).then_inc(m.s["named"], 1)
            pool.tensor_tensor(m.named[:, :, :, 1, :], m.one[:, :, :, :], kth[:, None, 0:m.K, None].broadcast_to([P, B, m.K, m.E]),
                               ALU.mult).then_inc(m.s["named"], 1)

        def rank_pe(pe, m):
            pe.wait_ge(m.s["mask"], m.before["mask"] + 1)
            for b in range(B):
                for i in range(b + 1):
                    mm = pe.matmul(bank[2][:, b * m.E:(b + 1) * m.E], (before if i == b else onesh)[:, :], m.mask[:, i, :],
                                   start=(i == 0), stop=(i == b))
            mm.then_inc(m.s["rank"], 1)
            for i in range(B):
                mm = pe.matmul(bank[3][:, 0:m.E], onesh[:, :], m.mask[:, i, :], start=(i == 0), stop=(i == B - 1))
            mm.then_inc(m.s["rank"], 1)

        def rank_dve(dve, chain, m, threshold):
            dve.wait_ge(m.s["rank"], m.before["rank"] + 1)
            chain.link(dve.tensor_tensor(m.picked[:, :, :, :], m.one[:, :, :, :],
                                         bank[2][:, 0:B * m.E].rearrange("p (b o e) -> p b o e", b=B, o=1).broadcast_to([P, B, m.K, m.E]),
                                         ALU.mult))
            chain.link(dve.tensor_reduce(m.rank[:, :, :], m.picked[:, :, :, :], AX.X, ALU.add))
            if threshold is not None:
                chain.link(dve.tensor_scalar(m.cum[:, :, :], m.active[:, :, :], -4.0 * T, 4.0 * T, ALU.mult, ALU.add))
                chain.link(dve.tensor_tensor(m.rank[:, :, :], m.rank[:, :, :], m.cum[:, :, :], ALU.add))

        def rounds_dve(dve, chain, m):
            dve.wait_ge(m.s["rank"], m.before["rank"] + 2)
            n = m.max_rounds - 1
            chain.link(dve.tensor_reduce(m.most[:, 0:1], bank[3][:, 0:m.E], AX.X, ALU.max))
            chain.link(dve.tensor_scalar(m.most[:, 1:1 + n], iota[:, 1:1 + n], float(m.C), None, ALU.mult))
            chain.link(dve.tensor_scalar(m.most[:, 1:1 + n], m.most[:, 1:1 + n], m.most[:, 0:1], None, ALU.is_lt))
            chain.link(dve.tensor_reduce(m.most[:, 9:10], m.most[:, 1:1 + n], AX.X, ALU.add))
            dve.tensor_scalar(m.rounds[:, 0:1], m.most[:, 9:10], 1.0, None, ALU.add).then_inc(m.s["rounds"], 1)

        def spare_dve(dve, chain, m):
            for i in range(m.nt):
                chain.link(dve.tensor_scalar(m.spare[:, i, :], iota[:, 0:m.E], float(m.nt * P), float(m.K * T + i * P),
                                             ALU.mult, ALU.add))
                chain.link(dve.tensor_scalar(m.spare[:, i, :], m.spare[:, i, :], tokens[:, 0:1], None, ALU.add))

        def read_rounds(engine, m):
            engine.wait_ge(m.s["rounds"], m.before["rounds"] + 1)
            return engine.value_load(m.rounds[0:1, 0:1], min_val=1, max_val=m.max_rounds)

        def lists_dve(dve, m, r):
            ranks = m.rank.rearrange("p b k -> p (b k)")
            with dve.Fori(0, B * m.K // 8) as g:
                for i in range(8):
                    dve.wait_ge(m.s["placed"], r * (B * m.K) + g * 8 + (i + 1))
                    dve.tensor_scalar(m.place[:, i % 4, :], iotah[:, 0:m.C], ranks[:, bass.ds(g * 8 + i, 1)], None,
                                      ALU.is_equal).then_inc(m.s["place"], 1)
            dve.wait_ge(m.s["placed"], r * (B * m.K) + (B * m.K + 4))
            dve.wait_ge(m.s["send"], r * (2 * m.NI) + 1)
            step = [0]

            def then(ins):
                step[0] += 1
                ins.then_inc(m.s["list"], 1)
                dve.wait_ge(m.s["list"], r * (2 * m.nt + 1) + step[0])

            for i in range(m.nt):
                token, pick = bank[6 + i][0:m.lot, 0:m.E], bank[6 + i][0:m.lot, m.E:2 * m.E]
                home = m.homef[0:m.lot, i, :]
                dve.tensor_scalar(m.list[0:m.lot, i, :], token, -1.0, 0.0, ALU.add, ALU.max)
                then(dve.scalar_tensor_tensor(out=home, in0=token, scalar=0.0, in1=m.spare[0:m.lot, i, :],
                                              op0=ALU.is_equal, op1=ALU.mult))
                then(dve.tensor_tensor(home, home, pick, ALU.add))
                dve.scalar_tensor_tensor(out=m.home[0:m.lot, i, :], in0=token, scalar=-1.0, in1=home,
                                         op0=ALU.add, op1=ALU.add)
            then(dve.tensor_scalar(ranks, ranks, -float(m.C), None, ALU.add))

        def lists_pe(pe, m, r):
            pe.wait_ge(m.s["named"], m.before["named"] + 2)
            for q in range(B * m.K):
                b, k = q // m.K, q % m.K
                pe.wait_ge(m.s["place"], r * (B * m.K) + q + 1)
                for i in range(m.nt):
                    mm = pe.matmul(bank[6 + i][0:m.lot, 0:2 * m.E], m.place[:, q % 4, i * m.lot:(i + 1) * m.lot], m.named[:, b, k, :, :],
                                   start=(q == 0), stop=(q == B * m.K - 1))
                    if i == m.nt - 1:
                        mm.then_inc(m.s["placed"], 1)

        def experts_loop(engine, m, r, step):
            with engine.Fori(0, m.NI - 1) as it:
                for j in range(8):
                    step(r * m.E + it * 8, it, r * m.NI + it, j, True)
            for j in range(8):
                step(r * m.E + (m.NI - 1) * 8, m.NI - 1, r * m.NI + (m.NI - 1), j, False)

        def ring_turn(turn, x):
            return 32 * turn + 32 * (x // 8 + 1)

        def plain(pool):
            pool.sem_inc(s_plain, 1)

        def round_pool(pool, m, r):
            AHEAD = 6
            pool.wait_ge(m.s["list"], r * (2 * m.nt + 1) + (2 * m.nt + 1))
            plain(pool)

            def columns(dst, src, edge, turn, it, x):
                pool.tensor_copy(dst[0:m.lot, x // 4 % 2, :, :], src[0:m.lot, :, bass.ds(it * 8 + x, 4)]).then_inc(m.s[edge], 1)
                pool.wait_ge(m.s[edge], turn * 2 + (x // 4 + 2))
                plain(pool)

            def fetch(n, it, turn, x):
                pool.wait_ge(m.s["t"], n + (x + 1))
                plain(pool)
                if x % 4 == 0:
                    columns(m.fetch, m.list, "fetch", turn, it, x)
                for i in range(m.nt):
                    pool.indirect_dma_start(out=m.xg[0:m.lot, x % 4, i, :], out_offset=None, in_=rows,
                                            in_offset=bass.IndirectOffsetOnAxis(
                                                ap=m.fetch[0:m.lot, x // 4 % 2, i, x % 4:x % 4 + 1], axis=0)
                                            ).then_inc(m.s_xg[x % 4], 16)

            def send(n, it, turn, x):
                pool.wait_ge(m.s["ye"], n + (x + 5))
                plain(pool)
                if x % 4 == 0:
                    columns(m.send, m.home, "send", turn, it, x)
                for i in range(m.nt):
                    pool.indirect_dma_start(out=m.y_rows, out_offset=bass.IndirectOffsetOnAxis(
                        ap=m.send[0:m.lot, x // 4 % 2, i, x % 4:x % 4 + 1], axis=0),
                        in_=m.y[0:m.lot, x % 4, i, :], in_offset=None).then_inc(m.s_yw[x % 4], 16)

            def step(n, it, turn, j, more):
                if more or j + AHEAD < 8:
                    fetch(n, it, turn, j + AHEAD)
                send(n, it, turn, j)

            for x in range(AHEAD):
                fetch(r * m.E, 0, r * m.NI, x)
            experts_loop(pool, m, r, step)

        def round_pe(pe, m, r):
            def turn_tiles(n, turn, x):
                pe.wait_ge(m.s_xg[x % 4], 16 * 2 * m.nt * turn + 16 * m.nt * (x // 4 + 1))
                pe.wait_ge(m.s["xc"], n + (x + 1))
                v = bank[x % 2][:, :].bitcast(F16)
                for c in range(4):
                    for i in range(m.nt):
                        at = c * m.C + i * m.lot
                        mm = pe.transpose(v[:, at:at + m.lot], m.xg[0:m.lot, x % 4, i, c * P:(c + 1) * P],
                                          identh[0:m.lot, 0:m.lot])
                mm.then_inc(m.s["t"], 1)

            def up(n, x):
                pe.wait_ge(m.s["xc"], n + (x + 3))
                pe.wait_ge(m.s["wl"], n + (x + 1))
                pe.wait_ge(m.s["hread"], n + (x + 1))
                for i in range(2):
                    k = 0
                    for d in range(DH):
                        c0 = d * 2 * m.im + i * m.im
                        for wp, xp in ((m.up_h, d), (m.up_l, d), (m.up_h, 2 + d)):
                            mm = pe.matmul(bank[2 + x % 2][0:m.im, i * m.C:(i + 1) * m.C], wp[:, x % 4, c0:c0 + m.im],
                                           m.xgT[:, x % 2, xp, :], start=(k == 0), stop=(k == 3 * DH - 1))
                            k += 1
                mm.then_inc(m.s["u"], 1)

            def down(n, x):
                pe.wait_ge(m.s["hl"], n + (x + 3))
                pe.wait_ge(m.s["ye"], n + (x + 3))
                for i in range(m.nt):
                    k = 0
                    for t in range(m.nk):
                        c0 = t * m.C + i * m.lot
                        for wp, hp in ((m.dn_h, m.hid_h), (m.dn_l, m.hid_h), (m.dn_h, m.hid_l)):
                            mm = pe.matmul(bank[4 + x % 2][0:m.lot, i * D:(i + 1) * D], hp[0:m.im, x % 2, c0:c0 + m.lot],
                                           wp[0:m.im, x % 4, t * D:(t + 1) * D], start=(k == 0), stop=(k == 3 * m.nk - 1))
                            k += 1
                mm.then_inc(m.s["y"], 1)

            def step(n, it, turn, j, more):
                if more or j + 3 < 8:
                    turn_tiles(n, turn, j + 3)
                if more or j + 2 < 8:
                    up(n, j + 2)
                down(n, j)

            for x in range(3):
                turn_tiles(r * m.E, r * m.NI, x)
            for x in range(2):
                up(r * m.E, x)
            experts_loop(pe, m, r, step)

        def round_act(act, m, r):
            def weights_high(n, turn, x):
                act.wait_ge(m.s_ring[x // 4 % 2], ring_turn(turn, x))
                act.wait_ge(m.s["u"], n + (x + 1))
                act.activation(m.up_h[:, x % 4, :], m.ring_up[:, x // 4 % 2, x % 4, :], ACT.Copy, scale=WS
                               ).then_inc(m.s["wuh"], 1)
                act.wait_ge(m.s["y"], n + (x + 1))
                act.activation(m.dn_h[0:m.im, x % 4, :], m.ring_dn[0:m.im, x // 4 % 2, x % 4, :], ACT.Copy, scale=WS
                               ).then_inc(m.s["wdh"], 1)

            def copy_tiles(n, x):
                act.wait_ge(m.s["u"], n + (x + 3))
                act.wait_ge(m.s["t"], n + (x + 5))
                v = bank[x % 2][:, :].bitcast(F16)[:, 0:4 * m.C]
                act.activation(m.xgT[:, x % 2, :, :].rearrange("p c t -> p (c t)"), v, ACT.Copy).then_inc(m.s["xc"], 1)

            def silu(n, x):
                act.wait_ge(m.s["u"], n + (x + 5))
                act.wait_ge(m.s["hl"], n + (x + 1))
                w = (1 if m.gated else 2) * m.C
                act.activation(m.act[0:m.im, x % 2, :], bank[2 + x % 2][0:m.im, 0:w], ACT.Silu, scale=1.0 / WS
                               ).then_inc(m.s["silu"], 1)

            def step(n, it, turn, j, more):
                if more or j + 1 < 8:
                    silu(n, j + 1)
                if more or j + 3 < 8:
                    weights_high(n, turn, j + 3)
                    copy_tiles(n, j + 3)

            for x in range(3):
                weights_high(r * m.E, r * m.NI, x)
                if x < 2:
                    copy_tiles(r * m.E, x)
            silu(r * m.E, 0)
            copy_tiles(r * m.E, 2)
            experts_loop(act, m, r, step)

        def round_dve(dve, m, r):
            def weights_low(n, x):
                dve.wait_ge(m.s["wuh"], n + (x + 1))
                dve.scalar_tensor_tensor(out=m.up_l[:, x % 4, :], in0=m.ring_up[:, x // 4 % 2, x % 4, :], scalar=WS,
                                         in1=m.up_h[:, x % 4, :], op0=ALU.mult, op1=ALU.subtract)
                dve.wait_ge(m.s["wdh"], n + (x + 1))
                dve.scalar_tensor_tensor(out=m.dn_l[0:m.im, x % 4, :], in0=m.ring_dn[0:m.im, x // 4 % 2, x % 4, :], scalar=WS,
                                         in1=m.dn_h[0:m.im, x % 4, :], op0=ALU.mult, op1=ALU.subtract).then_inc(m.s["wl"], 1)

            def hidden(n, x):
                dve.wait_ge(m.s["silu"], n + (x + 3))
                dve.wait_ge(m.s["y"], n + (x + 3))
                if m.gated:
                    dve.scalar_tensor_tensor(out=m.hid[0:m.im, x % 2, :], in0=bank[2 + x % 2][0:m.im, m.C:2 * m.C], scalar=1.0 / WS,
                                             in1=m.act[0:m.im, x % 2, :], op0=ALU.mult, op1=ALU.mult).then_inc(m.s["hread"], 1)
                    dve.wait_ge(m.s["hread"], n + (x + 3))
                    h = m.hid
                else:
                    h = m.act
                dve.tensor_copy(m.hid_h[0:m.im, x % 2, :], h[0:m.im, x % 2, :]).then_inc(m.s["hh"], 1)
                dve.wait_ge(m.s["hh"], n + (x + 1))
                dve.tensor_tensor(m.hid_l[0:m.im, x % 2, :], h[0:m.im, x % 2, :], m.hid_h[0:m.im, x % 2, :],
                                  ALU.subtract).then_inc(m.s["hl"], 1)

            def rows_down(n, turn, x):
                dve.wait_ge(m.s["y"], n + (x + 5))
                dve.wait_ge(m.s_yw[x % 4], 16 * 2 * m.nt * turn + 16 * m.nt * (x // 4 + 1))
                dve.tensor_scalar(m.y[0:m.lot, x % 4, :, :], bank[4 + x % 2][0:m.lot, 0:m.nt * D].rearrange(
                    "p (i d) -> p i d", i=m.nt), 1.0 / WS, None, ALU.mult).then_inc(m.s["ye"], 1)

            def step(n, it, turn, j, more):
                if more or j + 1 < 8:
                    hidden(n, j + 1)
                if more or j + 3 < 8:
                    weights_low(n, j + 3)
                rows_down(n, turn, j)

            for x in range(3):
                weights_low(r * m.E, x)
            hidden(r * m.E, 0)
            experts_loop(dve, m, r, step)

        def gather_sp(sp, m, rounds):
            for i in range(4):
                sp.wait_ge(m.s_yw[i], rounds * (16 * m.nt * m.E // 4) + 16 * m.nt)
            for b in range(B):
                if b >= 3:
                    sp.wait_ge(m.s["acc"], m.K * (b - 2))
                sp.dma_start(m.back[:, b % 3, :, :], m.y_rows[0:m.K * T, :].rearrange("(k t p) d -> p t k d", k=m.K, p=P)[:, b, :, :]
                             ).then_inc(m.s_back[b % 3], 16)

        def gather_dve(dve, m, b):
            dve.wait_ge(m.s_back[b % 3], 16 * (b // 3 + 1))
            for k in range(m.K):
                if k:
                    dve.wait_ge(m.s["acc"], m.K * b + k)
                dve.scalar_tensor_tensor(out=acc[:, b, :], in0=m.back[:, b % 3, k, :], scalar=m.weight[:, b, k:k + 1],
                                         in1=acc[:, b, :], op0=ALU.mult, op1=ALU.add).then_inc(m.s["acc"], 1)
            dve.wait_ge(m.s["acc"], m.K * b + m.K)

        def norm_all_dve(dve, chain, n, m, transposed):
            for b in range(B + 1):
                if b < B:
                    gather_dve(dve, m, b)
                    norm_stats(dve, chain, n, b, acc[:, b, :])
                if b >= 1:
                    norm_apply(dve, n, b - 1, acc[:, b - 1, :])
                if transposed and b >= 2 and b % 2 == 0:
                    norm_lo(dve, n, b // 2 - 1)

        def round_sp(sp, m, r):
            def step(n, it, turn, j, more):
                if j % 4 == 3:
                    sp.wait_ge(m.s["wl"], n + j + 1)
                    load_group(sp, m, (it * 2 + 2 + j // 4) if more else j // 4, j // 4)

            experts_loop(sp, m, r, step)

        def credits_sp(sp, m):
            for edge, free in (("t", 4), ("xc", 2), ("u", 4), ("y", 4), ("hl", 2), ("silu", 2), ("ye", 4), ("placed", 4),
                               ("send", 1), ("fetch", 1)):
                sp.sem_inc(m.s[edge], free)
            if m.gated:
                sp.sem_inc(m.s["hread"], 2)

        def credits_pool(pool, m):
            row = m.K * T + m.E * m.nt * P
            for q in range(4 * m.nt):
                pool.dma_start(m.y_rows[row + q:row + q + 1, 0:P], ident[0:1, :]).then_inc(m.s_yw[q % 4], 16)

        second = Region(CONV_WORDS)
        e0 = Experts("e0", second, 64, 6, 88, False, P, 1, ins["gate0"], ins["up0"], ins["down0"], 0)
        row_parts = sb("row_parts", [P, B, 2 * D], F16)
        shared = Region(0, arena2)
        SW = 352
        SI = SW // 4
        sg_f = shared("sg_f", [P, DH, 2 * SW])
        sg_h = shared("sg_h", [P, DH, 2 * SW], F16)
        sg_l = shared("sg_l", [P, DH, 2 * SW], F16)
        sd_f = shared("sd_f", [P, 4, D])
        sd_h = shared("sd_h", [P, 4, D], F16)
        sd_l = shared("sd_l", [P, 4, D], F16)
        sact = shared("sact", [P, 2, HALF])
        shid = shared("shid", [P, 2, HALF])
        shid_h = shared("shid_h", [P, B, HALF], F16)
        shid_l = shared("shid_l", [P, B, HALF], F16)
        c_u = sem("c_u")
        c_act = sem("c_act")
        c_hid = sem("c_hid")
        c_hh = sem("c_hh")
        c_hl = sem("c_hl")
        y_ready = sem("y_ready")
        acc_ready = sem("acc_ready")
        n3 = Norm(3, 2, 1)

        def stage3_sp(sp):
            sp.dma_start(before_f[:, :], ins["c_before"]).then_inc(s_c3, 16)
            sp.dma_start(iota[:, :], ins["c_iota"].partition_broadcast(P)).then_inc(s_c3, 16)
            sp.dma_start(tokens[:, :], ins["c_tokens"]).then_inc(s_c3, 16)
            sp.dma_start(kth[:, :], ins["c_pick_rows"].partition_broadcast(P)).then_inc(s_c3, 16)
            credits_sp(sp, e0)
            sp.wait_ge(done.x, n1.x + B)
            route_sp(sp, e0, n2)
            sp.wait_ge(b_o, H)
            sp.dma_start(sg_f[:, :, :], ins["shared_up"].rearrange("(d p) n -> p d n", p=P)).then_inc(weights_in, 16)
            sp.dma_start(sd_f[0:SI, :, :], ins["shared_down"].rearrange("(t p) n -> p t n", p=SI)).then_inc(weights_in, 16)
            rows_sp(sp, e0)
            rounds = read_rounds(sp, e0)
            with sp.Fori(0, rounds) as r:
                round_sp(sp, e0, r)
            gather_sp(sp, e0, rounds)
            for i in range(2):
                sp.wait_ge(e0.s_ring[i], rounds * (32 * e0.NI) + 32)

        def stage3_act(act):
            act.wait_ge(s_c3, 64)
            act.activation(before[:, :], before_f[:, :], ACT.Copy).then_inc(s_idh, 1)
            act.activation(identh[:, :], ident[:, :], ACT.Copy).then_inc(s_idh, 1)
            act.activation(iotah[:, :], iota[:, :], ACT.Copy).then_inc(s_idh, 1)
            gate_act(act, e0)
            act.wait_ge(weights_in, 16 + 32)
            act.activation(sg_h[:, :, :], sg_f[:, :, :], ACT.Copy, scale=WS).then_inc(weights_high, 1)
            act.activation(sd_h[0:SI, :, :], sd_f[0:SI, :, :], ACT.Copy, scale=WS).then_inc(weights_high, 1)
            for b in range(B):
                rows_act(act, e0, n2, b)
            soft_act(act, e0)
            for b in range(B):
                act.wait_ge(c_u, b + 1)
                if b >= 2:
                    act.wait_ge(c_hid, b - 1)
                act.activation(sact[0:SI, b % 2, :], bank[4 + 2 * (b % 2)][0:SI, :], ACT.Silu, scale=1.0 / WS).then_inc(c_act, 1)
                act.wait_ge(c_hid, b + 1)
                act.activation(shid_h[0:SI, b, :], shid[0:SI, b % 2, :], ACT.Copy).then_inc(c_hh, 1)
            rounds = read_rounds(act, e0)
            with act.Fori(0, rounds) as r:
                round_act(act, e0, r)
            for p in range(4):
                norm_hi(act, n3, p)

        def stage3_dve(dve, chain):
            chain.link(dve.memset(onesh[:, :], 1.0))
            gate_dve(dve, e0)
            dve.wait_ge(weights_high, 1 + 2)
            dve.scalar_tensor_tensor(out=sg_l[:, :, :], in0=sg_f[:, :, :], scalar=WS, in1=sg_h[:, :, :],
                                     op0=ALU.mult, op1=ALU.subtract).then_inc(weights_low, 1)
            dve.scalar_tensor_tensor(out=sd_l[0:SI, :, :], in0=sd_f[0:SI, :, :], scalar=WS, in1=sd_h[0:SI, :, :],
                                     op0=ALU.mult, op1=ALU.subtract).then_inc(weights_low, 1)
            dve.wait_ge(s_c3, 64)
            dve.wait_ge(s_idh, 3)
            spare_dve(dve, chain, e0)

            def share_out(b):
                dve.wait_ge(y_ready, b + 1)
                dve.scalar_tensor_tensor(out=acc[:, b, :], in0=bank[b % 2][:, 0:D], scalar=1.0 / WS, in1=X[:, b, :],
                                         op0=ALU.mult, op1=ALU.add).then_inc(acc_ready, 1)

            for b in range(B):
                pick_dve(dve, chain, e0, b)
            weigh_dve(dve, chain, e0, None)

            def shared_hidden(b):
                dve.wait_ge(c_act, b + 1)
                if b >= 2:
                    dve.wait_ge(c_hl, b - 1)
                dve.scalar_tensor_tensor(out=shid[0:SI, b % 2, :], in0=bank[5 + 2 * (b % 2)][0:SI, :], scalar=1.0 / WS,
                                         in1=sact[0:SI, b % 2, :], op0=ALU.mult, op1=ALU.mult).then_inc(c_hid, 1)

            def shared_low(b):
                dve.wait_ge(c_hh, b + 1)
                dve.tensor_tensor(shid_l[0:SI, b, :], shid[0:SI, b % 2, :], shid_h[0:SI, b, :],
                                  ALU.subtract).then_inc(c_hl, 1)

            for b in range(B + 1):
                if b < B:
                    shared_hidden(b)
                if b >= 1:
                    shared_low(b - 1)
                if b == 2:
                    rank_dve(dve, chain, e0, None)
            rounds_dve(dve, chain, e0)
            for b in range(B):
                share_out(b)
            rounds = read_rounds(dve, e0)
            with dve.Fori(0, rounds) as r:
                lists_dve(dve, e0, r)
                round_dve(dve, e0, r)
            norm_all_dve(dve, chain, n3, e0, True)

        def stage3_pe(pe):
            pe.wait_ge(e0.s["gl"], e0.before["gl"] + 1)
            for b in range(B):
                logits_pe(pe, e0, n2, b)
            pe.wait_ge(weights_low, 1 + 2)
            pe.wait_ge(s_idh, 3)

            def shared_up(b):
                th, t = b // 4, b % 4
                if b >= 2:
                    pe.wait_ge(c_hid, b - 1)
                for i in range(2):
                    k = 0
                    c0 = i * SW + t * SI
                    for d in range(DH):
                        for wp, xp in ((sg_h, xTh), (sg_l, xTh), (sg_h, xTl)):
                            mm = pe.matmul(bank[4 + 2 * (b % 2) + i][0:SI, :], wp[:, d, c0:c0 + SI],
                                           xp[:, d, th * HALF:(th + 1) * HALF], start=(k == 0), stop=(k == 3 * DH - 1))
                            k += 1
                mm.then_inc(c_u, 1)

            def shared_down(th):
                pe.wait_ge(c_hl, 4 * th + 4)
                for i in range(4):
                    b = 4 * th + i
                    if b >= 2:
                        pe.wait_ge(acc_ready, b - 1)
                    k = 0
                    for t in range(4):
                        for wp, hp in ((sd_h, shid_h), (sd_l, shid_h), (sd_h, shid_l)):
                            mm = pe.matmul(bank[b % 2][:, 0:D], hp[0:SI, 4 * th + t, i * P:(i + 1) * P], wp[0:SI, t, :],
                                           start=(k == 0), stop=(k == 11))
                            k += 1
                    mm.then_inc(y_ready, 1)

            for b in range(B):
                shared_up(b)
                if b == 1:
                    rank_pe(pe, e0)
            pe.wait_ge(e0.s["lread"], e0.before["lread"] + B)
            shared_down(0)
            shared_down(1)
            rounds = read_rounds(pe, e0)
            with pe.Fori(0, rounds) as r:
                lists_pe(pe, e0, r)
                round_pe(pe, e0, r)
            for p in range(4):
                norm_transpose(pe, n3, p)

        def stage3_pool(pool, chain):
            credits_pool(pool, e0)
            for b in range(B):
                rows_pool(pool, e0, b)
            name_pool(pool, e0)
            pool.wait_ge(e0.s_rows, e0.before["rows"] + 16 * B)
            rounds = read_rounds(pool, e0)
            with pool.Fori(0, rounds) as r:
                round_pool(pool, e0, r)
            for b in range(B):
                norm_rstd(pool, chain, n3, b)

        retain = Region(0, arena2)
        r_wf = retain("r_wf", [P, DH, 5, D])
        r_wh = retain("r_wh", [P, DH, 5, D], F16)
        r_wl = retain("r_wl", [P, DH, 5, D], F16)
        turns = retain("turns", [P, 4, DH, P])
        fade = retain("fade", [P, P])
        rqk = retain("rqk", [P, 2, DH, T])
        part = retain("part", [P, 2, 2, HALF])
        att = retain("att", [P, 2, P])
        tables_in = sem("tables_in")
        d_p = sem("d_p")
        d_pr = sem("d_pr")
        d_qk = sem("d_qk")
        d_v = sem("d_v")
        d_vc = sem("d_vc")
        scores_ready = sem("scores_ready")
        d_a = sem("d_a")
        n4 = Norm(4, 2, 2)

        def clear_sp(sp):
            sp.wait_ge(s_mh, 2)
            for k in range(e1.K):
                sp.dma_start(e1.y_rows[k * T:(k + 1) * T, :].rearrange("(t p) d -> p t d", p=P),
                             zero[:, None, :].broadcast_to([P, B, D])).then_inc(s_cleared, 16)

        def stage4_sp(sp):
            sp.wait_ge(acc_ready, B)
            sp.dma_start(r_wf[:, :, :, :], ins["w_qkv1"].rearrange("(d p) (c n) -> p d c n", p=P, c=5)).then_inc(weights_in, 16)
            sp.dma_start(turns[:, :, :, :], ins["c_turns"].rearrange("c (d p) t -> p c d t", p=P)).then_inc(tables_in, 16)
            sp.dma_start(fade[:, :], ins["c_fade"]).then_inc(tables_in, 16)
            clear_sp(sp)

        def stage4_pe(pe):
            pe.wait_ge(weights_high, 1 + 2 + 1)
            pe.wait_ge(weights_low, 1 + 2 + 1)
            for u in range(8):
                th, o, qk = u // 4, u // 2 % 2, u % 2
                pe.wait_ge(done.lo, n3.lo + 2 * th + 2)
                if u >= 2:
                    pe.wait_ge(d_pr, u - 1)
                for i in range(2):
                    k = 0
                    for d in range(DH):
                        for wp, xp in ((r_wh, xTh), (r_wl, xTh), (r_wh, xTl)):
                            mm = pe.matmul(bank[2 * (u % 2) + i][:, :], wp[:, d, 2 * qk + i, o * P:(o + 1) * P],
                                           xp[:, d, th * HALF:(th + 1) * HALF], start=(k == 0), stop=(k == 3 * DH - 1))
                            k += 1
                mm.then_inc(d_p, 1)
            for b in range(B):
                if b >= 2:
                    pe.wait_ge(d_vc, b - 1)
                k = 0
                for d in range(DH):
                    for wp, xp in ((r_wh, xTh), (r_wl, xTh), (r_wh, xTl)):
                        mm = pe.matmul(bank[4 + b % 2][:, 0:D], xp[:, d, b * P:(b + 1) * P], wp[:, d, 4, :],
                                       start=(k == 0), stop=(k == 3 * DH - 1))
                        k += 1
                mm.then_inc(d_v, 1)
            pe.wait_ge(d_pr, 8)

            def scores(b):
                pe.wait_ge(d_qk, 4 * (b // 4) + 4)
                if b >= 2:
                    pe.wait_ge(d_a, b - 1)
                for d in range(DH):
                    mm = pe.matmul(bank[b % 2][:, 0:P], rqk[:, 1, d, b * P:(b + 1) * P], rqk[:, 0, d, b * P:(b + 1) * P],
                                   start=(d == 0), stop=(d == DH - 1))
                mm.then_inc(scores_ready, 1)

            for b in range(B + 1):
                if b < B:
                    scores(b)
                if b >= 1:
                    pe.wait_ge(d_a, b)
                    pe.wait_ge(d_vc, b)
                    if b >= 3:
                        pe.wait_ge(done.sum, n4.sum + b - 2)
                    pe.matmul(bank[2 + (b - 1) % 2][:, 0:D], att[:, (b - 1) % 2, :], acc[:, b - 1, :], start=True, stop=True
                              ).then_inc(y_ready, 1)
            for p in range(4):
                norm_transpose(pe, n4, p)

        def stage4_act(act):
            act.wait_ge(weights_in, 16 + 32 + 16)
            act.activation(r_wh[:, :, :, :], r_wf[:, :, :, :], ACT.Copy, scale=WS).then_inc(weights_high, 1)
            act.wait_ge(done.x, n3.x + B)
            for b in range(B):
                act.wait_ge(d_v, b + 1)
                act.activation(acc[:, b, :], bank[4 + b % 2][:, 0:D], ACT.Copy, scale=1.0 / WS).then_inc(d_vc, 1)
            for p in range(4):
                act.wait_ge(done.t, n4.t + p + 1)
                act.activation(xTf[:, :, p * 256:(p + 1) * 256], bank[6 + p % 2][:, :].rearrange("q (d t) -> q d t", d=DH),
                               ACT.Copy).then_inc(done.lo, 1)

        def stage4_dve(dve, chain):
            dve.wait_ge(weights_high, 1 + 2 + 1)
            dve.scalar_tensor_tensor(out=r_wl[:, :, :, :].rearrange("p d c n -> p (d c n)"),
                                     in0=r_wf[:, :, :, :].rearrange("p d c n -> p (d c n)"), scalar=WS,
                                     in1=r_wh[:, :, :, :].rearrange("p d c n -> p (d c n)"),
                                     op0=ALU.mult, op1=ALU.subtract).then_inc(weights_low, 1)
            dve.wait_ge(tables_in, 32)
            for u in range(8):
                th, o, qk = u // 4, u // 2 % 2, u % 2
                dve.wait_ge(d_p, u + 1)
                if u >= 2:
                    dve.wait_ge(d_qk, u - 1)
                for i in range(2):
                    mm = dve.scalar_tensor_tensor(out=part[:, u % 2, i, :].rearrange("p (b t) -> p b t", b=4),
                                                  in0=bank[2 * (u % 2) + i][:, :].rearrange("p (b t) -> p b t", b=4), scalar=1.0 / WS,
                                                  in1=turns[:, 2 * qk + i, o, None, :].broadcast_to([P, 4, P]),
                                                  op0=ALU.mult, op1=ALU.mult)
                mm.then_inc(d_pr, 1)

            def fade_scores(b):
                dve.wait_ge(scores_ready, b + 1)
                if b >= 2:
                    dve.wait_ge(y_ready, B + b - 1)
                dve.tensor_tensor(att[:, b % 2, :], bank[b % 2][:, 0:P], fade[:, :], ALU.mult).then_inc(d_a, 1)

            for b in range(B + 2):
                if b < B:
                    fade_scores(b)
                if 1 <= b < B + 1:
                    dve.wait_ge(y_ready, B + b)
                    norm_sum(dve, chain, n4, b - 1, bank[2 + (b - 1) % 2][:, 0:D], 1.0)
                if b >= 2:
                    norm_apply(dve, n4, b - 2)

        def stage4_pool(pool, chain):
            pool.memset(zero[:, :], 0.0).then_inc(s_mh, 1)
            for u in range(8):
                th, o, qk = u // 4, u // 2 % 2, u % 2
                pool.wait_ge(d_pr, u + 1)
                pool.tensor_tensor(rqk[:, qk, o, th * HALF:(th + 1) * HALF], part[:, u % 2, 0, :], part[:, u % 2, 1, :],
                                   ALU.add).then_inc(d_qk, 1)
            for b in range(B):
                norm_rstd(pool, chain, n4, b)

        look = Region()
        ctxT = look("ctxT", [P, DH, T])
        ctxm = look("ctxm", [P, B, D])
        xTf = look("xTf", [P, DH, T])
        seen = look("seen", [P, T])
        unseen = look("unseen", [P, T])
        seen8 = look("seen8", [P, T], U8)
        sc5 = look("sc5", [P, 2, P])
        p5 = look("p5", [P, 2, P])
        pT5 = look("pT5", [P, 2, P])
        valid = sb("valid", [P, B])
        peak = sb("peak", [P, B])
        sum5 = sb("sum5", [P, B])
        f_sr = sem("f_sr")
        f_mx = sem("f_mx")
        f_e = sem("f_e")
        ctx_in = sem("ctx_in")
        n5 = Norm(5, 3, 2)

        def stage5_sp(sp):
            sp.wait_ge(done.sum, n2.sum + B)
            sp.dma_start(ctxT[:, :, :], ins["ctxT"].rearrange("(d p) t -> p d t", p=P)).then_inc(ctx_in, 16)
            sp.dma_start(ctxm[:, :, :], ins["ctx"].rearrange("b p d -> p b d")).then_inc(ctx_in, 16)
            sp.dma_start(seen8[:, :], ins["mask"].partition_broadcast(P)).then_inc(ctx_in, 16)

        def stage5_pe(pe):
            pe.wait_ge(ctx_in, 48)

            def scores(b):
                pe.wait_ge(done.lo, n4.lo + b // 2 + 1)
                if b >= 2:
                    pe.wait_ge(f_sr, b - 1)
                for d in range(DH):
                    mm = pe.matmul(bank[b % 2][:, 0:P], xTf[:, d, b * P:(b + 1) * P], ctxT[:, d, b * P:(b + 1) * P],
                                   start=(d == 0), stop=(d == DH - 1))
                mm.then_inc(scores_ready, 1)

            def turn(b):
                pe.wait_ge(f_e, b + 1)
                if b >= 2:
                    pe.wait_ge(d_vc, B + b - 1)
                pe.transpose(bank[2 + b % 2][:, 0:P], p5[:, b % 2, :], ident[:, :]).then_inc(d_v, 1)

            def read(b):
                pe.wait_ge(d_vc, B + b + 1)
                if b >= 2:
                    pe.wait_ge(done.sum, n5.sum + b - 1)
                pe.matmul(bank[4 + b % 2][:, 0:D], pT5[:, b % 2, :], ctxm[:, b, :], start=True, stop=True).then_inc(y_ready, 1)

            for b in range(B + 2):
                if b < B:
                    scores(b)
                if 1 <= b < B + 1:
                    turn(b - 1)
                if b >= 2:
                    read(b - 2)
            for p in range(4):
                norm_transpose(pe, n5, p)

        def stage5_act(act):
            def weigh(b):
                act.wait_ge(f_mx, b + 1)
                if b >= 2:
                    act.wait_ge(d_v, B + b - 1)
                act.activation(p5[:, b % 2, :], sc5[:, b % 2, :], ACT.Exp, bias=peak[:, b:b + 1],
                               accum_out=sum5[:, b:b + 1]).then_inc(f_e, 1)

            def copy(b):
                act.wait_ge(d_v, B + b + 1)
                if b >= 2:
                    act.wait_ge(y_ready, 2 * B + b - 1)
                act.activation(pT5[:, b % 2, :], bank[2 + b % 2][:, 0:P], ACT.Copy).then_inc(d_vc, 1)

            for b in range(B + 1):
                if b < B:
                    weigh(b)
                if b >= 1:
                    copy(b - 1)
            for p in range(4):
                norm_hi(act, n5, p)

        def masks_dve(dve, chain):
            dve.wait_ge(ctx_in, 48)
            chain.link(dve.tensor_copy(seen[:, :], seen8[:, :]))
            chain.link(dve.tensor_scalar(unseen[:, :], seen[:, :], -1.0, 1e30, ALU.add, ALU.mult))
            chain.link(dve.tensor_reduce(valid[:, :], seen[:, :].rearrange("p (b m) -> p b m", b=B), AX.X, ALU.max))

        def stage5_dve(dve, chain):
            def mask(b):
                dve.wait_ge(scores_ready, B + b + 1)
                if b >= 2:
                    dve.wait_ge(f_e, b - 1)
                dve.scalar_tensor_tensor(out=sc5[:, b % 2, :], in0=bank[b % 2][:, 0:P], scalar=float(D) ** -0.5,
                                         in1=seen[:, b * P:(b + 1) * P], op0=ALU.mult, op1=ALU.mult).then_inc(f_sr, 1)
                dve.wait_ge(f_sr, b + 1)
                chain.link(dve.tensor_tensor(sc5[:, b % 2, :], sc5[:, b % 2, :], unseen[:, b * P:(b + 1) * P], ALU.add))
                chain.link(dve.tensor_reduce(peak[:, b:b + 1], sc5[:, b % 2, :], AX.X, ALU.max))
                dve.tensor_scalar(peak[:, b:b + 1], peak[:, b:b + 1], -1.0, None, ALU.mult).then_inc(f_mx, 1)

            def add(b):
                dve.wait_ge(f_e, b + 1)
                chain.link(dve.reciprocal(sum5[:, b:b + 1], sum5[:, b:b + 1]))
                chain.link(dve.tensor_tensor(sum5[:, b:b + 1], sum5[:, b:b + 1], valid[:, b:b + 1], ALU.mult))
                dve.wait_ge(y_ready, 2 * B + b + 1)
                norm_sum(dve, chain, n5, b, bank[4 + b % 2][:, 0:D], sum5[:, b:b + 1])

            for b in range(B + 4):
                if b < B:
                    mask(b)
                if 2 <= b < B + 2:
                    add(b - 2)
                if 3 <= b < B + 3:
                    norm_apply(dve, n5, b - 3)
            for p in range(4):
                norm_lo(dve, n5, p)

        def stage5_pool(pool, chain):
            for b in range(B):
                norm_rstd(pool, chain, n5, b)

        e1 = Experts("e1", Region(CONV_WORDS), 32, 8, 96, True, 96, 2, ins["gate1"], ins["up1"], ins["down1"], 1)
        n6 = Norm(6, 4, 3)
        s_cleared = sem("s_cleared")
        zero = Region(ARENA2 - D, arena2)("zero", [P, D])
        KEEP = 0.8

        def stage6_sp(sp):
            credits_sp(sp, e1)
            sp.wait_ge(done.x, n3.x + B)
            route_sp(sp, e1, n5)
            rows_sp(sp, e1)
            rounds = read_rounds(sp, e1)
            with sp.Fori(0, rounds) as r:
                round_sp(sp, e1, r)
            gather_sp(sp, e1, rounds)
            for i in range(2):
                sp.wait_ge(e1.s_ring[i], rounds * (32 * e1.NI) + 32)
            for b in range(B):
                sp.wait_ge(done.x, n6.x + b + 1)
                sp.dma_start(out[b, :, :], X[:, b, :]).then_inc(s_out, 16)
            sp.wait_ge(s_out, 16 * B)

        def stage6_act(act):
            gate_act(act, e1)
            for b in range(B):
                rows_act(act, e1, n5, b)
            soft_act(act, e1)
            rounds = read_rounds(act, e1)
            with act.Fori(0, rounds) as r:
                round_act(act, e1, r)

        def stage6_dve(dve, chain):
            spare_dve(dve, chain, e1)
            gate_dve(dve, e1)
            for b in range(B):
                pick_dve(dve, chain, e1, b)
            weigh_dve(dve, chain, e1, KEEP)
            for b in range(B):
                dve.tensor_copy(acc[:, b, :], X[:, b, :]).then_inc(acc_ready, 1)
            rank_dve(dve, chain, e1, KEEP)
            rounds_dve(dve, chain, e1)
            dve.wait_ge(acc_ready, B + B)
            rounds = read_rounds(dve, e1)
            with dve.Fori(0, rounds) as r:
                lists_dve(dve, e1, r)
                round_dve(dve, e1, r)
            norm_all_dve(dve, chain, n6, e1, False)

        def stage6_pe(pe):
            pe.wait_ge(e1.s["gl"], e1.before["gl"] + 1)
            for b in range(B):
                logits_pe(pe, e1, n5, b)
            rank_pe(pe, e1)
            rounds = read_rounds(pe, e1)
            with pe.Fori(0, rounds) as r:
                lists_pe(pe, e1, r)
                round_pe(pe, e1, r)

        def stage6_pool(pool, chain):
            credits_pool(pool, e1)
            for b in range(B):
                rows_pool(pool, e1, b)
            name_pool(pool, e1)
            pool.wait_ge(e1.s_rows, e1.before["rows"] + 16 * B)
            pool.wait_ge(s_cleared, 16 * e1.K)
            rounds = read_rounds(pool, e1)
            with pool.Fori(0, rounds) as r:
                round_pool(pool, e1, r)
            for b in range(B):
                norm_rstd(pool, chain, n6, b)


        block = ctx.enter_context(nc.Block())

        @block.sync
        def _(sp):
            stage1_sp(sp)
            stage2_sp(sp)
            stage3_sp(sp)
            stage4_sp(sp)
            stage5_sp(sp)
            stage6_sp(sp)

        @block.tensor
        def _(pe):
            stage1_pe(pe)
            stage2_pe(pe)
            stage3_pe(pe)
            stage4_pe(pe)
            stage5_pe(pe)
            stage6_pe(pe)

        @block.scalar
        def _(act):
            stage1_act(act)
            stage2_act(act)
            stage3_act(act)
            stage4_act(act)
            stage5_act(act)
            stage6_act(act)

        @block.vector
        def _(dve):
            chain = Chain(dve, dve_chain_sem)
            stage1_dve(dve, chain)
            stage2_dve(dve, chain)
            stage3_dve(dve, chain)
            stage4_dve(dve, chain)
            masks_dve(dve, chain)
            stage5_dve(dve, chain)
            stage6_dve(dve, chain)

        @block.gpsimd
        def _(pool):
            chain = Chain(pool, pool_chain_sem)
            stage1_pool(pool, chain)
            stage2_pool(pool, chain)
            stage3_pool(pool, chain)
            stage4_pool(pool, chain)
            stage5_pool(pool, chain)
            stage6_pool(pool, chain)

def _heads_apart(w):
    return np.repeat(w.reshape(D, H, 1, HD), 2, axis=2).reshape(D, 2 * D)


def _way_up(w):
    e, n, _ = w.shape
    return w.reshape(e // 4, 4, n, DH, P).transpose(0, 4, 1, 3, 2).reshape(e // 4, P, 4, DH * n)


def _way_down(w, tiles):
    e, _, n = w.shape
    return w.reshape(e // 4, 4, D, tiles, n // tiles).transpose(0, 4, 1, 3, 2).reshape(e // 4, n // tiles, 4, tiles * D)


def _turns():
    at = np.arange(P, dtype=np.float32)
    pair = np.arange(0, D, 2, dtype=np.float32)
    scale = ((pair + np.float32(0.4 * D)) / np.float32(1.4 * D))[None, :] ** (at / np.float32(SCALE_BASE))[:, None]
    angle = at[:, None] * (np.float32(1.0) / np.float32(10000.0) ** (np.arange(D // 2, dtype=np.float32) / np.float32(D // 2)))
    sign = np.where(np.arange(D) % 2 == 0, -1.0, 1.0)[None, :]
    tables = []
    for s in (scale, np.float32(1.0) / scale):
        tables.append(np.repeat(np.cos(angle) * s, 2, axis=1).T)
        tables.append((np.repeat(np.sin(angle) * s, 2, axis=1) * sign).T)
    return np.stack(tables)


def _swap_pairs(w):
    return w.reshape(D, D // 2, 2)[:, :, ::-1].reshape(D, D)


def _constants():
    i = np.arange(P)
    key, query = i[:, None], i[None, :]
    c = {
        "c_ident": np.eye(P),
        "c_lows": np.where(key % 32 < HD, 0, -1),
        "c_diff": np.maximum(query - key, 0),
        "c_causal": query >= key,
        "c_turns": _turns(),
        "c_fade": np.where(query >= key, GAMMA ** np.maximum(query - key, 0), 0.0),
        "c_before": key < query,
        "c_iota": np.arange(IOTA),
        "c_tokens": key + P * np.arange(B) + 1,
        "c_pick_rows": T * np.arange(8),
        "c_anti": key + query == P - 1,
    }
    return {k: np.ascontiguousarray(v, np.float32) for k, v in c.items()}


def _layout(i):
    w = i["L0_attn_W_qkvu"].T
    a = {
        "x": i["x"],
        "xT": i["x"].reshape(T, D).T,
        "w_qkvu": np.concatenate([_heads_apart(w[:, :D]), _heads_apart(w[:, D:2 * D]), w[:, 2 * D:]], axis=1),
        "w_out": i["L0_attn_W_out"].T,
        "ctx_rev": i["ctx_2048"].transpose(2, 1, 0).reshape(DH, P, P * B)[:, ::-1].transpose(1, 0, 2).reshape(P, -1),
        "filters": np.concatenate([np.zeros((H, P - 1), np.float32), i["L0_xattn_ssm_kernel"]], axis=1),
        "w_qkv1": np.concatenate([i["L1_attn_W_Q"], _swap_pairs(i["L1_attn_W_Q"]), i["L1_attn_W_K"],
                                  _swap_pairs(i["L1_attn_W_K"]), i["L1_attn_W_V"]], axis=1),
        "ctx": i["ctx_2048"],
        "ctxT": i["ctx_2048"].reshape(T, D).T,
        "mask": i["mask_BxS2_bk0"].reshape(T),
        "gate1": i["L1_ffn_gate_weight"].T,
        "up1": _way_up(i["L1_ffn_gate_up_proj"]),
        "down1": _way_down(i["L1_ffn_down_proj"], 1),
        "gate0": i["L0_ffn_gate_w"].T,
        "up0": _way_up(i["L0_ffn_experts_w1"]),
        "down0": _way_down(i["L0_ffn_experts_w2"], 2),
        "shared_up": i["L0_ffn_shared_gate_up"].T,
        "shared_down": i["L0_ffn_shared_down"].T,
        "conv_d": i["L0_xattn_D"],
        "slope": i["L0_attn_slope_rate"].reshape(H),
    }
    return {k: np.ascontiguousarray(v) for k, v in a.items()} | _constants()


def kernel(**inputs):
    import concourse.bacc as bacc
    from concourse.bass_utils import run_bass_kernel_spmd

    nc = bacc.Bacc("TRN2", target_bir_lowering=False, num_devices=1)
    laid_out = _layout({name: np.asarray(value) for name, value in inputs.items()})
    arrays, ins = {}, {}
    for name, array in laid_out.items():
        arrays[f"in_{name}_dram"] = array
        ins[name] = nc.dram_tensor(f"in_{name}_dram", array.shape, mybir.dt.from_np(array.dtype), kind="ExternalInput").ap()
    out = nc.dram_tensor("out_0_dram", (B, P, D), F32, kind="ExternalOutput").ap()
    build_program(nc, ins, out)
    return run_bass_kernel_spmd(nc, [arrays], core_ids=[0]).results[0]["out_0_dram"]
```

```python
import numpy as np
from contextlib import ExitStack

import concourse.bass as bass
from concourse import mybir

F32 = mybir.dt.float32
F16 = mybir.dt.float16
I32 = mybir.dt.int32
U32 = mybir.dt.uint32
U8 = mybir.dt.uint8
ALU = mybir.AluOpType
ACT = mybir.ActivationFunctionType
AX = mybir.AxisListType

P = 128
D = 256
DH = D // P
B = 8
T = B * P
H = 16
HD = D // H
CJ = P // H
WS = 256.0
GAMMA = 0.96875
SCALE_BASE = 64
LN_EPS = 1e-5
RMS_EPS = 1e-6
ARENA = 28672
ARENA2 = 14336
PICKS = 11008
CONV_WORDS = 9216
BACK_SLOTS = 4
SPLIT_FROM = 2
SHARED = P // 2
IOTA = 2 * P
HALF = T // 2


class Chain:

    def __init__(self, engine, semaphore):
        self.engine, self.semaphore, self.n = engine, semaphore, 0

    def link(self, instruction):
        self.n += 1
        instruction.then_inc(self.semaphore, 1)
        self.engine.wait_ge(self.semaphore, self.n)


def build_program(nc, ins, out):
    with ExitStack() as ctx:
        def sb(name, shape, dt=F32):
            return ctx.enter_context(nc.sbuf_tensor(name, shape, dt))

        def sem(name):
            return ctx.enter_context(nc.semaphore(name))

        arena = sb("arena", [P, ARENA])
        arena2 = sb("arena2", [P, ARENA2])

        class Region:

            def __init__(self, start=0, memory=None):
                self.at = start
                self.memory = arena if memory is None else memory

            def __call__(self, name, shape, dt=F32):
                size = int(np.prod(shape[1:]))
                words = {F16: size // 2, U8: size // 4}.get(dt, size)
                view = self.memory[0:shape[0], self.at:self.at + words]
                self.at += words
                assert self.at <= self.memory.shape[1], (name, self.at)
                if dt != F32:
                    view = view.bitcast(dt)
                names = " ".join("abcde"[:len(shape) - 1])
                sizes = dict(zip("abcde", shape[1:]))
                return view.rearrange(f"p ({names}) -> p {names}", **sizes) if len(shape) > 2 else view

        bank = [ctx.enter_context(nc.psum_tensor(f"bank{i}", [P, 512], F32)) for i in range(8)]

        X = sb("X", [P, B, D])
        R = sb("R", [P, 4, D])
        xTh = sb("xTh", [P, DH, T], F16)
        xTl = sb("xTl", [P, DH, T], F16)
        stats = sb("stats", [P, 4, 6])
        mv = sb("mv", [P, B, 2])
        veps = sb("veps", [P, B])
        rstd = sb("rstd", [P, B])
        minus_half = sb("minus_half", [P, B])
        ident = sb("ident", [P, P])
        x_in = sem("x_in")
        ident_in = sem("ident_in")
        constant_set = sem("constant_set")
        out_written = sem("out_written")

        early = Region()
        w1h = early("w1h", [P, DH, 3, 512], F16)
        w1l = early("w1l", [P, DH, 3, 512], F16)
        wof = early("wof", [P, DH, D])
        woh = early("woh", [P, DH, D], F16)
        wol = early("wol", [P, DH, D], F16)
        later = Region(early.at)
        fresh = early("fresh", [P, 4, HALF])
        fresh_h = early("fresh_h", [P, 2, HALF], F16)
        lows = early("lows", [P, 1])
        qh = early("qh", [P, 4, T], F16)
        ql = early("ql", [P, 4, T], F16)
        kk = early("kk", [P, 4, T], F16)
        vh = early("vh", [P, B, D], F16)
        vl = early("vl", [P, B, D], F16)
        uu = early("uu", [P, B, D])
        diff = early("diff", [P, P])
        causal = early("causal", [P, P])
        slope = early("slope", [P, H])
        nslope = early("nslope", [P, H])
        decay = early("decay", [P, H, P])
        prob = early("prob", [P, 4, 4, P])
        ph = early("ph", [P, 4, 4, P], F16)
        pl = early("pl", [P, 4, 4, P], F16)
        junk = later("junk", [P, D])
        ssq = early("ssq", [P, B])
        rms = early("rms", [P, B])
        gated = later("gated", [P, 4, D])
        gTh = later("gTh", [P, 2, DH, P], F16)
        gTl = later("gTl", [P, 2, DH, P], F16)
        split_first = early.at
        xT0 = early("xT0", [P, DH, T])
        w1f = early("w1f", [P, DH, 3, 512])

        xt_in = sem("xt_in")
        w1_in = [sem(f"w1_in{i}") for i in range(3)]
        weights_in = sem("weights_in")
        masks_in = sem("masks_in")
        xt_high = sem("xt_high")
        xt_low = sem("xt_low")
        w1_high = sem("w1_high")
        w1_low = sem("w1_low")
        weights_high = sem("weights_high")
        weights_low = sem("weights_low")
        slopes_negated = sem("slopes_negated")
        decay_done = sem("decay_done")
        qk_product = sem("qk_product")
        qk_active = sem("qk_active")
        vu_product = sem("vu_product")
        qk_split = sem("qk_split")
        v_high = sem("v_high")
        v_low = sem("v_low")
        prob_high = sem("prob_high")
        prob_low_done = [sem(f"prob_low_done{i}") for i in range(2)]
        head_scores = sem("head_scores")
        prob_done = sem("prob_done")
        head_weighed = sem("head_weighed")
        squares_summed = sem("squares_summed")
        rms_done = sem("rms_done")
        gated_done = sem("gated_done")
        gated_turned = sem("gated_turned")
        gated_high = sem("gated_high")
        gated_low = sem("gated_low")
        attended = sem("attended")
        dve_chain_sem = sem("dve_chain")
        pool_chain_sem = sem("pool_chain")

        class NormDone:
            sum = sem("norm_sum")
            mv = sem("norm_mv")
            rstd = sem("norm_rstd")
            x = sem("norm_x")
            t = sem("norm_t")
            hi = sem("norm_hi")
            lo = sem("norm_lo")

        done = NormDone

        class Norm:

            def __init__(self, stage, sums, highs):
                self.sum = B * sums
                self.mv = self.rstd = self.x = B * (stage - 1)
                self.t = self.lo = B // 2 * (stage - 1)
                self.hi = B // 2 * highs

        n1 = Norm(1, 0, 0)

        def norm_sum(dve, chain, n, b, y, scale):
            if b >= 4:
                dve.wait_ge(done.x, n.x + b - 3)
            dve.scalar_tensor_tensor(out=R[:, b % 4, :], in0=y, scalar=scale, in1=X[:, b, :],
                                     op0=ALU.mult, op1=ALU.add).then_inc(done.sum, 1)
            dve.wait_ge(done.sum, n.sum + b + 1)
            norm_stats(dve, chain, n, b, R[:, b % 4, :])

        def norm_stats(dve, chain, n, b, src):
            chain.link(dve.bn_stats(stats[:, b % 4, :], src))
            dve.bn_aggr(mv[:, b, :], stats[:, b % 4, :]).then_inc(done.mv, 1)

        def norm_rstd(pool, chain, n, b):
            pool.wait_ge(done.mv, n.mv + b + 1)
            chain.link(pool.tensor_scalar(veps[:, b:b + 1], mv[:, b, 1:2], LN_EPS, None, ALU.add))
            pool.tensor_tensor(rstd[:, b:b + 1], veps[:, b:b + 1], minus_half[:, 0:1], ALU.pow).then_inc(done.rstd, 1)

        def norm_apply(dve, n, b, src=None):
            dve.wait_ge(done.rstd, n.rstd + b + 1)
            dve.tensor_scalar(X[:, b, :], R[:, b % 4, :] if src is None else src, mv[:, b, 0:1], rstd[:, b:b + 1],
                              ALU.subtract, ALU.mult).then_inc(done.x, 1)

        def norm_transpose(pe, n, p):
            pe.wait_ge(done.x, n.x + 2 * p + 2)
            if p >= 2:
                pe.wait_ge(done.lo, n.lo + p - 1)
            v = bank[6 + p % 2][:, :].rearrange("q (d b t) -> q d b t", d=DH, b=2)
            for i in range(2):
                for d in range(DH):
                    mm = pe.transpose(v[:, d, i, :], X[:, 2 * p + i, d * P:(d + 1) * P], ident[:, :])
            mm.then_inc(done.t, 1)

        def norm_hi(act, n, p):
            act.wait_ge(done.t, n.t + p + 1)
            act.activation(xTh[:, :, p * 256:(p + 1) * 256], bank[6 + p % 2][:, :].rearrange("q (d t) -> q d t", d=DH),
                           ACT.Copy).then_inc(done.hi, 1)

        def norm_lo(dve, n, p):
            dve.wait_ge(done.hi, n.hi + p + 1)
            dve.tensor_tensor(xTl[:, :, p * 256:(p + 1) * 256], bank[6 + p % 2][:, :].rearrange("q (d t) -> q d t", d=DH),
                              xTh[:, :, p * 256:(p + 1) * 256], ALU.subtract).then_inc(done.lo, 1)

        def stage1_sp(sp):
            sp.dma_start(slope[:, :], ins["slope"].partition_broadcast(P)).then_inc(masks_in, 16)
            sp.dma_start(diff[:, :], ins["c_diff"]).then_inc(masks_in, 16)
            sp.dma_start(causal[:, :], ins["c_causal"]).then_inc(masks_in, 16)
            sp.dma_start(xT0[:, :, :], ins["xT"].rearrange("(d p) t -> p d t", p=P)).then_inc(xt_in, 16)
            wv = ins["w_qkvu"].rearrange("(d p) (c n) -> p d c n", p=P, c=3)
            for c in range(3):
                sp.dma_start(w1f[:, :, c, :], wv[:, :, c, :]).then_inc(w1_in[c], 16)
            sp.dma_start(X[:, :, :], ins["x"].rearrange("b p d -> p b d")).then_inc(x_in, 16)
            sp.dma_start(lows[:, :], ins["c_lows"]).then_inc(x_in, 16)
            sp.dma_start(ident[:, :], ins["c_ident"]).then_inc(ident_in, 16)
            sp.dma_start(wof[:, :, :], ins["w_out"].rearrange("(d p) n -> p d n", p=P)).then_inc(weights_in, 16)

        def stage1_pe(pe):
            def proj(dst, cols, c, t0, n):
                k = 0
                for d in range(DH):
                    for wp, xp in ((w1h, xTh), (w1l, xTh), (w1h, xTl)):
                        mm = pe.matmul(dst, wp[:, d, c, cols:cols + P], xp[:, d, t0:t0 + n],
                                       start=(k == 0), stop=(k == 3 * DH - 1))
                        k += 1
                return mm

            pe.wait_ge(xt_high, DH)
            pe.wait_ge(xt_low, DH)
            g = 0
            for c in range(2):
                pe.wait_ge(w1_high, c + 1)
                pe.wait_ge(w1_low, c + 1)
                for th in range(2):
                    for q in range(4):
                        if g >= 4:
                            pe.wait_ge(qk_active, g - 3)
                        proj(bank[g % 4][:, :], q * P, c, th * HALF, HALF).then_inc(qk_product, 1)
                        g += 1
            pe.wait_ge(w1_high, 3)
            pe.wait_ge(w1_low, 3)
            pe.wait_ge(qk_active, 16)
            for b in range(B):
                if b >= 2:
                    pe.wait_ge(v_low, b - 1)
                k = 0
                for d in range(DH):
                    for wp, xp in ((w1h, xTh), (w1l, xTh), (w1h, xTl)):
                        mm = pe.matmul(bank[b % 2][:, :], xp[:, d, b * P:(b + 1) * P], wp[:, d, 2, :],
                                       start=(k == 0), stop=(k == 3 * DH - 1))
                        k += 1
                mm.then_inc(vu_product, 1)

            pe.wait_ge(qk_split, 16)
            pe.wait_ge(v_low, B)

            def weigh(j):
                th, h = j // H, j % H
                pe.wait_ge(prob_high, j + 1)
                pe.wait_ge(prob_low_done[j % 2], j // 2 + 1)
                for i in range(4):
                    b = 4 * th + i
                    for k, (pp, vp) in enumerate(((ph, vh), (ph, vl), (pl, vh))):
                        mm = pe.matmul(bank[4 + b // 2][:, (b % 2) * D + h * HD:(b % 2) * D + (h + 1) * HD],
                                       pp[:, j % 4, i, :], vp[:, b, h * HD:(h + 1) * HD], start=(k == 0), stop=(k == 2))
                mm.then_inc(head_weighed, 1)

            for j in range(2 * H):
                th, h = j // H, j % H
                q, a = h // 4, 32 * (h % 4)
                if j >= 4:
                    pe.wait_ge(prob_done, j - 3)
                for i in range(4):
                    t0 = th * HALF + i * P
                    for k, qp in enumerate((qh, ql)):
                        mm = pe.matmul(bank[j % 4][:, i * P:(i + 1) * P], kk[a:a + 2 * HD, q, t0:t0 + P],
                                       qp[a:a + 2 * HD, q, t0:t0 + P], start=(k == 0), stop=(k == 1))
                mm.then_inc(head_scores, 1)
                if j >= 3:
                    weigh(j - 3)
            weigh(2 * H - 3)
            weigh(2 * H - 2)
            weigh(2 * H - 1)

            pe.wait_ge(ident_in, 16)
            pe.wait_ge(weights_high, 1)
            pe.wait_ge(weights_low, 1)

            def turn(b):
                pe.wait_ge(gated_done, b + 1)
                if b >= 2:
                    pe.wait_ge(gated_low, b - 1)
                for d in range(DH):
                    mm = pe.transpose(bank[b % 2][:, d * P:(d + 1) * P], gated[:, b % 4, d * P:(d + 1) * P], ident[:, :])
                mm.then_inc(gated_turned, 1)

            def back(b):
                pe.wait_ge(gated_low, b + 1)
                if b >= 2:
                    pe.wait_ge(done.sum, n1.sum + b - 1)
                k = 0
                for d in range(DH):
                    for wp, xp in ((woh, gTh), (wol, gTh), (woh, gTl)):
                        mm = pe.matmul(bank[2 + b % 2][:, 0:D], xp[:, b % 2, d, :], wp[:, d, :],
                                       start=(k == 0), stop=(k == 3 * DH - 1))
                        k += 1
                mm.then_inc(attended, 1)

            for b in range(B + 1):
                if b < B:
                    turn(b)
                if b >= 1:
                    back(b - 1)
            for p in range(4):
                norm_transpose(pe, n1, p)

        def stage1_act(act):
            act.wait_ge(xt_in, 16)
            for d in range(DH):
                act.activation(xTh[:, d, :], xT0[:, d, :], ACT.Copy).then_inc(xt_high, 1)
            for c in range(3):
                act.wait_ge(w1_in[c], 16)
                act.activation(w1h[:, :, c, :], w1f[:, :, c, :], ACT.Copy, scale=WS).then_inc(w1_high, 1)
            act.wait_ge(slopes_negated, 1)
            for h in range(H):
                act.activation(decay[:, h, :], diff[:, :], ACT.Exp, scale=nslope[:, h:h + 1]).then_inc(decay_done, 1)
            for g in range(16):
                c, th, q = g // 8, g // 4 % 2, g % 4
                act.wait_ge(qk_product, g + 1)
                if g >= 4:
                    act.wait_ge(qk_split, g - 3)
                if c == 0:
                    act.activation(qh[:, q, th * HALF:(th + 1) * HALF], bank[g % 4][:, :], ACT.Silu, scale=1.0 / WS)
                act.activation(fresh[:, g % 4, :], bank[g % 4][:, :], ACT.Silu, scale=1.0 / WS).then_inc(qk_active, 1)
            for b in range(B):
                act.wait_ge(vu_product, b + 1)
                act.activation(uu[:, b, :], bank[b % 2][:, D:2 * D], ACT.Copy, scale=1.0 / WS)
                act.activation(vh[:, b, :], bank[b % 2][:, 0:D], ACT.Copy, scale=1.0 / WS).then_inc(v_high, 1)
            act.wait_ge(weights_in, 16)
            act.activation(woh[:, :, :], wof[:, :, :], ACT.Copy, scale=WS).then_inc(weights_high, 1)
            for j in range(2 * H):
                act.wait_ge(prob_done, j + 1)
                if j >= 4:
                    act.wait_ge(head_weighed, j - 3)
                act.activation(ph[:, j % 4, :, :], prob[:, j % 4, :, :], ACT.Copy).then_inc(prob_high, 1)
            for b in range(B):
                act.wait_ge(head_weighed, H * (b // 4 + 1))
                if b:
                    act.wait_ge(squares_summed, b)
                act.activation(junk[:, :], bank[4 + b // 2][:, (b % 2) * D:(b % 2 + 1) * D], ACT.Square,
                               accum_out=ssq[:, b:b + 1]).then_inc(squares_summed, 1)
            for b in range(B):
                act.wait_ge(gated_turned, b + 1)
                if b >= 2:
                    act.wait_ge(attended, b - 1)
                act.activation(gTh[:, b % 2, :, :], bank[b % 2][:, 0:D].rearrange("q (d t) -> q d t", d=DH),
                               ACT.Copy).then_inc(gated_high, 1)

        def prob_low(engine, j):
            engine.wait_ge(prob_high, j + 1)
            if j >= 4:
                engine.wait_ge(head_weighed, j - 3)
            engine.tensor_tensor(pl[:, j % 4, :, :], prob[:, j % 4, :, :], ph[:, j % 4, :, :],
                                 ALU.subtract).then_inc(prob_low_done[j % 2], 1)

        def stage1_dve(dve, chain):
            dve.wait_ge(masks_in, 48)
            dve.tensor_scalar(nslope[:, :], slope[:, :], -1.0, None, ALU.mult).then_inc(slopes_negated, 1)
            dve.wait_ge(xt_in, 16)
            for d in range(DH):
                dve.wait_ge(xt_high, d + 1)
                dve.tensor_tensor(xTl[:, d, :], xT0[:, d, :], xTh[:, d, :], ALU.subtract).then_inc(xt_low, 1)
            for c in range(3):
                dve.wait_ge(w1_high, c + 1)
                dve.scalar_tensor_tensor(out=w1l[:, :, c, :], in0=w1f[:, :, c, :], scalar=WS, in1=w1h[:, :, c, :],
                                         op0=ALU.mult, op1=ALU.subtract).then_inc(w1_low, 1)
            dve.wait_ge(decay_done, H)
            chain.link(dve.tensor_tensor(decay[:, :, :], decay[:, :, :], causal[:, None, :].broadcast_to([P, H, P]), ALU.mult))
            dve.wait_ge(x_in, 32)
            for g in range(16):
                c, th, q = g // 8, g // 4 % 2, g % 4
                at = slice(th * HALF, (th + 1) * HALF)
                dve.wait_ge(qk_active, g + 1)
                if c == 0:
                    dve.tensor_tensor(ql[:, q, at], fresh[:, g % 4, :], qh[:, q, at], ALU.subtract).then_inc(qk_split, 1)
                else:
                    if g >= 10:
                        dve.wait_ge(qk_split, g - 1)
                    chain.link(dve.tensor_copy(fresh_h[:, g % 2, :], fresh[:, g % 4, :]))
                    dve.scalar_tensor_tensor(out=kk[:, q, at], in0=fresh_h[:, g % 2, :], scalar=lows[:, 0:1],
                                             in1=fresh[:, g % 4, :], op0=ALU.mult, op1=ALU.add).then_inc(qk_split, 1)
            for b in range(B):
                dve.wait_ge(v_high, b + 1)
                dve.scalar_tensor_tensor(out=vl[:, b, :], in0=bank[b % 2][:, 0:D], scalar=1.0 / WS, in1=vh[:, b, :],
                                         op0=ALU.mult, op1=ALU.subtract).then_inc(v_low, 1)
                conv_filters_dve(dve, range(2 * b, 2 * b + 2))
            dve.wait_ge(weights_high, 1)
            dve.scalar_tensor_tensor(out=wol[:, :, :], in0=wof[:, :, :], scalar=WS, in1=woh[:, :, :],
                                     op0=ALU.mult, op1=ALU.subtract).then_inc(weights_low, 1)
            for j in range(2 * H):
                dve.wait_ge(head_scores, j + 1)
                if j >= 4:
                    dve.wait_ge(prob_high, j - 3)
                    dve.wait_ge(prob_low_done[j % 2], (j - 4) // 2 + 1)
                dve.tensor_tensor(prob[:, j % 4, :, :], bank[j % 4][:, :].rearrange("q (i t) -> q i t", i=4),
                                  decay[:, j % H, None, :].broadcast_to([P, 4, P]), ALU.mult).then_inc(prob_done, 1)
                if j % 2:
                    prob_low(dve, j - 1)

            def gate(b):
                dve.wait_ge(rms_done, b // 4 + 1)
                if b >= 4:
                    dve.wait_ge(gated_turned, b - 3)
                dve.scalar_tensor_tensor(out=gated[:, b % 4, :], in0=bank[4 + b // 2][:, (b % 2) * D:(b % 2 + 1) * D],
                                         scalar=rms[:, b:b + 1], in1=uu[:, b, :],
                                         op0=ALU.mult, op1=ALU.mult).then_inc(gated_done, 1)

            def low(b):
                dve.wait_ge(gated_high, b + 1)
                if b >= 2:
                    dve.wait_ge(attended, b - 1)
                dve.tensor_tensor(gTl[:, b % 2, :, :], bank[b % 2][:, 0:D].rearrange("q (d t) -> q d t", d=DH),
                                  gTh[:, b % 2, :, :], ALU.subtract).then_inc(gated_low, 1)

            for b in range(B + 3):
                if b < B:
                    gate(b)
                if 1 <= b < B + 1:
                    low(b - 1)
                if 2 <= b < B + 2:
                    dve.wait_ge(attended, b - 1)
                    norm_sum(dve, chain, n1, b - 2, bank[2 + b % 2][:, 0:D], 1.0 / WS)
                if b >= 3:
                    norm_apply(dve, n1, b - 3)

        def stage1_pool(pool, chain):
            pool.memset(minus_half[:, :], -0.5).then_inc(constant_set, 1)
            pool.wait_ge(constant_set, 1)
            pool.wait_ge(ident_in, 16)
            credits_pool(pool, e0)
            pool.wait_ge(ctx_rev_in, 16)
            for h in range(KV_AT_ONCE):
                if h == KVH:
                    pool.wait_ge(xt_low, DH)
                    pool.wait_ge(w1_low, 3)
                conv_products_pool(pool, h)
            for j in range(1, 2 * H, 2):
                prob_low(pool, j)
            for th in range(2):
                pool.wait_ge(squares_summed, 4 * th + 4)
                v = slice(4 * th, 4 * th + 4)
                chain.link(pool.tensor_scalar(ssq[:, v], ssq[:, v], 1.0 / D, RMS_EPS, ALU.mult, ALU.add))
                pool.tensor_tensor(rms[:, v], ssq[:, v], minus_half[:, 0:4], ALU.pow).then_inc(rms_done, 1)
            for b in range(B):
                norm_rstd(pool, chain, n1, b)
        conv = Region()
        filtering = Region(0, arena2)
        KVH = H // 2
        KV_AT_ONCE = KVH + 5
        ctxr = filtering("ctxr", [P, DH, P, B])
        toep = filtering("toep", [P, H, 2 * P])
        dvec = sb("dvec", [P, H])
        anti = sb("anti", [P, P])
        kv = filtering("kv", [P, KVH, DH, CJ * CJ * B])
        kv_more = Region(split_first)("kv_more", [P, KV_AT_ONCE - KVH, DH, CJ * CJ * B])

        def products(h):
            h %= KV_AT_ONCE
            return kv[:, h, :, :] if h < KVH else kv_more[:, h - KVH, :, :]

        qc = conv("qc", [P, DH, P, B])
        pr = conv("pr", [P, 3, DH, CJ, CJ * B])
        pr4 = conv("pr4", [P, 3, DH, CJ // 2, CJ * B])
        pr2 = conv("pr2", [P, 2, DH, CJ // 4, CJ * B])
        convT = conv("convT", [P, DH, B, P])

        ctx_rev_in = sem("ctx_rev_in")
        filters_in = sem("filters_in")
        filter_ready = sem("filter_ready")
        products_ready = sem("products_ready")
        convolved = sem("convolved")
        queried = sem("queried")
        folded_once = sem("folded_once")
        head_done = sem("head_done")
        conv_turned = sem("conv_turned")
        n2 = Norm(2, 1, 0)

        def stage2_sp(sp):
            sp.dma_start(ctxr[:, :, :, :], ins["ctx_rev"].rearrange("p (d s b) -> p d s b", d=DH, b=B)).then_inc(ctx_rev_in, 16)
            filters = bass.AP(ins["filters"].tensor, 0, [[1, P], [3 * P - 1, H], [1, 2 * P]])
            sp.dma_start(toep[:, :, :], filters).then_inc(filters_in, 16)
            sp.dma_start(dvec[:, :], ins["conv_d"].partition_broadcast(P)).then_inc(filters_in, 16)
            sp.dma_start(anti[:, :], ins["c_anti"]).then_inc(filters_in, 16)

        def conv_products_pool(pool, h):
            for d in range(DH):
                if h >= KV_AT_ONCE:
                    pool.wait_ge(convolved, 2 * (h - KV_AT_ONCE) + 2)
                c = ctxr[:, d, h * CJ:(h + 1) * CJ, :]
                pool.tensor_tensor(products(h)[:, d, :].rearrange("p (i j b) -> p i j b", i=CJ, j=CJ),
                                   c[:, :, None, :].broadcast_to([P, CJ, CJ, B]),
                                   c[:, None, :, :].broadcast_to([P, CJ, CJ, B]), ALU.mult).then_inc(products_ready, 1)

        def conv_filters_dve(dve, heads):
            dve.wait_ge(filters_in, 48)
            for h in heads:
                dve.scalar_tensor_tensor(out=toep[:, h, 0:P], in0=anti[:, :], scalar=dvec[:, h:h + 1],
                                         in1=toep[:, h, 0:P], op0=ALU.mult, op1=ALU.add).then_inc(filter_ready, 1)

        def stage2_pe(pe):
            pe.wait_ge(filter_ready, H)
            for h in range(H):
                pe.wait_ge(products_ready, 2 * h + 2)
                for d in range(DH):
                    u = 2 * h + d
                    if u >= 4:
                        pe.wait_ge(queried, u - 3)
                    if d:
                        pe.matmul(bank[u % 4][:, :], toep[:, h, P:2 * P], products(h)[:, 0, :], start=True, stop=False)
                    pe.matmul(bank[u % 4][:, :], toep[:, h, 0:P], products(h)[:, d, :], start=not d, stop=True).then_inc(convolved, 1)
            pe.wait_ge(head_done, H)
            for b in range(B):
                if b >= 2:
                    pe.wait_ge(done.sum, n2.sum + b - 1)
                for d in range(DH):
                    mm = pe.transpose(bank[4 + b % 2][:, d * P:(d + 1) * P], convT[:, d, b, :], ident[:, :])
                mm.then_inc(conv_turned, 1)
            for p in range(4):
                norm_transpose(pe, n2, p)

        def stage2_act(act):
            for p in range(4):
                act.wait_ge(done.t, n1.t + p + 1)
                act.activation(qc[:, :, :, 2 * p:2 * p + 2].rearrange("q d t b -> q d b t"),
                               bank[6 + p % 2][:, :].rearrange("q (d b t) -> q d b t", d=DH, b=2),
                               ACT.Copy).then_inc(done.lo, 1)
            gate_act(act, e0)
            for p in range(4):
                if p == 1:
                    shared_high_act(act)
                norm_hi(act, n2, p)

        def stage2_dve(dve, chain):
            dve.wait_ge(done.lo, n1.lo + 4)

            def fold(h):
                dve.wait_ge(folded_once, h + 1)
                chain.link(dve.tensor_tensor(pr2[:, h % 2, :, :, :], pr4[:, h % 3, :, 0:2, :], pr4[:, h % 3, :, 2:4, :], ALU.add))
                dve.tensor_tensor(convT[:, :, :, h * CJ:(h + 1) * CJ].rearrange("p d b j -> p d j b"),
                                  pr2[:, h % 2, :, 0, :].rearrange("p d (j b) -> p d j b", b=B),
                                  pr2[:, h % 2, :, 1, :].rearrange("p d (j b) -> p d j b", b=B), ALU.add).then_inc(head_done, 1)

            for h in range(H + 2):
                if h < H:
                    if h >= 3:
                        dve.wait_ge(folded_once, h - 2)
                    for d in range(DH):
                        u = 2 * h + d
                        dve.wait_ge(convolved, u + 1)
                        dve.tensor_tensor(pr[:, h % 3, d, :, :].rearrange("p i (j b) -> p i j b", b=B),
                                          bank[u % 4][:, :].rearrange("p (i j b) -> p i j b", i=CJ, j=CJ),
                                          qc[:, d, h * CJ:(h + 1) * CJ, None, :].broadcast_to([P, CJ, CJ, B]),
                                          ALU.mult).then_inc(queried, 1)
                if h >= 2:
                    fold(h - 2)
            gate_dve(dve, e0)
            for b in range(B + 1):
                if b < B:
                    dve.wait_ge(conv_turned, b + 1)
                    norm_sum(dve, chain, n2, b, bank[4 + b % 2][:, 0:D], 1.0)
                if b >= 1:
                    norm_apply(dve, n2, b - 1)
            for p in range(4):
                if p == 2:
                    shared_low_dve(dve)
                norm_lo(dve, n2, p)

        def stage2_pool(pool, chain):
            for h in range(H):
                pool.wait_ge(queried, 2 * h + 2)
                if h >= 3:
                    pool.wait_ge(head_done, h - 2)
                pool.tensor_tensor(pr4[:, h % 3, :, :, :], pr[:, h % 3, :, 0:4, :], pr[:, h % 3, :, 4:8, :],
                                   ALU.add).then_inc(folded_once, 1)
                if h < H - KV_AT_ONCE:
                    conv_products_pool(pool, h + KV_AT_ONCE)
            for b in range(B):
                norm_rstd(pool, chain, n2, b)

        acc = sb("acc", [P, B, D])
        identh = sb("identh", [P, P], F16)
        before = sb("before", [P, P], F16)
        onesh = sb("onesh", [P, P], F16)
        before_f = Region(ARENA - P)("before_f", [P, P])
        iota = sb("iota", [P, IOTA])
        iotah = sb("iotah", [P, IOTA], F16)
        tokens = sb("tokens", [P, B])
        kth = sb("kth", [P, 8])
        waits_taken = sem("waits_taken")
        tables3_in = sem("tables3_in")
        tables3_half = sem("tables3_half")

        rows = nc.dram_tensor("token_rows", [T, 2 * D], F16).ap()

        routing_counts = {"gate_in": 16, "gate_high": 1, "gate_low": 1, "logits": B, "logits_read": B, "scaled": 1, "softened": 1,
                          "mask": 1, "rank": 2, "named": 1, "based": 1, "rounds": 1, "rows_high": B, "rows_low": B,
                          "rows": 16 * B, "weighed": B, "summed": B}
        routing = {edge: sem("route_" + edge) for edge in routing_counts if edge != "rows"}
        rows_written = sem("rows_written")

        class Experts:

            def __init__(self, name, region, experts, top, width, gated, places, lead, w_gate, w_up, w_down, earlier):
                self.name, self.E, self.K, self.gated = name, experts, top, gated
                self.lead = lead
                self.C = places
                assert places in (P, P + SHARED)
                self.nt = tiles = -(-places // P)
                self.list_steps = 2 * tiles + tiles
                self.im = width
                self.nk = 1 if gated else 2
                self.NI = experts // 8
                self.max_rounds = -(-T // self.C)
                self.w_gate, self.w_up, self.w_down = w_gate, w_up, w_down
                E, K, C, im, nk = self.E, self.K, self.C, self.im, self.nk
                self.gate_f = region(name + "_gate_f", [P, DH, E])
                self.gate_h = region(name + "_gate_h", [P, DH, E], F16)
                self.gate_l = region(name + "_gate_l", [P, DH, E], F16)
                self.top = region(name + "_top", [P, B, 8])
                self.pick = region(name + "_pick", [P, B, 8], U32)
                self.pickf = region(name + "_pickf", [P, B, 8])
                self.weight = region(name + "_weight", [P, B, 8])
                self.total = region(name + "_total", [P, B])
                self.active = region(name + "_active", [P, B, 8])
                self.cum = region(name + "_cum", [P, B, 8])
                self.one = Region(PICKS, arena2)(name + "_one", [P, B, K, E], F16)
                self.picked = Region(PICKS + B * K * E // 2, arena2)(name + "_picked", [P, B, K, E], F16)
                self.rank = region(name + "_rank", [P, B, K])
                self.mask = region(name + "_mask", [P, B, E], F16)
                self.named = region(name + "_named", [P, B, K, 2, E], F16)
                self.most = region(name + "_most", [P, 16])
                self.rounds = region(name + "_rounds", [P, 2], I32)
                self.place = Region(PICKS + B * K * E // 2, arena2)(name + "_place", [P, 2, K, tiles * P], F16)
                self.list = region(name + "_list", [P, tiles, E], I32)
                self.home = region(name + "_home", [P, tiles, E], I32)
                self.homef = region(name + "_homef", [P, tiles, E])
                self.spare = region(name + "_spare", [P, tiles, E])
                self.fetch = region(name + "_fetch", [P, 2, tiles, 4], I32)
                self.send = region(name + "_send", [P, 2, tiles, 4], I32)
                self.xg = region(name + "_xg", [P, 4, tiles, 2 * D], F16)
                self.xgT = region(name + "_xgT", [P, 2, 4, C], F16)
                self.ring_up = region(name + "_ring_up", [P, 2, 4, DH * 2 * im])
                self.ring_dn = region(name + "_ring_dn", [P, 2, 4, nk * D])
                here = Region(region.at)
                self.up_h = region(name + "_up_h", [P, 4, DH * 2 * im], F16)
                self.up_l = region(name + "_up_l", [P, 4, DH * 2 * im], F16)
                self.dn_h = region(name + "_dn_h", [P, 4, nk * D], F16)
                self.dn_l = region(name + "_dn_l", [P, 4, nk * D], F16)
                self.act = region(name + "_act", [P, 2, (2 if not gated else 1) * C])
                self.hid = region(name + "_hid", [P, 2, C]) if gated else None
                self.hid_h = region(name + "_hid_h", [P, 2, nk * C], F16)
                self.hid_l = region(name + "_hid_l", [P, 2, nk * C], F16)
                self.y = region(name + "_y", [P, 4, tiles, D])
                self.back = (Region() if gated else here)(name + "_back", [P, BACK_SLOTS, K, D])
                self.y_rows = nc.dram_tensor(name + "_y_rows", [K * T + E * tiles * P + 4 * tiles, D], F32).ap()
                edges = ("places_made places_listed lists fetch send turned tiles_copied w_high w_low went_up silu_done "
                         "hid_high hid_low came_down y_copied added").split() + ["factor_read"] * gated
                self.s = routing | {edge: sem(f"{name}_{edge}") for edge in edges}
                self.before = {edge: count * earlier for edge, count in routing_counts.items()}
                if not gated:
                    self.s["factor_read"] = self.s["silu_done"]
                self.rows_written = rows_written
                self.weights_in = [sem(f"{name}_weights_in{i}") for i in range(2)]
                self.fetched = [sem(f"{name}_fetched{i}") for i in range(4)]
                self.sent = [sem(f"{name}_sent{i}") for i in range(4)]
                self.returned = [sem(f"{name}_returned{i}") for i in range(BACK_SLOTS)]

            def fetches(self, x):
                return 2 if self.nt == 2 and x % 2 == 0 else 1

            def sends(self, x):
                return 2 if self.nt == 2 and x % 2 else 1

        def load_pair(sp, m, group, slot, pair):
            two = slice(2 * pair, 2 * pair + 2)
            sp.dma_start(m.ring_up[:, slot, two, :], m.w_up[bass.ds(group, 1), :, two, :].rearrange("g p e n -> p (g e) n")
                         ).then_inc(m.weights_in[slot], 16)
            sp.dma_start(m.ring_dn[0:m.im, slot, two, :], m.w_down[bass.ds(group, 1), :, two, :].rearrange("g p e n -> p (g e) n")
                         ).then_inc(m.weights_in[slot], 16)

        def route_sp(sp, m):
            sp.dma_start(m.gate_f[:, :, :], m.w_gate.rearrange("(d p) e -> p d e", p=P)).then_inc(m.s["gate_in"], 16)
            for g in range(2):
                for pair in range(2):
                    load_pair(sp, m, g, g, pair)

        def rows_sp(sp, m):
            for b in range(B):
                sp.wait_ge(m.s["rows_low"], m.before["rows_low"] + b + 1)
                sp.dma_start(rows[b * P:(b + 1) * P, :], row_parts[:, b, :]).then_inc(m.rows_written, 16)

        def rows_act(act, m, n, b):
            act.wait_ge(done.x, n.x + b + 1)
            act.activation(row_parts[:, b, 0:D], X[:, b, :], ACT.Copy).then_inc(m.s["rows_high"], 1)

        def rows_pool(pool, m, b):
            pool.wait_ge(m.s["rows_high"], m.before["rows_high"] + b + 1)
            pool.tensor_tensor(row_parts[:, b, D:2 * D], X[:, b, :], row_parts[:, b, 0:D],
                               ALU.subtract).then_inc(m.s["rows_low"], 1)

        def gate_act(act, m):
            act.wait_ge(m.s["gate_in"], m.before["gate_in"] + 16)
            act.activation(m.gate_h[:, :, :], m.gate_f[:, :, :], ACT.Copy, scale=WS).then_inc(m.s["gate_high"], 1)

        def gate_dve(dve, m):
            dve.wait_ge(m.s["gate_high"], m.before["gate_high"] + 1)
            dve.scalar_tensor_tensor(out=m.gate_l[:, :, :], in0=m.gate_f[:, :, :], scalar=WS, in1=m.gate_h[:, :, :],
                                     op0=ALU.mult, op1=ALU.subtract).then_inc(m.s["gate_low"], 1)

        def logits_pe(pe, m, n, b):
            pe.wait_ge(done.lo, n.lo + b // 2 + 1)
            if b >= 4:
                pe.wait_ge(m.s["logits_read"], m.before["logits_read"] + b - 3)
            k = 0
            for d in range(DH):
                for wp, xp in ((m.gate_h, xTh), (m.gate_l, xTh), (m.gate_h, xTl)):
                    mm = pe.matmul(bank[b % 4][:, 0:m.E], xp[:, d, b * P:(b + 1) * P], wp[:, d, :],
                                   start=(k == 0), stop=(k == 3 * DH - 1))
                    k += 1
            mm.then_inc(m.s["logits"], 1)

        def pick_dve(dve, chain, m, b):
            dve.wait_ge(m.s["logits"], m.before["logits"] + b + 1)
            chain.link(dve.max(m.top[:, b, :], bank[b % 4][:, 0:m.E]))
            dve.max_index(m.pick[:, b, :], m.top[:, b, :], bank[b % 4][:, 0:m.E]).then_inc(m.s["logits_read"], 1)

        def soft_act(act, m):
            act.wait_ge(m.s["scaled"], m.before["scaled"] + 1)
            act.activation(m.weight[:, :, :], m.weight[:, :, :], ACT.Exp, scale=1.0 / WS).then_inc(m.s["softened"], 1)

        def weigh_dve(dve, chain, m, threshold):
            w = m.weight[:, :, 0:m.K]

            dve.wait_ge(m.s["logits_read"], m.before["logits_read"] + B)
            dve.tensor_tensor(m.weight[:, :, :], m.top[:, :, :], m.top[:, :, 0:1].broadcast_to([P, B, 8]),
                              ALU.subtract).then_inc(m.s["scaled"], 1)
            chain.link(dve.tensor_copy(m.pickf[:, :, :], m.pick[:, :, :]))
            chain.link(dve.tensor_scalar(m.pickf[:, :, :], m.pickf[:, :, :], 1.0, None, ALU.add))
            if threshold is not None:
                chain.link(dve.memset(m.active[:, :, :], 1.0))
                chain.link(dve.memset(m.active[:, :, 0:1], 0.0))
            dve.wait_ge(m.s["softened"], m.before["softened"] + 1)
            chain.link(dve.tensor_reduce(m.total[:, :], w, AX.X, ALU.add))
            chain.link(dve.reciprocal(m.total[:, :], m.total[:, :]))
            chain.link(dve.tensor_tensor(w, w, m.total[:, :, None].broadcast_to([P, B, m.K]), ALU.mult))
            if threshold is not None:
                flat = [v[:, :, :].rearrange("p b k -> p (b k)") for v in (m.cum, m.active, m.weight)]
                chain.link(dve.tensor_tensor_scan(flat[0], flat[1], flat[2], 0.0, ALU.mult, ALU.add))
                chain.link(dve.tensor_scalar(m.active[:, :, 1:8], m.cum[:, :, 0:7], threshold, None, ALU.is_lt))
                chain.link(dve.memset(m.active[:, :, 0:1], 1.0))
                chain.link(dve.tensor_tensor(m.pickf[:, :, :], m.pickf[:, :, :], m.active[:, :, :], ALU.mult))
                chain.link(dve.tensor_tensor(w, w, m.active[:, :, :], ALU.mult))
            chain.link(dve.tensor_tensor(m.one[:, :, :, :], m.pickf[:, :, 0:m.K, None].broadcast_to([P, B, m.K, m.E]),
                                         iota[:, None, None, 1:m.E + 1].broadcast_to([P, B, m.K, m.E]), ALU.is_equal))
            with nc.allow_low_precision(reason="a pick is 0 or 1"):
                dve.tensor_reduce(m.mask[:, :, :], m.one[:, :, :, :].rearrange("p b k e -> p b e k"), AX.X, ALU.add
                                  ).then_inc(m.s["mask"], 1)

        def name_pool(pool, m):
            pool.wait_ge(m.s["mask"], m.before["mask"] + 1)
            pool.tensor_tensor(m.named[:, :, :, 0, :], m.one[:, :, :, :], tokens[:, :, None, None].broadcast_to([P, B, m.K, m.E]),
                               ALU.mult).then_inc(m.s["named"], 1)

        def base(engine, m):
            engine.wait_ge(m.s["mask"], m.before["mask"] + 1)
            engine.tensor_tensor(m.named[:, :, :, 1, :], m.one[:, :, :, :], kth[:, None, 0:m.K, None].broadcast_to([P, B, m.K, m.E]),
                                 ALU.mult).then_inc(m.s["based"], 1)

        def rank_pe(pe, m):
            pe.wait_ge(m.s["mask"], m.before["mask"] + 1)
            for b in range(B):
                for i in range(b + 1):
                    mm = pe.matmul(bank[2][:, b * m.E:(b + 1) * m.E], (before if i == b else onesh)[:, :], m.mask[:, i, :],
                                   start=(i == 0), stop=(i == b))
            mm.then_inc(m.s["rank"], 1)
            for i in range(B):
                mm = pe.matmul(bank[3][:, 0:m.E], onesh[:, :], m.mask[:, i, :], start=(i == 0), stop=(i == B - 1))
            mm.then_inc(m.s["rank"], 1)

        def rank_dve(dve, chain, m, threshold):
            dve.wait_ge(m.s["rank"], m.before["rank"] + 1)
            chain.link(dve.tensor_tensor(m.picked[:, :, :, :], m.one[:, :, :, :],
                                         bank[2][:, 0:B * m.E].rearrange("p (b o e) -> p b o e", b=B, o=1).broadcast_to([P, B, m.K, m.E]),
                                         ALU.mult))
            chain.link(dve.tensor_reduce(m.rank[:, :, :], m.picked[:, :, :, :], AX.X, ALU.add))
            if threshold is not None:
                chain.link(dve.tensor_scalar(m.cum[:, :, :], m.active[:, :, :], -4.0 * T, 4.0 * T, ALU.mult, ALU.add))
                chain.link(dve.tensor_tensor(m.rank[:, :, :], m.rank[:, :, :], m.cum[:, :, :], ALU.add))
                w = m.weight[:, :, 0:m.K]
                chain.link(dve.tensor_reduce(m.total[:, :], w, AX.X, ALU.add))
                chain.link(dve.reciprocal(m.total[:, :], m.total[:, :]))
                chain.link(dve.tensor_tensor(w, w, m.total[:, :, None].broadcast_to([P, B, m.K]), ALU.mult))

        def rounds_dve(dve, chain, m):
            dve.wait_ge(m.s["rank"], m.before["rank"] + 2)
            n = m.max_rounds - 1
            chain.link(dve.tensor_reduce(m.most[:, 0:1], bank[3][:, 0:m.E], AX.X, ALU.max))
            chain.link(dve.tensor_scalar(m.most[:, 1:1 + n], iota[:, 1:1 + n], float(m.C), None, ALU.mult))
            chain.link(dve.tensor_scalar(m.most[:, 1:1 + n], m.most[:, 1:1 + n], m.most[:, 0:1], None, ALU.is_lt))
            chain.link(dve.tensor_reduce(m.most[:, 9:10], m.most[:, 1:1 + n], AX.X, ALU.add))
            dve.tensor_scalar(m.rounds[:, 0:1], m.most[:, 9:10], 1.0, None, ALU.add).then_inc(m.s["rounds"], 1)

        def spare_dve(dve, chain, m):
            for i in range(m.nt):
                chain.link(dve.tensor_scalar(m.spare[:, i, :], iota[:, 0:m.E], float(m.nt * P), float(m.K * T + i * P),
                                             ALU.mult, ALU.add))
                chain.link(dve.tensor_scalar(m.spare[:, i, :], m.spare[:, i, :], tokens[:, 0:1], None, ALU.add))

        def read_rounds(engine, m):
            engine.wait_ge(m.s["rounds"], m.before["rounds"] + 1)
            return engine.value_load(m.rounds[0:1, 0:1], min_val=1, max_val=m.max_rounds)

        def lists_dve(dve, m, r):
            ranks = m.rank.rearrange("p b k -> p (b k)")
            for b in range(B):
                dve.wait_ge(m.s["places_listed"], r * B + (b + 1))
                for k in range(m.K):
                    mm = dve.tensor_scalar(m.place[:, b % 2, k, :], iotah[:, 0:m.nt * P], m.rank[:, b, k:k + 1], None,
                                           ALU.is_equal)
                mm.then_inc(m.s["places_made"], 1)
            dve.wait_ge(m.s["places_listed"], r * B + (B + 2))
            dve.wait_ge(m.s["send"], r * (2 * m.NI) + 1)
            step = [0]

            def then(ins):
                step[0] += 1
                ins.then_inc(m.s["lists"], 1)
                dve.wait_ge(m.s["lists"], r * m.list_steps + step[0])

            for i in range(m.nt):
                token, pick = bank[6 + i][:, 0:m.E], bank[6 + i][:, m.E:2 * m.E]
                home = m.homef[:, i, :]
                dve.tensor_scalar(m.list[:, i, :], token, -1.0, 0.0, ALU.add, ALU.max)
                then(dve.scalar_tensor_tensor(out=home, in0=token, scalar=0.0, in1=m.spare[:, i, :],
                                              op0=ALU.is_equal, op1=ALU.mult))
                then(dve.tensor_tensor(home, home, pick, ALU.add))
                mm = dve.scalar_tensor_tensor(out=m.home[:, i, :], in0=token, scalar=-1.0, in1=home, op0=ALU.add, op1=ALU.add)
                if i == 1:
                    then(mm)
                    up, near, far = slice(SHARED, P), slice(0, m.E - 1), slice(1, m.E)
                    dve.tensor_scalar(m.list[up, i, near], token[up, far], -1.0, 0.0, ALU.add, ALU.max)
                    dve.scalar_tensor_tensor(out=m.home[up, i, near], in0=token[up, far], scalar=-1.0,
                                             in1=home[up, far], op0=ALU.add, op1=ALU.add)
            then(dve.tensor_scalar(ranks, ranks, -float(m.C), None, ALU.add))

        def lists_pe(pe, m, r):
            pe.wait_ge(m.s["named"], m.before["named"] + 1)
            pe.wait_ge(m.s["based"], m.before["based"] + 1)
            for b in range(B):
                pe.wait_ge(m.s["places_made"], r * B + (b + 1))
                for k in range(m.K):
                    for i in range(m.nt):
                        mm = pe.matmul(bank[6 + i][:, 0:2 * m.E], m.place[:, b % 2, k, i * P:(i + 1) * P],
                                       m.named[:, b, k, :, :], start=(b == 0 and k == 0), stop=(b == B - 1 and k == m.K - 1))
                mm.then_inc(m.s["places_listed"], 1)

        def experts_loop(engine, m, r, step):
            with engine.Fori(0, m.NI - 1) as it:
                for j in range(8):
                    step(r * m.E + it * 8, it, r * m.NI + it, j, True)
            for j in range(8):
                step(r * m.E + (m.NI - 1) * 8, m.NI - 1, r * m.NI + (m.NI - 1), j, False)

        def ring_turn(turn, x):
            return 64 * turn + 64 * (x // 8 + 1)

        def plain(pool):
            pool.sem_inc(waits_taken, 1)

        def round_pool(pool, m, r):
            AHEAD = 6
            pool.wait_ge(m.s["lists"], r * m.list_steps + m.list_steps)
            plain(pool)

            def columns(dst, src, edge, turn, it, x):
                pool.tensor_copy(dst[:, x // 4 % 2, :, :], src[:, :, bass.ds(it * 8 + x, 4)]).then_inc(m.s[edge], 1)
                pool.wait_ge(m.s[edge], turn * 2 + (x // 4 + 2))
                plain(pool)

            def fetch(n, it, turn, x):
                pool.wait_ge(m.s["turned"], n + (x + (2 if m.nt == 2 and x % 2 == 0 else 1)))
                plain(pool)
                if x % 4 == 0:
                    columns(m.fetch, m.list, "fetch", turn, it, x)
                for i in range(m.fetches(x)):
                    pool.indirect_dma_start(out=m.xg[:, x % 4, i, :], out_offset=None, in_=rows,
                                            in_offset=bass.IndirectOffsetOnAxis(
                                                ap=m.fetch[:, x // 4 % 2, i, x % 4:x % 4 + 1], axis=0)
                                            ).then_inc(m.fetched[x % 4], 16)

            def send(n, it, turn, x):
                pool.wait_ge(m.s["y_copied"], n + (x + 5))
                plain(pool)
                if x % 4 == 0:
                    columns(m.send, m.home, "send", turn, it, x)
                for i in range(m.sends(x)):
                    y = x - i
                    pool.indirect_dma_start(out=m.y_rows, out_offset=bass.IndirectOffsetOnAxis(
                        ap=m.send[:, y // 4 % 2, i, y % 4:y % 4 + 1], axis=0),
                        in_=m.y[:, y % 4, i, :], in_offset=None).then_inc(m.sent[x % 4], 16)

            def step(n, it, turn, j, more):
                if more or j + AHEAD < 8:
                    fetch(n, it, turn, j + AHEAD)
                send(n, it, turn, j)

            for x in range(AHEAD):
                fetch(r * m.E, 0, r * m.NI, x)
            experts_loop(pool, m, r, step)

        def round_pe(pe, m, r):
            def turn_tiles(n, turn, x):
                pe.wait_ge(m.fetched[x % 4], 32 * m.fetches(x) * turn + 16 * m.fetches(x) * (x // 4 + 1))
                pe.wait_ge(m.s["tiles_copied"], n + (x + 1))
                v = bank[x % 2][:, :].bitcast(F16)
                for c in range(4):
                    mm = pe.transpose(v[:, c * m.C:c * m.C + P], m.xg[:, x % 4, 0, c * P:(c + 1) * P], identh[:, :])
                    if m.nt == 2:
                        mine = slice(SHARED * (x % 2), SHARED * (x % 2) + SHARED)
                        mm = pe.transpose(v[:, c * m.C + P:(c + 1) * m.C], m.xg[mine, x // 2 * 2 % 4, 1, c * P:(c + 1) * P],
                                          identh[mine, mine])
                mm.then_inc(m.s["turned"], 1)

            def up(n, x):
                pe.wait_ge(m.s["tiles_copied"], n + (x + 3))
                pe.wait_ge(m.s["w_low"], n + (x + 1))
                pe.wait_ge(m.s["factor_read"], n + (x + 1))
                for i in range(2):
                    k = 0
                    for d in range(DH):
                        c0 = d * 2 * m.im + i * m.im
                        for wp, xp in ((m.up_h, d), (m.up_l, d), (m.up_h, 2 + d)):
                            mm = pe.matmul(bank[2 + x % 2][0:m.im, i * m.C:(i + 1) * m.C], wp[:, x % 4, c0:c0 + m.im],
                                           m.xgT[:, x % 2, xp, :], start=(k == 0), stop=(k == 3 * DH - 1))
                            k += 1
                mm.then_inc(m.s["went_up"], 1)

            def down(n, x):
                pe.wait_ge(m.s["hid_low"], n + (x + 3))
                pe.wait_ge(m.s["y_copied"], n + (x + 3))
                lots = ((0, P),) + (((P, SHARED), (P - SHARED, P))[x % 2],) * (m.nt - 1)
                for i, (first, count) in enumerate(lots):
                    k = 0
                    for t in range(m.nk):
                        c0 = t * m.C + first
                        for wp, hp in ((m.dn_h, m.hid_h), (m.dn_l, m.hid_h), (m.dn_h, m.hid_l)):
                            mm = pe.matmul(bank[4 + x % 2][0:count, i * D:(i + 1) * D], hp[0:m.im, x % 2, c0:c0 + count],
                                           wp[0:m.im, x % 4, t * D:(t + 1) * D], start=(k == 0), stop=(k == 3 * m.nk - 1))
                            k += 1
                mm.then_inc(m.s["came_down"], 1)

            def step(n, it, turn, j, more):
                if more or j + 3 < 8:
                    turn_tiles(n, turn, j + 3)
                if more or j + 2 < 8:
                    up(n, j + 2)
                down(n, j)

            for x in range(3):
                turn_tiles(r * m.E, r * m.NI, x)
            for x in range(2):
                up(r * m.E, x)
            experts_loop(pe, m, r, step)

        def round_act(act, m, r):
            def split_high(n, turn, x):
                act.wait_ge(m.weights_in[x // 4 % 2], ring_turn(turn, x))
                act.wait_ge(m.s["went_up"], n + (x + 1))
                act.activation(m.up_h[:, x % 4, :], m.ring_up[:, x // 4 % 2, x % 4, :], ACT.Copy, scale=WS)
                act.wait_ge(m.s["came_down"], n + (x + 1))
                act.activation(m.dn_h[0:m.im, x % 4, :], m.ring_dn[0:m.im, x // 4 % 2, x % 4, :], ACT.Copy, scale=WS
                               ).then_inc(m.s["w_high"], 1)

            def copy_tiles(n, x):
                act.wait_ge(m.s["went_up"], n + (x + 3))
                act.wait_ge(m.s["turned"], n + (x + 5))
                v = bank[x % 2][:, :].bitcast(F16)[:, 0:4 * m.C]
                act.activation(m.xgT[:, x % 2, :, :].rearrange("p c t -> p (c t)"), v, ACT.Copy).then_inc(m.s["tiles_copied"], 1)

            def silu(n, x):
                act.wait_ge(m.s["went_up"], n + (x + 5))
                act.wait_ge(m.s["hid_low"], n + (x + 1))
                w = (1 if m.gated else 2) * m.C
                act.activation(m.act[0:m.im, x % 2, :], bank[2 + x % 2][0:m.im, 0:w], ACT.Silu, scale=1.0 / WS
                               ).then_inc(m.s["silu_done"], 1)

            def step(n, it, turn, j, more):
                if more or j + 1 < 8:
                    silu(n, j + 1)
                if more or j + 3 < 8:
                    split_high(n, turn, j + 3)
                    copy_tiles(n, j + 3)

            for x in range(3):
                split_high(r * m.E, r * m.NI, x)
                if x < 2:
                    copy_tiles(r * m.E, x)
            silu(r * m.E, 0)
            copy_tiles(r * m.E, 2)
            experts_loop(act, m, r, step)

        def round_dve(dve, m, r):
            def split_low(n, x):
                dve.wait_ge(m.s["w_high"], n + (x + 1))
                dve.scalar_tensor_tensor(out=m.up_l[:, x % 4, :], in0=m.ring_up[:, x // 4 % 2, x % 4, :], scalar=WS,
                                         in1=m.up_h[:, x % 4, :], op0=ALU.mult, op1=ALU.subtract)
                dve.scalar_tensor_tensor(out=m.dn_l[0:m.im, x % 4, :], in0=m.ring_dn[0:m.im, x // 4 % 2, x % 4, :], scalar=WS,
                                         in1=m.dn_h[0:m.im, x % 4, :], op0=ALU.mult, op1=ALU.subtract).then_inc(m.s["w_low"], 1)

            def hidden(n, x):
                dve.wait_ge(m.s["silu_done"], n + (x + 3))
                dve.wait_ge(m.s["came_down"], n + (x + 3))
                if m.gated:
                    dve.scalar_tensor_tensor(out=m.hid[0:m.im, x % 2, :], in0=bank[2 + x % 2][0:m.im, m.C:2 * m.C], scalar=1.0 / WS,
                                             in1=m.act[0:m.im, x % 2, :], op0=ALU.mult, op1=ALU.mult).then_inc(m.s["factor_read"], 1)
                    dve.wait_ge(m.s["factor_read"], n + (x + 3))
                    h = m.hid
                else:
                    h = m.act
                dve.tensor_copy(m.hid_h[0:m.im, x % 2, :], h[0:m.im, x % 2, :]).then_inc(m.s["hid_high"], 1)
                dve.wait_ge(m.s["hid_high"], n + (x + 1))
                dve.tensor_tensor(m.hid_l[0:m.im, x % 2, :], h[0:m.im, x % 2, :], m.hid_h[0:m.im, x % 2, :],
                                  ALU.subtract).then_inc(m.s["hid_low"], 1)

            def rows_down(n, turn, x):
                dve.wait_ge(m.s["came_down"], n + (x + 5))
                for slot in {x % 4, x // 2 * 2 % 4 + m.nt - 1} if m.nt == 2 else {x % 4}:
                    dve.wait_ge(m.sent[slot], 32 * m.sends(slot) * turn + 16 * m.sends(slot) * (x // 4 + 1))
                mm = dve.tensor_scalar(m.y[:, x % 4, 0, :], bank[4 + x % 2][:, 0:D], 1.0 / WS, None, ALU.mult)
                if m.nt == 2:
                    mine = slice(SHARED * (x % 2), SHARED * (x % 2) + SHARED)
                    mm = dve.tensor_scalar(m.y[mine, x // 2 * 2 % 4, 1, :], bank[4 + x % 2][mine, D:2 * D], 1.0 / WS, None, ALU.mult)
                mm.then_inc(m.s["y_copied"], 1)

            def step(n, it, turn, j, more):
                if more or j + 1 < 8:
                    hidden(n, j + 1)
                if more or j + 3 < 8:
                    split_low(n, j + 3)
                rows_down(n, turn, j)

            for x in range(3):
                split_low(r * m.E, x)
            hidden(r * m.E, 0)
            experts_loop(dve, m, r, step)

        def gather_sp(sp, m, rounds, meanwhile=None):
            for i in range(4):
                sp.wait_ge(m.sent[i], rounds * (16 * m.sends(i) * m.E // 4) + 16 * m.sends(i))
            for b in range(B):
                if b == SPLIT_FROM + 1 and meanwhile is not None:
                    meanwhile(sp)
                if b >= BACK_SLOTS:
                    sp.wait_ge(m.s["added"], (m.lead + 1) * (b - BACK_SLOTS) + m.lead - (1 if b > BACK_SLOTS else 0))
                    sp.wait_ge(m.s["summed"], m.before["summed"] + b - BACK_SLOTS + 1)
                sp.dma_start(m.back[:, b % BACK_SLOTS, :, :], m.y_rows[0:m.K * T, :].rearrange("(k t p) d -> p t k d", k=m.K, p=P)[:, b, :, :]
                             ).then_inc(m.returned[b % BACK_SLOTS], 16)

        def added(m, b):
            return (m.lead + 1) * (b + 1) + (m.lead if b < B - 1 else 0)

        def gather_act(act, m, b):
            act.wait_ge(m.returned[b % BACK_SLOTS], 16 * (b // BACK_SLOTS + 1))
            for k in range(m.lead, m.K):
                mm = act.activation(m.back[:, b % BACK_SLOTS, k, :], m.back[:, b % BACK_SLOTS, k, :], ACT.Copy, scale=m.weight[:, b, k:k + 1])
            mm.then_inc(m.s["weighed"], 1)

        def gather_pe(pe, m, b):
            pe.wait_ge(m.s["weighed"], m.before["weighed"] + b + 1)
            if b >= 2:
                pe.wait_ge(m.s["added"], added(m, b - 2))
            for k in range(m.lead, m.K):
                mm = pe.matmul(bank[2 + b % 2][:, 0:D], ident[:, :], m.back[:, b % BACK_SLOTS, k, :],
                               start=(k == m.lead), stop=(k == m.K - 1))
            mm.then_inc(m.s["summed"], 1)

        def gather_dve(dve, m, b):
            dve.wait_ge(m.returned[b % BACK_SLOTS], 16 * (b // BACK_SLOTS + 1))
            for k in range(m.lead):
                count = (m.lead + 1) * b + k - (1 if b else 0)
                if k:
                    dve.wait_ge(m.s["added"], count)
                dve.scalar_tensor_tensor(out=acc[:, b, :], in0=m.back[:, b % BACK_SLOTS, k, :], scalar=m.weight[:, b, k:k + 1],
                                         in1=acc[:, b, :], op0=ALU.mult, op1=ALU.add).then_inc(m.s["added"], 1)

        def gather_rest_dve(dve, m, b):
            dve.wait_ge(m.s["summed"], m.before["summed"] + b + 1)
            dve.wait_ge(m.s["added"], added(m, b) - 1)
            dve.tensor_tensor(acc[:, b, :], acc[:, b, :], bank[2 + b % 2][:, 0:D], ALU.add).then_inc(m.s["added"], 1)
            dve.wait_ge(m.s["added"], added(m, b))

        def norm_all_dve(dve, chain, n, m, transposed, meanwhile=None):
            for b in range(B + 3):
                if b < B:
                    gather_dve(dve, m, b)
                if 1 <= b < B + 1:
                    gather_rest_dve(dve, m, b - 1)
                    norm_stats(dve, chain, n, b - 1, acc[:, b - 1, :])
                if meanwhile is not None and b > SPLIT_FROM:
                    meanwhile(dve, b - SPLIT_FROM - 1)
                if 2 <= b < B + 2:
                    norm_apply(dve, n, b - 2, acc[:, b - 2, :])
                if transposed and b >= 4 and b % 2 == 0:
                    norm_lo(dve, n, b // 2 - 2)

        def norm_all_act(act, n, m, transposed, meanwhile=None):
            for b in range(B + 3):
                if b < B:
                    gather_act(act, m, b)
                if b == SPLIT_FROM and meanwhile is not None:
                    meanwhile(act)
                if transposed and b >= 4 and b % 2 == 0:
                    norm_hi(act, n, b // 2 - 2)

        def norm_all_pe(pe, n, m, transposed):
            for b in range(B):
                gather_pe(pe, m, b)
                if transposed and b >= 3 and b % 2:
                    norm_transpose(pe, n, b // 2 - 1)
            if transposed:
                norm_transpose(pe, n, B // 2 - 1)

        def norm_all_pool(pool, chain, n):
            for b in range(B):
                norm_rstd(pool, chain, n, b)

        def round_sp(sp, m, r):
            def step(n, it, turn, j, more):
                if j % 2:
                    sp.wait_ge(m.s["w_low"], n + j + 1)
                    load_pair(sp, m, (it * 2 + 2 + j // 4) if more else j // 4, j // 4, j // 2 % 2)

            experts_loop(sp, m, r, step)

        def credits_sp(sp, m):
            for edge, free in (("turned", 4), ("tiles_copied", 2), ("went_up", 4), ("came_down", 4), ("hid_low", 2),
                               ("silu_done", 2), ("y_copied", 4), ("places_listed", 2), ("send", 1), ("fetch", 1)):
                sp.sem_inc(m.s[edge], free)
            if m.gated:
                sp.sem_inc(m.s["factor_read"], 2)

        def credits_pool(pool, m):
            row = m.K * T + m.E * m.nt * P
            for q in range(4 * m.nt):
                if q // 4 < m.sends(q):
                    pool.dma_start(m.y_rows[row + q:row + q + 1, 0:P], ident[0:1, :]).then_inc(m.sent[q % 4], 16)

        second = Region(CONV_WORDS)
        e0 = Experts("e0", second, 64, 6, 88, False, P, 2, ins["gate0"], ins["up0"], ins["down0"], 0)
        row_parts = sb("row_parts", [P, B, 2 * D], F16)
        shared = Region(0, arena2)
        SW = 352
        SI = SW // 4
        sg_f = shared("sg_f", [P, DH, 2 * SW])
        sg_h = shared("sg_h", [P, DH, 2 * SW], F16)
        sg_l = shared("sg_l", [P, DH, 2 * SW], F16)
        sd_f = shared("sd_f", [P, 4, D])
        sd_h = shared("sd_h", [P, 4, D], F16)
        sd_l = shared("sd_l", [P, 4, D], F16)
        sact = shared("sact", [P, 2, HALF])
        sup = shared("sup", [P, 2, HALF])
        shid_h = shared("shid_h", [P, B, HALF], F16)
        shid_l = shared("shid_l", [P, B, HALF], F16)
        shared_up_done = sem("shared_up_done")
        shared_active = sem("shared_active")
        shared_hidden = sem("shared_hidden")
        shared_hidden_high = sem("shared_hidden_high")
        shared_hidden_low = sem("shared_hidden_low")
        y_ready = sem("y_ready")
        acc_ready = sem("acc_ready")
        n3 = Norm(3, 2, 1)

        def stage3_sp(sp):
            sp.dma_start(iota[:, :], ins["c_iota"].partition_broadcast(P)).then_inc(tables3_in, 16)
            sp.dma_start(tokens[:, :], ins["c_tokens"]).then_inc(tables3_in, 16)
            sp.dma_start(kth[:, :], ins["c_pick_rows"].partition_broadcast(P)).then_inc(tables3_in, 16)
            credits_sp(sp, e0)
            sp.wait_ge(done.x, n1.x + B)
            route_sp(sp, e0)
            sp.wait_ge(head_done, H)
            sp.dma_start(before_f[:, :], ins["c_before"]).then_inc(tables3_in, 16)
            sp.dma_start(sg_f[:, :, :], ins["shared_up"].rearrange("(d p) n -> p d n", p=P)).then_inc(weights_in, 16)
            sp.dma_start(sd_f[0:SI, :, :], ins["shared_down"].rearrange("(t p) n -> p t n", p=SI)).then_inc(weights_in, 16)
            rows_sp(sp, e0)
            stage5_loads_sp(sp)
            rounds = read_rounds(sp, e0)
            with sp.Fori(0, rounds) as r:
                round_sp(sp, e0, r)
            gather_sp(sp, e0, rounds, stage4_loads_sp)
            for i in range(2):
                sp.wait_ge(e0.weights_in[i], rounds * (64 * e0.NI) + 64)

        def shared_high_act(act):
            act.wait_ge(weights_in, 16 + 32)
            act.activation(sg_h[:, :, :], sg_f[:, :, :], ACT.Copy, scale=WS).then_inc(weights_high, 1)
            act.activation(sd_h[0:SI, :, :], sd_f[0:SI, :, :], ACT.Copy, scale=WS).then_inc(weights_high, 1)

        def shared_low_dve(dve):
            dve.wait_ge(weights_high, 1 + 2)
            dve.scalar_tensor_tensor(out=sg_l[:, :, :], in0=sg_f[:, :, :], scalar=WS, in1=sg_h[:, :, :],
                                     op0=ALU.mult, op1=ALU.subtract).then_inc(weights_low, 1)
            dve.scalar_tensor_tensor(out=sd_l[0:SI, :, :], in0=sd_f[0:SI, :, :], scalar=WS, in1=sd_h[0:SI, :, :],
                                     op0=ALU.mult, op1=ALU.subtract).then_inc(weights_low, 1)

        def stage3_act(act):
            act.wait_ge(tables3_in, 64)
            act.activation(before[:, :], before_f[:, :], ACT.Copy).then_inc(tables3_half, 1)
            act.activation(identh[:, :], ident[:, :], ACT.Copy).then_inc(tables3_half, 1)
            act.activation(iotah[:, :], iota[:, :], ACT.Copy).then_inc(tables3_half, 1)
            for b in range(B):
                rows_act(act, e0, n2, b)
            soft_act(act, e0)
            for b in range(B + 1):
                if b < B:
                    act.wait_ge(shared_up_done, b + 1)
                    if b >= 2:
                        act.wait_ge(shared_hidden_low, b - 1)
                    act.activation(sact[0:SI, b % 2, :], bank[4 + 2 * (b % 2)][0:SI, :], ACT.Silu, scale=1.0 / WS)
                    act.activation(sup[0:SI, b % 2, :], bank[5 + 2 * (b % 2)][0:SI, :], ACT.Copy, scale=1.0 / WS
                                   ).then_inc(shared_active, 1)
                if b >= 1:
                    act.wait_ge(shared_hidden, b)
                    act.activation(shid_h[0:SI, b - 1, :], sact[0:SI, (b - 1) % 2, :], ACT.Copy).then_inc(shared_hidden_high, 1)
            rounds = read_rounds(act, e0)
            with act.Fori(0, rounds) as r:
                round_act(act, e0, r)
            norm_all_act(act, n3, e0, True, split_high_act)

        def shared_product(engine, b):
            engine.wait_ge(shared_active, b + 1)
            engine.tensor_tensor(sact[0:SI, b % 2, :], sact[0:SI, b % 2, :], sup[0:SI, b % 2, :], ALU.mult).then_inc(shared_hidden, 1)

        def shared_low(engine, b):
            engine.wait_ge(shared_hidden_high, b + 1)
            engine.tensor_tensor(shid_l[0:SI, b, :], sact[0:SI, b % 2, :], shid_h[0:SI, b, :], ALU.subtract).then_inc(shared_hidden_low, 1)

        def stage3_dve(dve, chain):
            chain.link(dve.memset(onesh[:, :], 1.0))
            dve.wait_ge(tables3_in, 64)
            dve.wait_ge(tables3_half, 3)
            spare_dve(dve, chain, e0)

            def share_out(b):
                dve.wait_ge(y_ready, b + 1)
                dve.scalar_tensor_tensor(out=acc[:, b, :], in0=bank[b % 2][:, 0:D], scalar=1.0 / WS, in1=X[:, b, :],
                                         op0=ALU.mult, op1=ALU.add).then_inc(acc_ready, 1)

            for b in range(B):
                pick_dve(dve, chain, e0, b)
            weigh_dve(dve, chain, e0, None)

            base(dve, e0)
            rank_dve(dve, chain, e0, None)
            rounds_dve(dve, chain, e0)
            for b in range(4, B + 1):
                if b < B:
                    shared_product(dve, b)
                if b >= 5:
                    shared_low(dve, b - 1)
            rounds = read_rounds(dve, e0)
            with dve.Fori(0, rounds) as r:
                lists_dve(dve, e0, r)
                round_dve(dve, e0, r)
            for b in range(B):
                share_out(b)
                if b < 3:
                    masks_dve(dve, chain, b)
            norm_all_dve(dve, chain, n3, e0, True, split_low_dve)

        def stage3_pe(pe):
            pe.wait_ge(e0.s["gate_low"], e0.before["gate_low"] + 1)
            for b in range(B):
                logits_pe(pe, e0, n2, b)
            pe.wait_ge(weights_low, 1 + 2)
            pe.wait_ge(tables3_half, 3)

            def shared_up(b):
                th, t = b // 4, b % 4
                if b >= 2:
                    pe.wait_ge(shared_active, b - 1)
                for i in range(2):
                    k = 0
                    c0 = i * SW + t * SI
                    for d in range(DH):
                        for wp, xp in ((sg_h, xTh), (sg_l, xTh), (sg_h, xTl)):
                            mm = pe.matmul(bank[4 + 2 * (b % 2) + i][0:SI, :], wp[:, d, c0:c0 + SI],
                                           xp[:, d, th * HALF:(th + 1) * HALF], start=(k == 0), stop=(k == 3 * DH - 1))
                            k += 1
                mm.then_inc(shared_up_done, 1)

            def shared_down(th):
                pe.wait_ge(shared_hidden_low, 4 * th + 4)
                for i in range(4):
                    b = 4 * th + i
                    if b >= 2:
                        pe.wait_ge(acc_ready, b - 1)
                    k = 0
                    for t in range(4):
                        for wp, hp in ((sd_h, shid_h), (sd_l, shid_h), (sd_h, shid_l)):
                            mm = pe.matmul(bank[b % 2][:, 0:D], hp[0:SI, 4 * th + t, i * P:(i + 1) * P], wp[0:SI, t, :],
                                           start=(k == 0), stop=(k == 11))
                            k += 1
                    mm.then_inc(y_ready, 1)

            for b in range(B):
                shared_up(b)
                if b == 3:
                    rank_pe(pe, e0)
            pe.wait_ge(shared_active, B)
            rounds = read_rounds(pe, e0)
            with pe.Fori(0, rounds) as r:
                lists_pe(pe, e0, r)
                round_pe(pe, e0, r)
            shared_down(0)
            shared_down(1)
            norm_all_pe(pe, n3, e0, True)

        def stage3_pool(pool, chain):
            for b in range(B):
                rows_pool(pool, e0, b)
            for b in range(5):
                if b < 4:
                    shared_product(pool, b)
                if b >= 1:
                    shared_low(pool, b - 1)
                if b == 4:
                    name_pool(pool, e0)
            pool.memset(zero[:, :], 0.0).then_inc(constant_set, 1)
            credits_pool(pool, e1)
            pool.wait_ge(e0.rows_written, e0.before["rows"] + 16 * B)
            rounds = read_rounds(pool, e0)
            with pool.Fori(0, rounds) as r:
                round_pool(pool, e0, r)
            norm_all_pool(pool, chain, n3)

        retain = Region(0, arena2)
        r_wf = retain("r_wf", [P, DH, 3, D])
        r_wh = retain("r_wh", [P, DH, 3, D], F16)
        r_wl = retain("r_wl", [P, DH, 3, D], F16)
        turns = retain("turns", [P, 4, P])
        fade = retain("fade", [P, P])
        rqk = retain("rqk", [P, 2, DH, T])
        part = retain("part", [P, 2, 4, HALF])
        att = retain("att", [P, 2, P])
        tables_in = sem("tables_in")
        qk1_product = sem("qk1_product")
        turn_parts = sem("turn_parts")
        turned = sem("turned")
        v_ready = sem("v_ready")
        v_copied = sem("v_copied")
        scores_ready = sem("scores_ready")
        faded = sem("faded")
        n4 = Norm(4, 2, 2)

        def clear_sp(sp):
            sp.wait_ge(constant_set, 2)
            for k in range(e1.K):
                sp.dma_start(e1.y_rows[k * T:(k + 1) * T, :].rearrange("(t p) d -> p t d", p=P),
                             zero[:, None, :].broadcast_to([P, B, D])).then_inc(cleared, 16)

        def stage4_loads_sp(sp):
            sp.wait_ge(acc_ready, B)
            sp.dma_start(r_wf[:, :, :, :], ins["w_qkv1"].rearrange("(d p) (c n) -> p d c n", p=P, c=3)).then_inc(weights_in, 16)
            sp.dma_start(turns[:, :, :], ins["c_turns"].rearrange("c p t -> p c t")).then_inc(tables_in, 16)
            sp.dma_start(fade[:, :], ins["c_fade"]).then_inc(tables_in, 16)

        def split_high_act(act):
            act.wait_ge(weights_in, 16 + 32 + 16)
            act.activation(r_wh[:, :, :, :], r_wf[:, :, :, :], ACT.Copy, scale=WS).then_inc(weights_high, 1)

        def split_low_dve(dve, c):
            if c < 3:
                dve.wait_ge(weights_high, 1 + 2 + 1)
                dve.scalar_tensor_tensor(out=r_wl[:, :, c, :], in0=r_wf[:, :, c, :], scalar=WS, in1=r_wh[:, :, c, :],
                                         op0=ALU.mult, op1=ALU.subtract).then_inc(weights_low, 1)

        def stage4_pe(pe):
            pe.wait_ge(weights_high, 1 + 2 + 1)
            pe.wait_ge(weights_low, 1 + 2 + 3)

            def values(b):
                if b >= 2:
                    pe.wait_ge(v_copied, b - 1)
                k = 0
                for d in range(DH):
                    for wp, xp in ((r_wh, xTh), (r_wl, xTh), (r_wh, xTl)):
                        mm = pe.matmul(bank[4 + b % 2][:, 0:D], xp[:, d, b * P:(b + 1) * P], wp[:, d, 2, :],
                                       start=(k == 0), stop=(k == 3 * DH - 1))
                        k += 1
                mm.then_inc(v_ready, 1)

            for u in range(4):
                th, qk = u // 2, u % 2
                pe.wait_ge(done.lo, n3.lo + 2 * th + 2)
                if u >= 2:
                    pe.wait_ge(turn_parts, 2 * (u - 1))
                for o in range(2):
                    k = 0
                    for d in range(DH):
                        for wp, xp in ((r_wh, xTh), (r_wl, xTh), (r_wh, xTl)):
                            mm = pe.matmul(bank[2 * (u % 2) + o][:, :], wp[:, d, qk, o * P:(o + 1) * P],
                                           xp[:, d, th * HALF:(th + 1) * HALF], start=(k == 0), stop=(k == 3 * DH - 1))
                            k += 1
                mm.then_inc(qk1_product, 1)
                for b in (2 * u, 2 * u + 1) if u < 2 else ():
                    values(b)
            for b in range(4, B):
                values(b)
            pe.wait_ge(turn_parts, 8)

            def scores(b):
                pe.wait_ge(turned, 4 * (b // 4) + 4)
                if b >= 2:
                    pe.wait_ge(faded, b - 1)
                for d in range(DH):
                    mm = pe.matmul(bank[b % 2][:, 0:P], rqk[:, 1, d, b * P:(b + 1) * P], rqk[:, 0, d, b * P:(b + 1) * P],
                                   start=(d == 0), stop=(d == DH - 1))
                mm.then_inc(scores_ready, 1)

            for b in range(B + 1):
                if b < B:
                    scores(b)
                if b >= 1:
                    pe.wait_ge(faded, b)
                    pe.wait_ge(v_copied, b)
                    if b >= 3:
                        pe.wait_ge(done.sum, n4.sum + b - 2)
                    pe.matmul(bank[2 + (b - 1) % 2][:, 0:D], att[:, (b - 1) % 2, :], acc[:, b - 1, :], start=True, stop=True
                              ).then_inc(y_ready, 1)
            for p in range(4):
                norm_transpose(pe, n4, p)

        def stage4_act(act):
            act.wait_ge(done.x, n3.x + B)
            for b in range(B):
                act.wait_ge(v_ready, b + 1)
                act.activation(acc[:, b, :], bank[4 + b % 2][:, 0:D], ACT.Copy, scale=1.0 / WS).then_inc(v_copied, 1)
            for p in range(4):
                act.wait_ge(done.t, n4.t + p + 1)
                act.activation(xTf[:, :, p * 256:(p + 1) * 256], bank[6 + p % 2][:, :].rearrange("q (d t) -> q d t", d=DH),
                               ACT.Copy).then_inc(done.lo, 1)

        def stage4_dve(dve, chain):
            dve.wait_ge(tables_in, 32)
            for u in range(4):
                qk = u % 2
                dve.wait_ge(qk1_product, u + 1)
                if u >= 2:
                    dve.wait_ge(turned, 2 * (u - 1))
                for i, (o, table) in enumerate(((0, 0), (1, 1), (1, 0), (0, 1))):
                    mm = dve.scalar_tensor_tensor(out=part[:, u % 2, i, :].rearrange("p (b t) -> p b t", b=4),
                                                  in0=bank[2 * (u % 2) + o][:, :].rearrange("p (b t) -> p b t", b=4), scalar=1.0 / WS,
                                                  in1=turns[:, 2 * qk + table, None, :].broadcast_to([P, 4, P]),
                                                  op0=ALU.mult, op1=ALU.mult)
                    if i % 2:
                        mm.then_inc(turn_parts, 1)

            def fade_scores(b):
                dve.wait_ge(scores_ready, b + 1)
                if b >= 2:
                    dve.wait_ge(y_ready, B + b - 1)
                dve.tensor_tensor(att[:, b % 2, :], bank[b % 2][:, 0:P], fade[:, :], ALU.mult).then_inc(faded, 1)

            for b in range(B + 2):
                if b < B:
                    fade_scores(b)
                if 1 <= b < B + 1:
                    dve.wait_ge(y_ready, B + b)
                    norm_sum(dve, chain, n4, b - 1, bank[2 + (b - 1) % 2][:, 0:D], 1.0)
                if b >= 2:
                    norm_apply(dve, n4, b - 2)

        def stage4_pool(pool, chain):
            for g in range(8):
                u, o = g // 2, g % 2
                pool.wait_ge(turn_parts, g + 1)
                pool.tensor_tensor(rqk[:, u % 2, o, u // 2 * HALF:(u // 2 + 1) * HALF], part[:, u % 2, 2 * o, :],
                                   part[:, u % 2, 2 * o + 1, :], ALU.add if o else ALU.subtract).then_inc(turned, 1)
            for b in range(B):
                norm_rstd(pool, chain, n4, b)

        look = Region()
        ctxT = look("ctxT", [P, DH, T])
        ctxm = look("ctxm", [P, B, D])
        xTf = look("xTf", [P, DH, T])
        seen = look("seen", [P, T])
        unseen = look("unseen", [P, T])
        seen8 = look("seen8", [P, T], U8)
        sc5 = look("sc5", [P, 2, P])
        p5 = look("p5", [P, 2, P])
        pT5 = look("pT5", [P, 2, P])
        valid = sb("valid", [P, B])
        peak = sb("peak", [P, B])
        sum5 = sb("sum5", [P, B])
        peak_found = sem("peak_found")
        exp_done = sem("exp_done")
        ctx_in = sem("ctx_in")
        n5 = Norm(5, 3, 2)

        def stage5_loads_sp(sp):
            sp.wait_ge(done.sum, n2.sum + B)
            sp.dma_start(ctxT[:, :, :], ins["ctxT"].rearrange("(d p) t -> p d t", p=P)).then_inc(ctx_in, 16)
            sp.dma_start(ctxm[:, :, :], ins["ctx"].rearrange("b p d -> p b d")).then_inc(ctx_in, 16)
            sp.dma_start(seen8[:, :], ins["mask"].partition_broadcast(P)).then_inc(ctx_in, 16)

        def stage5_pe(pe):
            pe.wait_ge(ctx_in, 48)

            def scores(b):
                pe.wait_ge(done.lo, n4.lo + b // 2 + 1)
                if b >= 2:
                    pe.wait_ge(peak_found, b - 1)
                for d in range(DH):
                    mm = pe.matmul(bank[b % 2][:, 0:P], xTf[:, d, b * P:(b + 1) * P], ctxT[:, d, b * P:(b + 1) * P],
                                   start=(d == 0), stop=(d == DH - 1))
                mm.then_inc(scores_ready, 1)

            def turn(b):
                pe.wait_ge(exp_done, b + 1)
                if b >= 2:
                    pe.wait_ge(v_copied, B + b - 1)
                pe.transpose(bank[2 + b % 2][:, 0:P], p5[:, b % 2, :], ident[:, :]).then_inc(v_ready, 1)

            def read(b):
                pe.wait_ge(v_copied, B + b + 1)
                if b >= 2:
                    pe.wait_ge(done.sum, n5.sum + b - 1)
                pe.matmul(bank[4 + b % 2][:, 0:D], pT5[:, b % 2, :], ctxm[:, b, :], start=True, stop=True).then_inc(y_ready, 1)

            for b in range(B + 2):
                if b < B:
                    scores(b)
                if 1 <= b < B + 1:
                    turn(b - 1)
                if b >= 2:
                    read(b - 2)
            for p in range(4):
                norm_transpose(pe, n5, p)

        def stage5_act(act):
            def weigh(b):
                act.wait_ge(peak_found, b + 1)
                if b >= 2:
                    act.wait_ge(v_ready, B + b - 1)
                act.activation(p5[:, b % 2, :], sc5[:, b % 2, :], ACT.Exp, scale=-1.0, bias=peak[:, b:b + 1],
                               accum_out=sum5[:, b:b + 1]).then_inc(exp_done, 1)

            def copy(b):
                act.wait_ge(v_ready, B + b + 1)
                if b >= 2:
                    act.wait_ge(y_ready, 2 * B + b - 1)
                act.activation(pT5[:, b % 2, :], bank[2 + b % 2][:, 0:P], ACT.Copy, scale=valid[:, b:b + 1]).then_inc(v_copied, 1)

            for b in range(B + 1):
                if b < B:
                    weigh(b)
                if b >= 1:
                    copy(b - 1)
            for p in range(4):
                norm_hi(act, n5, p)

        def masks_dve(dve, chain, part):
            dve.wait_ge(ctx_in, 48)
            if part == 0:
                chain.link(dve.tensor_copy(seen[:, :], seen8[:, :]))
            elif part == 1:
                chain.link(dve.tensor_scalar(unseen[:, :], seen[:, :], -1e30, 1e30, ALU.mult, ALU.add))
            else:
                chain.link(dve.tensor_reduce(valid[:, :], seen[:, :].rearrange("p (b m) -> p b m", b=B), AX.X, ALU.max))

        def stage5_dve(dve, chain):
            def mask(b):
                dve.wait_ge(scores_ready, B + b + 1)
                if b >= 2:
                    dve.wait_ge(exp_done, b - 1)
                chain.link(dve.scalar_tensor_tensor(out=sc5[:, b % 2, :], in0=bank[b % 2][:, 0:P], scalar=-float(D) ** -0.5,
                                                    in1=unseen[:, b * P:(b + 1) * P], op0=ALU.mult, op1=ALU.add))
                dve.tensor_reduce(peak[:, b:b + 1], sc5[:, b % 2, :], AX.X, ALU.min).then_inc(peak_found, 1)

            def add(b):
                dve.wait_ge(exp_done, b + 1)
                chain.link(dve.reciprocal(sum5[:, b:b + 1], sum5[:, b:b + 1]))
                dve.wait_ge(y_ready, 2 * B + b + 1)
                norm_sum(dve, chain, n5, b, bank[4 + b % 2][:, 0:D], sum5[:, b:b + 1])

            for b in range(B + 4):
                if b < B:
                    mask(b)
                if 2 <= b < B + 2:
                    add(b - 2)
                if 3 <= b < B + 3:
                    norm_apply(dve, n5, b - 3)
            for p in range(4):
                norm_lo(dve, n5, p)

        def stage5_pool(pool, chain):
            for b in range(B):
                norm_rstd(pool, chain, n5, b)

        e1 = Experts("e1", Region(CONV_WORDS), 32, 8, 96, True, P + SHARED, 3, ins["gate1"], ins["up1"], ins["down1"], 1)
        n6 = Norm(6, 4, 3)
        cleared = sem("cleared")
        zero = Region(ARENA2 - D, arena2)("zero", [P, D])
        KEEP = 0.8

        def stage6_sp(sp):
            credits_sp(sp, e1)
            sp.wait_ge(done.x, n3.x + B)
            route_sp(sp, e1)
            rows_sp(sp, e1)
            rounds = read_rounds(sp, e1)
            with sp.Fori(0, rounds) as r:
                round_sp(sp, e1, r)
            gather_sp(sp, e1, rounds)
            for i in range(2):
                sp.wait_ge(e1.weights_in[i], rounds * (64 * e1.NI) + 64)
            for b in range(B):
                sp.wait_ge(done.x, n6.x + b + 1)
                sp.dma_start(out[b, :, :], X[:, b, :]).then_inc(out_written, 16)
            sp.wait_ge(out_written, 16 * B)

        def stage6_act(act):
            gate_act(act, e1)
            for b in range(B):
                rows_act(act, e1, n5, b)
            soft_act(act, e1)
            for b in range(B):
                act.activation(acc[:, b, :], X[:, b, :], ACT.Copy).then_inc(acc_ready, 1)
            rounds = read_rounds(act, e1)
            with act.Fori(0, rounds) as r:
                round_act(act, e1, r)
            norm_all_act(act, n6, e1, False)

        def stage6_dve(dve, chain):
            spare_dve(dve, chain, e1)
            gate_dve(dve, e1)
            for b in range(B):
                pick_dve(dve, chain, e1, b)
            weigh_dve(dve, chain, e1, KEEP)
            rank_dve(dve, chain, e1, KEEP)
            rounds_dve(dve, chain, e1)
            dve.wait_ge(acc_ready, B + B)
            rounds = read_rounds(dve, e1)
            with dve.Fori(0, rounds) as r:
                lists_dve(dve, e1, r)
                round_dve(dve, e1, r)
            norm_all_dve(dve, chain, n6, e1, False)

        def stage6_pe(pe):
            pe.wait_ge(e1.s["gate_low"], e1.before["gate_low"] + 1)
            for b in range(B):
                logits_pe(pe, e1, n5, b)
            rank_pe(pe, e1)
            rounds = read_rounds(pe, e1)
            with pe.Fori(0, rounds) as r:
                lists_pe(pe, e1, r)
                round_pe(pe, e1, r)
            norm_all_pe(pe, n6, e1, False)

        def stage6_pool(pool, chain):
            for b in range(B):
                rows_pool(pool, e1, b)
            name_pool(pool, e1)
            base(pool, e1)
            pool.wait_ge(e1.rows_written, e1.before["rows"] + 16 * B)
            pool.wait_ge(cleared, 16 * e1.K)
            rounds = read_rounds(pool, e1)
            with pool.Fori(0, rounds) as r:
                round_pool(pool, e1, r)
            norm_all_pool(pool, chain, n6)


        block = ctx.enter_context(nc.Block())

        @block.sync
        def _(sp):
            stage1_sp(sp)
            stage2_sp(sp)
            stage3_sp(sp)
            clear_sp(sp)
            stage6_sp(sp)

        @block.tensor
        def _(pe):
            stage1_pe(pe)
            stage2_pe(pe)
            stage3_pe(pe)
            stage4_pe(pe)
            stage5_pe(pe)
            stage6_pe(pe)

        @block.scalar
        def _(act):
            stage1_act(act)
            stage2_act(act)
            stage3_act(act)
            stage4_act(act)
            stage5_act(act)
            stage6_act(act)

        @block.vector
        def _(dve):
            chain = Chain(dve, dve_chain_sem)
            stage1_dve(dve, chain)
            stage2_dve(dve, chain)
            stage3_dve(dve, chain)
            stage4_dve(dve, chain)
            stage5_dve(dve, chain)
            stage6_dve(dve, chain)

        @block.gpsimd
        def _(pool):
            chain = Chain(pool, pool_chain_sem)
            stage1_pool(pool, chain)
            stage2_pool(pool, chain)
            stage3_pool(pool, chain)
            stage4_pool(pool, chain)
            stage5_pool(pool, chain)
            stage6_pool(pool, chain)

def _heads_apart(w):
    return np.repeat(w.reshape(D, H, 1, HD), 2, axis=2).reshape(D, 2 * D)


def _way_up(w):
    e, n, _ = w.shape
    return w.reshape(e // 4, 4, n, DH, P).transpose(0, 4, 1, 3, 2).reshape(e // 4, P, 4, DH * n)


def _way_down(w, tiles):
    e, _, n = w.shape
    return w.reshape(e // 4, 4, D, tiles, n // tiles).transpose(0, 4, 1, 3, 2).reshape(e // 4, n // tiles, 4, tiles * D)


def _turns():
    at = np.arange(P, dtype=np.float32)
    pair = np.arange(0, D, 2, dtype=np.float32)
    scale = ((pair + np.float32(0.4 * D)) / np.float32(1.4 * D))[None, :] ** (at / np.float32(SCALE_BASE))[:, None]
    angle = at[:, None] * (np.float32(1.0) / np.float32(10000.0) ** (np.arange(D // 2, dtype=np.float32) / np.float32(D // 2)))
    return np.stack([(f(angle) * s).T for s in (scale, np.float32(1.0) / scale) for f in (np.cos, np.sin)])


def _even_first(w):
    return np.concatenate([w[:, 0::2], w[:, 1::2]], axis=1)


def _constants():
    i = np.arange(P)
    key, query = i[:, None], i[None, :]
    c = {
        "c_ident": np.eye(P),
        "c_lows": np.where(key % 32 < HD, 0, -1),
        "c_diff": np.maximum(query - key, 0),
        "c_causal": query >= key,
        "c_turns": _turns(),
        "c_fade": np.where(query >= key, GAMMA ** np.maximum(query - key, 0), 0.0),
        "c_before": key < query,
        "c_iota": np.concatenate([np.arange(P + SHARED), np.arange(P, P + SHARED)]),
        "c_tokens": key + P * np.arange(B) + 1,
        "c_pick_rows": T * np.arange(8),
        "c_anti": key + query == P - 1,
    }
    return {k: np.ascontiguousarray(v, np.float32) for k, v in c.items()}


def _layout(i):
    w = i["L0_attn_W_qkvu"].T
    a = {
        "x": i["x"],
        "xT": i["x"].reshape(T, D).T,
        "w_qkvu": np.concatenate([_heads_apart(w[:, :D]), _heads_apart(w[:, D:2 * D]), w[:, 2 * D:]], axis=1),
        "w_out": i["L0_attn_W_out"].T,
        "ctx_rev": i["ctx_2048"].transpose(2, 1, 0).reshape(DH, P, P * B)[:, ::-1].transpose(1, 0, 2).reshape(P, -1),
        "filters": np.concatenate([np.zeros((H, P - 1), np.float32), i["L0_xattn_ssm_kernel"]], axis=1),
        "w_qkv1": np.concatenate([_even_first(i["L1_attn_W_Q"]), _even_first(i["L1_attn_W_K"]), i["L1_attn_W_V"]], axis=1),
        "ctx": i["ctx_2048"],
        "ctxT": i["ctx_2048"].reshape(T, D).T,
        "mask": i["mask_BxS2_bk0"].reshape(T),
        "gate1": i["L1_ffn_gate_weight"].T,
        "up1": _way_up(i["L1_ffn_gate_up_proj"]),
        "down1": _way_down(i["L1_ffn_down_proj"], 1),
        "gate0": i["L0_ffn_gate_w"].T,
        "up0": _way_up(i["L0_ffn_experts_w1"]),
        "down0": _way_down(i["L0_ffn_experts_w2"], 2),
        "shared_up": i["L0_ffn_shared_gate_up"].T,
        "shared_down": i["L0_ffn_shared_down"].T,
        "conv_d": i["L0_xattn_D"],
        "slope": i["L0_attn_slope_rate"].reshape(H),
    }
    return {k: np.ascontiguousarray(v) for k, v in a.items()} | _constants()


def kernel(**inputs):
    import concourse.bacc as bacc
    from concourse.bass_utils import run_bass_kernel_spmd

    nc = bacc.Bacc("TRN2", target_bir_lowering=False, num_devices=1)
    laid_out = _layout({name: np.asarray(value) for name, value in inputs.items()})
    arrays, ins = {}, {}
    for name, array in laid_out.items():
        arrays[f"in_{name}_dram"] = array
        ins[name] = nc.dram_tensor(f"in_{name}_dram", array.shape, mybir.dt.from_np(array.dtype), kind="ExternalInput").ap()
    out = nc.dram_tensor("out_0_dram", (B, P, D), F32, kind="ExternalOutput").ap()
    build_program(nc, ins, out)
    return run_bass_kernel_spmd(nc, [arrays], core_ids=[0]).results[0]["out_0_dram"]
```
